# Optimizing a Trainium2 kernel written in Bass

```python
import numpy as np
import jax
import jax.numpy as jnp

def _softmax(x, axis=-1):
    return jax.nn.softmax(x, axis=axis)

def _gelu(x):
    return jax.nn.gelu(x, approximate=True)

def _silu(x):
    return jax.nn.silu(x)

def _sigmoid(x):
    return jax.nn.sigmoid(x)

def _layernorm(x, axis=-1, eps=1e-05):
    m = jnp.mean(x, axis=axis, keepdims=True)
    v = jnp.var(x, axis=axis, keepdims=True)
    return (x - m) / jnp.sqrt(v + eps)

def _scatter_add(tgt, idx, src, axis=0):
    return tgt.at[idx].add(src)

def _segment_sum(src, seg, n):
    return jax.ops.segment_sum(src, seg, n)
kernel_name = 'mk_decoder_preln_d1_seqx_r8_5ca915'

def setup_inputs(seed: int=0):
    np.random.seed(seed)
    _w = jnp.asarray

    def _rec_inputs():
        import jax
        import jax.numpy as jnp
        _rk = jax.random.key(seed)
        x = -0.0002928 + 1 * jax.random.normal(jax.random.fold_in(_rk, 1), (8, 256, 128), jnp.float32)
        _lenS = 256 - jax.random.randint(jax.random.fold_in(_rk, 7), (8,), 0, max(1, 256 // 4) + 1, jnp.int32)
        _lenS2 = 256 - jax.random.randint(jax.random.fold_in(_rk, 8), (8,), 0, max(1, 256 // 4) + 1, jnp.int32)
        _ctx_1024P = jax.random.normal(jax.random.fold_in(_rk, 11), (8, 16, 128), jnp.float32)
        _ctx_1024c = jax.random.dirichlet(jax.random.fold_in(_rk, 511), 0.3 * jnp.ones((16,), jnp.float32), (8, 256))
        _ctx_1024t = jnp.einsum('bsk,bkd->bsd', _ctx_1024c, _ctx_1024P)
        _ctx_1024t = _ctx_1024t * jax.lax.rsqrt(jnp.mean(jnp.square(_ctx_1024t)) + 1e-12) * 0.953939
        ctx_1024 = -1.39393e-06 + 0.999914 * (_ctx_1024t + 0.3 * jax.random.normal(jax.random.fold_in(_rk, 611), (8, 256, 128), jnp.float32))
        return (x, ctx_1024)
    x, ctx_1024 = _rec_inputs()

    def _L0_attn_setup():
        import jax, jax.numpy as jnp
        import numpy as np
        import math
        N_HEAD = 16
        N_LATENTS = 64
        CHUNK = 128
        ROPE_THETA = 10000.0

        def _rope_cos_sin(T, D, theta):
            inv = 1.0 / theta ** (jnp.arange(0, D, 2, dtype=jnp.float32) / D)
            ang = jnp.arange(T, dtype=jnp.float32)[:, None] * inv[None, :]
            return (jnp.cos(ang), jnp.sin(ang))

        def _apply_rope(k, cos, sin):
            B, T, H, D = k.shape
            kr = k.reshape(B, T, H, D // 2, 2)
            a, b = (kr[..., 0], kr[..., 1])
            c = cos[None, :, None, :]
            s = sin[None, :, None, :]
            out = jnp.stack([a * c - b * s, a * s + b * c], axis=-1)
            return out.reshape(B, T, H, D).astype(k.dtype)
        key = jax.random.key(seed)
        ks = jax.random.split(key, 6)
        B, T, C = (8, 512, 128)
        H, L = (N_HEAD, N_LATENTS)
        D = C // H
        std_in = 1.0 / math.sqrt(C)
        return {'x': jax.random.normal(ks[0], (B, T, C), jnp.float32), 'latent_queries': jax.random.normal(ks[1], (1, L, H, D), jnp.float32) * (1.0 / math.sqrt(D)), 'W_k': jax.random.normal(ks[2], (C, C), jnp.float32) * std_in, 'W_v': jax.random.normal(ks[3], (C, C), jnp.float32) * std_in, 'W_g': jax.random.normal(ks[4], (H * L, C), jnp.float32) * std_in, 'W_p': jax.random.normal(ks[5], (C, C), jnp.float32) * std_in}
    _L0_attn_all = _L0_attn_setup()
    _L0_attn_in = {k: v for k, v in _L0_attn_all.items() if k in ('latent_queries', 'W_k', 'W_v', 'W_g', 'W_p')}
    del _L0_attn_all

    def _L0_xattn_setup():
        import jax, jax.numpy as jnp
        import numpy as np
        B, S, E, NH = (2, 256, 128, 4)
        HD = E // NH

        def _mlstm_head(q, k, v, ig, fg, eps=1e-06):
            s, dh = q.shape
            log_f = jax.nn.log_sigmoid(fg)
            cs = jnp.concatenate([jnp.zeros((1, 1), log_f.dtype), jnp.cumsum(log_f, axis=0)], axis=0)
            neg = jnp.asarray(-0.7 * jnp.finfo(cs.dtype).max, cs.dtype)
            log_d = jnp.where(jnp.tri(s, dtype=bool), (cs - cs.T)[1:, 1:] + ig.T, neg)
            m = jnp.max(log_d, axis=-1, keepdims=True)
            d = jnp.exp(log_d - m)
            c = q @ (k.T / jnp.sqrt(dh)) * d
            n = jnp.maximum(jnp.sum(c, axis=-1, keepdims=True), jnp.exp(-m))
            return c / (n + eps) @ v
        key = jax.random.key(seed)
        ks = jax.random.split(key, 8)
        return {'q': jax.random.normal(ks[0], (B, S, E), jnp.float32), 'k': jax.random.normal(ks[1], (B, S, E), jnp.float32), 'v': jax.random.normal(ks[2], (B, S, E), jnp.float32), 'igate_kernel': jax.random.normal(ks[3], (3 * E, NH), jnp.float32) * 0.02, 'igate_bias': jax.random.normal(ks[4], (NH,), jnp.float32) * 0.1, 'fgate_kernel': jax.random.normal(ks[5], (3 * E, NH), jnp.float32) * 0.02, 'fgate_bias': jnp.linspace(3.0, 6.0, NH, dtype=jnp.float32), 'rms_scale': jax.random.normal(ks[6], (HD,), jnp.float32) * 0.02}
    _L0_xattn_all = _L0_xattn_setup()
    _L0_xattn_in = {k: v for k, v in _L0_xattn_all.items() if k in ('igate_kernel', 'igate_bias', 'fgate_kernel', 'fgate_bias', 'rms_scale')}
    del _L0_xattn_all

    def _L0_ffn_setup():
        import math
        import jax, jax.numpy as jnp
        import numpy as np
        B, S, H = (4, 256, 128)
        E, K, I = (8, 2, 128)
        NSH = 2
        CF, RSF = (1.25, 1.0)
        key = jax.random.key(seed)
        ks = jax.random.split(key, 8)
        w = lambda k, sh: jax.random.normal(k, sh, dtype=jnp.float32) * 0.02
        return {'hidden_states': jax.random.normal(ks[0], (B, S, H), dtype=jnp.float32), 'gate_w': w(ks[1], (E, H)), 'we_gate': w(ks[2], (E, I, H)), 'we_up': w(ks[3], (E, I, H)), 'we_down': w(ks[4], (E, H, I)), 'ws_gate': w(ks[5], (NSH * I, H)), 'ws_up': w(ks[6], (NSH * I, H)), 'ws_down': w(ks[7], (H, NSH * I))}
    _L0_ffn_all = _L0_ffn_setup()
    _L0_ffn_in = {k: v for k, v in _L0_ffn_all.items() if k in ('gate_w', 'we_gate', 'we_up', 'we_down', 'ws_gate', 'ws_up', 'ws_down')}
    del _L0_ffn_all
    return {'x': x, 'ctx_1024': ctx_1024, 'L0_attn_latent_queries': _L0_attn_in['latent_queries'], 'L0_attn_W_k': _L0_attn_in['W_k'], 'L0_attn_W_v': _L0_attn_in['W_v'], 'L0_attn_W_g': _L0_attn_in['W_g'], 'L0_attn_W_p': _L0_attn_in['W_p'], 'L0_xattn_igate_kernel': _L0_xattn_in['igate_kernel'], 'L0_xattn_igate_bias': _L0_xattn_in['igate_bias'], 'L0_xattn_fgate_kernel': _L0_xattn_in['fgate_kernel'], 'L0_xattn_fgate_bias': _L0_xattn_in['fgate_bias'], 'L0_xattn_rms_scale': _L0_xattn_in['rms_scale'], 'L0_ffn_gate_w': _L0_ffn_in['gate_w'], 'L0_ffn_we_gate': _L0_ffn_in['we_gate'], 'L0_ffn_we_up': _L0_ffn_in['we_up'], 'L0_ffn_we_down': _L0_ffn_in['we_down'], 'L0_ffn_ws_gate': _L0_ffn_in['ws_gate'], 'L0_ffn_ws_up': _L0_ffn_in['ws_up'], 'L0_ffn_ws_down': _L0_ffn_in['ws_down']}

def reference(x, ctx_1024, L0_attn_latent_queries, L0_attn_W_k, L0_attn_W_v, L0_attn_W_g, L0_attn_W_p, L0_xattn_igate_kernel, L0_xattn_igate_bias, L0_xattn_fgate_kernel, L0_xattn_fgate_bias, L0_xattn_rms_scale, L0_ffn_gate_w, L0_ffn_we_gate, L0_ffn_we_up, L0_ffn_we_down, L0_ffn_ws_gate, L0_ffn_ws_up, L0_ffn_ws_down):
    import jax
    import jax.numpy as jnp

    def _L0_attn_ref(x, latent_queries, W_k, W_v, W_g, W_p):
        import jax, jax.numpy as jnp
        import numpy as np
        import math
        N_HEAD = 16
        N_LATENTS = 64
        CHUNK = 128
        ROPE_THETA = 10000.0

        def _rope_cos_sin(T, D, theta):
            inv = 1.0 / theta ** (jnp.arange(0, D, 2, dtype=jnp.float32) / D)
            ang = jnp.arange(T, dtype=jnp.float32)[:, None] * inv[None, :]
            return (jnp.cos(ang), jnp.sin(ang))

        def _apply_rope(k, cos, sin):
            B, T, H, D = k.shape
            kr = k.reshape(B, T, H, D // 2, 2)
            a, b = (kr[..., 0], kr[..., 1])
            c = cos[None, :, None, :]
            s = sin[None, :, None, :]
            out = jnp.stack([a * c - b * s, a * s + b * c], axis=-1)
            return out.reshape(B, T, H, D).astype(k.dtype)
        B, T, C = x.shape
        H, L, cs = (N_HEAD, N_LATENTS, CHUNK)
        D = C // H
        scale = 1.0 / math.sqrt(D)
        k = (x @ W_k.T).reshape(B, T, H, D)
        v = (x @ W_v.T).reshape(B, T, H, D)
        cos, sin = _rope_cos_sin(T, D, ROPE_THETA)
        k = _apply_rope(k, cos, sin)
        gates = jax.nn.softmax((x @ W_g.T).reshape(B, T, H, L) * scale, axis=-1)
        q = jnp.transpose(latent_queries, (0, 2, 1, 3))
        nc = T // cs
        kc = jnp.transpose(k, (0, 2, 1, 3)).reshape(B, H, nc, cs, D)
        vc = jnp.transpose(v, (0, 2, 1, 3)).reshape(B, H, nc, cs, D)
        scores = jnp.einsum('zhld,bhncd->bhnlc', q, kc) * scale
        causal = jnp.arange(cs)[None, :] <= jnp.arange(L)[:, None]
        scores = jnp.where(causal[None, None, None], scores, -jnp.inf)
        probs = jax.nn.softmax(scores, axis=-1)
        attn = jnp.einsum('bhnlc,bhncd->bhld', probs, vc)
        weighted = jnp.einsum('bhld,bthl->bthd', attn, gates)
        out = weighted.reshape(B, T, C) @ W_p.T
        return out

    def _L0_xattn_ref(q, k, v, igate_kernel, igate_bias, fgate_kernel, fgate_bias, rms_scale):
        import jax, jax.numpy as jnp
        import numpy as np
        B, S, E, NH = (2, 256, 128, 4)
        HD = E // NH

        def _mlstm_head(q, k, v, ig, fg, eps=1e-06):
            s, dh = q.shape
            log_f = jax.nn.log_sigmoid(fg)
            cs = jnp.concatenate([jnp.zeros((1, 1), log_f.dtype), jnp.cumsum(log_f, axis=0)], axis=0)
            neg = jnp.asarray(-0.7 * jnp.finfo(cs.dtype).max, cs.dtype)
            log_d = jnp.where(jnp.tri(s, dtype=bool), (cs - cs.T)[1:, 1:] + ig.T, neg)
            m = jnp.max(log_d, axis=-1, keepdims=True)
            d = jnp.exp(log_d - m)
            c = q @ (k.T / jnp.sqrt(dh)) * d
            n = jnp.maximum(jnp.sum(c, axis=-1, keepdims=True), jnp.exp(-m))
            return c / (n + eps) @ v
        b, s, e = q.shape
        nh = igate_kernel.shape[1]
        hd = e // nh
        gate_in = jnp.concatenate((q, k, v), axis=-1)
        ig = (gate_in @ igate_kernel + igate_bias).swapaxes(-1, -2)[..., None]
        fg = (gate_in @ fgate_kernel + fgate_bias).swapaxes(-1, -2)[..., None]
        qh = q.reshape(b, s, nh, hd).swapaxes(1, 2)
        kh = k.reshape(b, s, nh, hd).swapaxes(1, 2)
        vh = v.reshape(b, s, nh, hd).swapaxes(1, 2)
        h = jax.vmap(jax.vmap(_mlstm_head))(qh, kh, vh, ig, fg)
        var = jnp.mean(jnp.square(h.astype(jnp.float32)), axis=-1, keepdims=True)
        h = (h * jax.lax.rsqrt(var + 1e-06)).astype(h.dtype) * (1.0 + rms_scale)
        return h.swapaxes(1, 2).reshape(b, s, e)

    def _L0_ffn_ref(hidden_states, gate_w, we_gate, we_up, we_down, ws_gate, ws_up, ws_down):
        import math
        import jax, jax.numpy as jnp
        import numpy as np
        B, S, H = (4, 256, 128)
        E, K, I = (8, 2, 128)
        NSH = 2
        CF, RSF = (1.25, 1.0)
        orig_shape = hidden_states.shape
        x = hidden_states.reshape(-1, H)
        N = x.shape[0]
        logits = x.astype(jnp.float32) @ gate_w.astype(jnp.float32).T
        scores = jax.nn.softmax(logits, axis=-1)
        topk_w, topk_idx = jax.lax.top_k(scores, K)
        topk_w = topk_w / (topk_w.sum(-1, keepdims=True) + 1e-20) * RSF
        capacity = math.ceil(CF * N * K / E)
        flat = topk_idx.reshape(-1)
        one_hot = jax.nn.one_hot(flat, E, dtype=jnp.int32)
        pos = jnp.cumsum(one_hot, axis=0) - 1
        pos_tok = jnp.take_along_axis(pos, flat[:, None], axis=1)[:, 0]
        keep = (pos_tok < capacity).reshape(N, K)
        topk_w = topk_w * keep.astype(topk_w.dtype)
        comb = jnp.zeros((N, E), jnp.float32).at[jnp.arange(N)[:, None], topk_idx].add(topk_w)
        g = jnp.einsum('nh,eih->nei', x, we_gate)
        u = jnp.einsum('nh,eih->nei', x, we_up)
        eo = jnp.einsum('nei,ehi->neh', jax.nn.silu(g) * u, we_down)
        y = jnp.einsum('neh,ne->nh', eo, comb)
        sh = jax.nn.silu(x @ ws_gate.T) * (x @ ws_up.T) @ ws_down.T
        return (y + sh).reshape(orig_shape)
    x = x + _L0_attn_ref(_layernorm(x, axis=-1), L0_attn_latent_queries, L0_attn_W_k, L0_attn_W_v, L0_attn_W_g, L0_attn_W_p)
    x = x + _L0_xattn_ref(_layernorm(x, axis=-1), ctx_1024, ctx_1024, L0_xattn_igate_kernel, L0_xattn_igate_bias, L0_xattn_fgate_kernel, L0_xattn_fgate_bias, L0_xattn_rms_scale)
    x = x + _L0_ffn_ref(_layernorm(x, axis=-1), L0_ffn_gate_w, L0_ffn_we_gate, L0_ffn_we_up, L0_ffn_we_down, L0_ffn_ws_gate, L0_ffn_ws_up, L0_ffn_ws_down)
    return x

_drawn_inputs = setup_inputs


def setup_inputs(seed=0):
    import zlib

    import numpy as np

    out = dict(_drawn_inputs(seed))
    spreads = {}
    factors = {'L0_attn_latent_queries': 3.467,
     'L0_attn_W_k': 3.13,
     'L0_attn_W_g': 3.656,
     'L0_xattn_igate_bias': 64.0,
     'L0_xattn_fgate_kernel': 2.772,
     'L0_xattn_rms_scale': 3.994,
     'L0_ffn_gate_w': 8.0,
     'L0_ffn_we_gate': 8.0,
     'L0_ffn_we_up': 8.0,
     'L0_ffn_we_down': 8.0,
     'L0_ffn_ws_gate': 8.0,
     'L0_ffn_ws_up': 8.0,
     'L0_ffn_ws_down': 8.0}
    for name, (base, spread) in spreads.items():
        noise = np.random.default_rng([zlib.crc32(name.encode()), seed]).standard_normal(out[name].shape)
        drawn = base * np.exp(spread * noise) if base else spread * noise
        out[name] = jnp.asarray(drawn.astype(out[name].dtype))
    for name, factor in factors.items():
        out[name] = (out[name] * factor).astype(out[name].dtype)
    return out
```

```python
from contextlib import ExitStack

import numpy as np

import concourse.bass as bass
from concourse import mybir

ALU = mybir.AluOpType
ACT = mybir.ActivationFunctionType
AX_X = mybir.AxisListType.X
F32 = mybir.dt.float32
BF16 = mybir.dt.bfloat16
U32 = mybir.dt.uint32

B, T, C = 8, 256, 128
P = 128
TT = T // P
NT = B * TT
H, L, D = 16, 64, 8
HP = H // 2
NH, HD = 4, 32
BH = B * NH
E, I = 8, 128
NSH = 2
CAP = 640
BLK = 4
NB = NT // BLK
WV = 2 * D + 1
VCOLS = (HP - 1) * TT * WV + P
LN_EPS = 1e-5
RMS_EPS = 1e-6
KV_LOADS = NH + 1
ATTN_DVE_STEPS = 18
MIX_DVE_STEPS = 8
NEG = -1.0e30

def constants():
    pos = np.concatenate([np.arange(L) + n * P for n in range(TT)]).astype(np.float32)
    inv = (np.float32(1.0) / np.float32(10000.0) ** (np.arange(0, D, 2, dtype=np.float32) / np.float32(D))).astype(np.float32)
    ang = pos[None, :] * inv[(np.arange(C) % D) // 2][:, None]
    sign = np.where(np.arange(C) % 2 == 0, -1.0, 1.0).astype(np.float32)[:, None]
    latent = np.where(np.arange(L)[None, :] <= (np.arange(P) % L)[:, None], 0.0, NEG)
    i = np.arange(P)
    return {
        "ident": np.eye(P, dtype=np.float32),
        "rope_cos": np.cos(ang).astype(np.float32),
        "rope_sin": (np.sin(ang) * sign).astype(np.float32),
        "latent_mask": np.tile(latent, (1, 8)).astype(np.float32),
        "causal_mask": np.where(i[:, None] <= i[None, :], 0.0, NEG).astype(np.float32),
        "before": (i[:, None] < i[None, :]).astype(np.float32),
        "expert_ids": np.tile(np.repeat(np.arange(E), NT)[None, :], (P, 1)).astype(np.float32),
    }


class Chain:

    def __init__(self, eng, sem):
        self.eng, self.sem, self.total, self.base, self.k = eng, sem, 0, 0, 0

    def loop(self, t, per):
        self.total += self.k
        self.base, self.per, self.k = self.total + t * per, per, 0

    def end(self, n):
        assert self.k == self.per, f"steps in the loop: {self.k}"
        self.total += n * self.per
        self.base, self.k = self.total, 0

    def count(self, ins):
        self.k += 1
        ins.then_inc(self.sem, 1)

    def wait(self):
        self.eng.wait_ge(self.sem, self.base + self.k)

    def step(self, ins):
        self.count(ins)
        self.wait()


def decoder_layer(nc, a, out):
    scale = 1.0 / float(np.sqrt(D))
    qk_scale = 1.0 / float(np.sqrt(HD))
    with ExitStack() as ctx:
        def sb(name, shape, dt=F32):
            return ctx.enter_context(nc.sbuf_tensor(name, shape, dt))

        def pb(name, shape):
            return ctx.enter_context(nc.psum_tensor(name, shape, F32))

        def sem(name):
            return ctx.enter_context(nc.semaphore(name))

        x = sb("x_res", [P, NT, C])
        qT = sb("qT", [C, B * T])
        xT = sb("xT", [C, B * T])
        ctxT = sb("ctxT_s", [C, B * T])
        wk, wkr, wv, wp = (sb(n, [C, C]) for n in ("wk", "wkr", "wv", "wp"))
        wg = sb("wg", [C, H * L])
        qblk = sb("qblk_s", [C, HP, P])
        we_g, we_u, we_d = (sb(n, [P, E + NSH, P]) for n in ("we_g_s", "we_u_s", "we_d_s"))
        gate_w = sb("gate_w_s", [C, 96])
        kq, kk, kv = (sb(n, [C, B, 2 * BH]) for n in ("kq_s", "kk_s", "kv_s"))
        gate_bias = sb("gate_bias_s", [2 * BH, 1])
        rms = sb("rms_s", [P, TT, C])
        ident, ident_b = sb("ident_s", [P, P]), sb("ident_b", [P, P], BF16)
        cos, sin = sb("cos", [C, P]), sb("sin", [C, P])
        latent_mask, latent_mask_b = sb("latent_mask_s", [P, 512]), sb("latent_mask_b", [P, 512], BF16)
        causal, causal_b = sb("causal_s", [P, P]), sb("causal_b", [P, P], BF16)
        before, before_b = sb("before_s", [P, P]), sb("before_b", [P, P], BF16)
        ones_b, ones_f = sb("ones_b", [P, P], BF16), sb("ones_f", [P, HD])
        pick = sb("pick", [3 * BH, BH, P], BF16)
        ids = sb("ids", [P, E, NT])
        minus = sb("minus", [P, TT])
        mhalf, ln_eps, rms_eps = sb("mhalf", [P, TT * NH]), sb("ln_eps", [P, TT]), sb("rms_eps", [P, TT, NH])
        bn1, bn2, bn3 = (sb(f"bn{i}", [P, TT, 6]) for i in (1, 2, 3))
        mv1, mv2, mv3 = (sb(f"mv{i}", [P, TT, 2]) for i in (1, 2, 3))
        ve1, ve2, ve3 = (sb(f"ve{i}", [P, TT]) for i in (1, 2, 3))
        rs1, rs2, rs3 = (sb(f"rs{i}", [P, TT]) for i in (1, 2, 3))
        nb1, nb2, nb3 = (sb(f"nb{i}", [P, TT]) for i in (1, 2, 3))
        xn1, xn2, xn3 = (sb(f"xn{i}", [P, TT, C]) for i in (1, 2, 3))
        xnT, xkT = sb("xnT", [C, T]), sb("xkT", [C, P])
        k1, k2, kT = sb("k1", [C, P]), sb("k2", [C, P]), sb("kT", [C, P])
        vaug = sb("vaug", [P, VCOLS])
        s_max, s_sub, prob, pT = sb("s_max", [P, 16]), sb("s_sub", [P, 1024]), sb("prob", [P, 1024]), sb("pT", [P, 1024])
        g_max, g_sub, g_exp = sb("g_max", [P, TT, H]), sb("g_sub", [P, TT, 1024]), sb("g_exp", [P, TT, 1024])
        eT = sb("eT", [P, HP, T])
        a_rden, a_n0, a_n1 = sb("a_rden", [P, HP, TT]), sb("a_n0", [P, HP, D]), sb("a_n1", [P, HP, D])
        lat = sb("lat", [P, HP, 32])
        wu, wnT = sb("wu", [P, 2, T]), sb("wnT", [C, T])
        w_rden, wn = sb("w_rden", [P, NH * HP]), sb("wn", [P, TT, C])
        krow, gr = sb("krow", [2 * BH, T]), sb("gr", [2 * BH, T])
        f_abs, f_exp, f_log, f_min = (sb(n, [2 * BH, T]) for n in ("f_abs", "f_exp", "f_log", "f_min"))
        logf, cs, zeros, gi, top, m_row, em = (sb(n, [BH, T]) for n in ("logf", "cs", "zeros_r", "gi", "top", "m_row", "em"))
        neg, neg_r1, neg_r2 = (sb(n, [BH, T]) for n in ("neg", "neg_r1", "neg_r2"))
        neg_b1, neg_b2 = sb("neg_b1", [BH, T], BF16), sb("neg_b2", [BH, T], BF16)
        neg3 = sb("neg3", [3 * BH, T], BF16)
        rowT = sb("rowT", [P, 2, TT, BH])
        kTm = [sb(f"kTm{i}", [C, NH, T]) for i in range(2)]
        vv = [sb(f"vv{i}", [P, TT, C]) for i in range(2)]
        decay = sb("decay", [P, 2, 384])
        cc = [sb(f"cc{i}", [P, NH, 384]) for i in range(2)]
        hs, ss, sq = sb("hs", [P, T]), sb("ss", [P, T]), sb("sq", [P, TT * NH, HD])
        n4, n4e, r4, s4, r4s, v4, ve4, rs4, f4 = (sb(n, [P, TT, NH]) for n in ("n4", "n4e", "r4", "s4", "r4s", "v4", "ve4", "rs4", "f4"))
        y1, y2 = sb("y1", [P, TT, C]), sb("y2", [P, TT, C])
        lmax, lsub, lexp = sb("lmax", [P, NT]), sb("lsub", [P, NT, E]), sb("lexp", [P, NT, E])
        lsum, lrec, score = sb("lsum", [P, NT]), sb("lrec", [P, NT]), sb("score", [P, NT, E])
        top8, idx8, idxf = sb("top8", [P, NT, 8]), sb("idx8", [P, NT, 8], U32), sb("idxf", [P, 2, NT])
        wsum, wrec, w2 = sb("wsum", [P, NT]), sb("wrec", [P, NT]), sb("w2", [P, 2, NT])
        oh0, oh1, ohb = sb("oh0", [P, E, NT]), sb("oh1", [P, E, NT]), sb("ohb", [P, E, NT], BF16)
        carry, tot, pre, pos = (sb(n, [P, E, NT]) for n in ("carry", "tot", "pre", "pos"))
        ow0, ow1, ow, comb = (sb(n, [P, E, NT]) for n in ("ow0", "ow1", "ow", "comb"))
        act_warm = sb("act_warm", [P, 1])
        si = [sb(f"si{i}", [P, BLK * P]) for i in range(2)]
        hh = [sb(f"hh{i}", [P, BLK * P]) for i in range(2)]
        yw = [sb(f"yw{i}", [P, BLK, C]) for i in range(2)]
        acc, fin = sb("acc", [P, BLK, C]), sb("fin", [P, BLK, C])

        ps0, ps1, ps2 = pb("ps0", [P, 1024]), pb("ps1", [P, 1024]), pb("ps2", [P, 1024])
        ps3, ps4 = pb("ps3", [P, 512]), pb("ps4", [P, 512])

        x0_ld, x_ld, attn_ld, mask_ld, rows_ld, exp_ld = (sem(n) for n in ("x0_ld", "x_ld", "attn_ld", "mask_ld", "rows_ld", "exp_ld"))
        kv_ld = [sem(f"kv_ld{i}") for i in range(2)]
        out_st = sem("out_st")
        const_v, const_p = sem("const_v"), sem("const_p")
        dve_own, act_own, pool_own = sem("dve_own"), sem("act_own"), sem("pool_own")
        krow_mm, krow_a = sem("krow_mm"), sem("krow_a")
        kv_mm, g_mm, s_mm, pt_mm, at_mm, et_mm = (sem(n) for n in ("kv_mm", "g_mm", "s_mm", "pt_mm", "at_mm", "et_mm"))
        wt_mm, wtr_mm, wn_mm, pr_mm, xn_mm, q_mm = (sem(n) for n in ("wt_mm", "wtr_mm", "wn_mm", "pr_mm", "xn_mm", "q_mm"))
        ge_a, p_a, wu_a, wnT_a, xnT_a, pT_a, eT_a, qT_a = (sem(n) for n in ("ge_a", "p_a", "wu_a", "wnT_a", "xnT_a", "pT_a", "eT_a", "qT_a"))
        var1_v, var2_v, var3_v = sem("var1_v"), sem("var2_v"), sem("var3_v")
        rs1_p, rs2_p, rs3_p = sem("rs1_p"), sem("rs2_p"), sem("rs3_p")
        xn1_a, xn2_a, xn3_a = sem("xn1_a"), sem("xn2_a"), sem("xn3_a")
        kT_v, v_a, gsub_v, ssub_v, lat_v, wn_v, x1_v = (sem(n) for n in ("kT_v", "v_a", "gsub_v", "ssub_v", "lat_v", "wn_v", "x1_v"))
        kkv_a, gates_mm, gr_v, flog_a, m_v, em_a, gi_v, neg3_v, rowT_mm, rowT_v = (
            sem(n) for n in ("kkv_a", "gates_mm", "gr_v", "flog_a", "m_v", "em_a", "gi_v", "neg3_v", "rowT_mm", "rowT_v"))
        d_mm, qk_mm, d_a, c_v, pv_mm, hs_a, ht_mm = (sem(n) for n in ("d_mm", "qk_mm", "d_a", "c_v", "pv_mm", "hs_a", "ht_mm"))
        sq_a, n4_v, var4_v, rs4_p, y_v, y2_p, x2_v, x3_mm, x3_a = (
            sem(n) for n in ("sq_a", "n4_v", "var4_v", "rs4_p", "y_v", "y2_p", "x2_v", "x3_mm", "x3_a"))
        lg_mm, lsub_v, lexp_a, ohb_v, cnt_mm, comb_v = (sem(n) for n in ("lg_mm", "lsub_v", "lexp_a", "ohb_v", "cnt_mm", "comb_v"))
        gu_mm, si_a, hh_v, dn_mm, yw_v, acc_p, fin_v = (sem(n) for n in ("gu_mm", "si_a", "hh_v", "dn_mm", "yw_v", "acc_p", "fin_v"))

        block = ctx.enter_context(nc.Block())

        x_dram = a["x"].rearrange("b (n p) d -> p (b n) d", p=P)
        ctx_dram = a["ctx"].rearrange("b (n p) d -> b p n d", p=P)
        out_dram = out.rearrange("b (n p) d -> p (b n) d", p=P)
        attn_loads = ((wk, "wkT"), (wkr, "wkrT"), (wv, "wvT"), (cos, "rope_cos"), (sin, "rope_sin"), (wg, "wgT"),
                      (qblk, "qblk"), (wp, "wpT"))
        mask_loads = ((latent_mask, "latent_mask"), (causal, "causal_mask"), (before, "before"))
        rows_loads = ((ctxT, "ctxT"), (kq, "kq"), (kk, "kk"), (kv, "kv"), (gate_bias, "gate_bias"), (rms, "rms"))
        exp_loads = ((gate_w, "gate_w"), (ids, "expert_ids"), (we_g, "we_g"), (we_u, "we_u"), (we_d, "we_d"))
        tiles = lambda b: bass.ds(b * TT, TT)
        toks = lambda b: bass.ds(b * T, T)
        halves = lambda ps, j: ps[:, 512 * (j % 2):512 * (j % 2) + 512]

        @block.sync
        def _(sp):
            sp.dma_start(x[:, 0:TT, :], x_dram[:, 0:TT, :]).then_inc(x0_ld, 16)
            sp.dma_start(ident[:], a["ident"]).then_inc(x0_ld, 16)
            for dst, src in attn_loads:
                sp.dma_start(dst[:], a[src]).then_inc(attn_ld, 16)
            sp.dma_start(x[:, TT:NT, :], x_dram[:, TT:NT, :]).then_inc(x_ld, 16)
            for dst, src in rows_loads:
                sp.dma_start(dst[:], a[src]).then_inc(rows_ld, 16)
            for dst, src in exp_loads:
                sp.dma_start(dst[:], a[src]).then_inc(exp_ld, 16)

            def load_kv(b, par):
                for h in range(NH):
                    rows = slice(HD * h, HD * h + HD)
                    sp.dma_start(kTm[par][rows, h, :], a["ctxT"][rows, toks(b)]).then_inc(kv_ld[par], 16)
                sp.dma_start(vv[par][:], ctx_dram[b]).then_inc(kv_ld[par], 16)

            sp.wait_ge(const_p, 2)
            load_kv(0, 0)
            load_kv(1, 1)
            with sp.Fori(0, B // 2 - 1) as i:
                for par in range(2):
                    sp.wait_ge(pv_mm, 2 * i + par + 1)
                    load_kv(2 * i + par + 2, par)
            with sp.Fori(0, NB) as k:
                sp.wait_ge(fin_v, k + 1)
                sp.dma_start(out_dram[:, bass.ds(k * BLK, BLK), :], x[:, bass.ds(k * BLK, BLK), :]).then_inc(out_st, 16)
            sp.wait_ge(out_st, 16 * NB)

        @block.gpsimd
        def _(pool):
            own = Chain(pool, pool_own)
            own.step(pool.memset(mhalf[:], -0.5))
            own.step(pool.memset(minus[:], -1.0))
            own.step(pool.memset(ln_eps[:], LN_EPS))
            own.step(pool.memset(rms_eps[:], RMS_EPS))
            pool.memset(kTm[0][:], 0.0).then_inc(const_p, 1)
            pool.memset(kTm[1][:], 0.0).then_inc(const_p, 1)

            def root(var_ready, b, var, eps, ve, rs, done):
                pool.wait_ge(var_ready, b + 1)
                own.step(pool.tensor_tensor(ve, var, eps, ALU.add))
                pool.tensor_tensor(rs, ve, mh4, ALU.pow).then_inc(done, 1)

            def scale_bias(var_ready, b, mv, ve, rs, nb, applied, done):
                pool.wait_ge(var_ready, b + 1)
                if isinstance(b, int) and b > 0:
                    pool.wait_ge(applied, b)
                own.count(pool.tensor_tensor(nb, mv[:, :, 0], minus[:], ALU.mult))
                own.step(pool.tensor_tensor(ve, mv[:, :, 1], ln_eps[:], ALU.add))
                own.step(pool.tensor_tensor(rs, ve, mhalf[:, 0:TT], ALU.pow))
                pool.tensor_tensor(nb, nb, rs, ALU.mult).then_inc(done, 1)

            mh4 = mhalf[:].rearrange("p (n h) -> p n h", n=TT)

            def attn_step(t, first=False, last=False, front=True, tail=True):
                if front:
                    scale_bias(var1_v, t + 1, mv1, ve1[:], rs1[:], nb1[:], xn1_a, rs1_p)
                if tail:
                    scale_bias(var2_v, t - 1, mv2, ve2[:], rs2[:], nb2[:], xn2_a, rs2_p)

            scale_bias(var1_v, 0, mv1, ve1[:], rs1[:], nb1[:], xn1_a, rs1_p)
            attn_step(0, tail=False)
            with pool.Fori(1, B - 1) as t:
                own.loop(t - 1, 6)
                attn_step(t)
            own.end(B - 2)
            attn_step(B - 1, front=False)
            attn_step(B, front=False)

            def mix_step(t, mid=True, tail=True):
                if tail:
                    scale_bias(var3_v, t - 2, mv3, ve3[:], rs3[:], nb3[:], xn3_a, rs3_p)
                if mid:
                    root(var4_v, t - 1, v4[:], rms_eps[:], ve4[:], rs4[:], rs4_p)
                    pool.wait_ge(y_v, t)
                    if tail:
                        pool.wait_ge(x2_v, t - 1)
                    pool.tensor_tensor(y2[:], y1[:], rms[:], ALU.mult).then_inc(y2_p, 1)

            pool.wait_ge(kkv_a, 2)
            mix_step(1, tail=False)
            with pool.Fori(2, B + 1) as t:
                own.loop(t - 2, 4)
                mix_step(t)
            own.end(B - 1)
            mix_step(B + 1, mid=False)

            def sum_experts(k, first):
                for e in range(1, E):
                    pool.wait_ge(yw_v, k * E + e + 1)
                    if e > 1:
                        pool.wait_ge(acc_p, k * (E - 1) + e - 1)
                    elif not first:
                        pool.wait_ge(fin_v, k)
                    pool.tensor_tensor(acc[:], acc[:] if e > 1 else yw[0][:], yw[e % 2][:], ALU.add).then_inc(acc_p, 1)

            sum_experts(0, True)
            with pool.Fori(1, NB) as k:
                sum_experts(k, False)

        @block.scalar
        def _(act):
            own = Chain(act, act_own)

            for dst, src in mask_loads:
                act.dma_start(dst[:], a[src]).then_inc(mask_ld, 16)

            def context_rows():
                act.wait_ge(krow_mm, 1)
                act.wait_ge(rows_ld, 16 * len(rows_loads))
                act.activation(krow[:], ps1[0:2 * BH, 0:T], ACT.Identity, bias=gate_bias[:]).then_inc(krow_a, 1)

            def exp_gates(b, n, first):
                act.wait_ge(gsub_v, 2 * b + n + 1)
                if not first:
                    act.wait_ge(et_mm, 2 * b + n - 1)
                act.activation(g_exp[:, n, :], g_sub[:, n, :], ACT.Exp, scale=scale).then_inc(ge_a, 1)

            def copy_xnT(b):
                act.wait_ge(xn_mm, b + 1)
                act.copy(xkT[:].rearrange("c (n t) -> c n t", n=TT), ps3[:, 0:T].rearrange("c (n t) -> c n t", n=TT)[:, :, 0:L])
                act.copy(xnT[:], ps3[:, 0:T]).then_inc(xnT_a, 1)

            def normalise(t, rs, nb, xn, ready, done):
                act.wait_ge(ready, t + 1)
                for n in range(TT):
                    ins = act.activation(xn[:, n, :], x[:, t * TT + n, :], ACT.Identity, bias=nb[:, n:n + 1], scale=rs[:, n:n + 1])
                ins.then_inc(done, 1)

            normalise(0, rs1, nb1, xn1, rs1_p, xn1_a)
            copy_xnT(0)

            def step(t, front=True, nxt=True, tail=True, q=True):
                if front:
                    act.wait_ge(kT_v, t + 1)
                    if tail:
                        act.wait_ge(at_mm, t)
                    vps = ps3[:, 2 * P:3 * P].rearrange("q (p j) -> q p j", p=HP)
                    va = vaug[:, 0:HP * TT * WV].rearrange("q (p n j) -> q p n j", p=HP, n=TT)
                    act.copy(va[0:64, :, 0, 0:2 * D], vps[0:64])
                    act.copy(va[64:128, :, 1, 0:2 * D], vps[64:128]).then_inc(v_a, 1)
                if q:
                    normalise(t - 2, rs2, nb2, xn2, rs2_p, xn2_a)
                if nxt:
                    normalise(t + 1, rs1, nb1, xn1, rs1_p, xn1_a)
                if tail:
                    act.wait_ge(wt_mm, t)
                    act.copy(wu[:].rearrange("p g t -> p (g t)"), ps4[:]).then_inc(wu_a, 1)
                if front:
                    exp_gates(t, 0, not tail)
                if q:
                    act.wait_ge(q_mm, t - 1)
                    act.copy(qT[:, toks(t - 2)], ps3[:, T:2 * T]).then_inc(qT_a, 1)
                if front:
                    act.wait_ge(ssub_v, t + 1)
                    if tail:
                        act.wait_ge(pt_mm, t)
                    act.activation(prob[:], s_sub[:], ACT.Exp, scale=scale).then_inc(p_a, 1)

                def copy_eT(n, ps):
                    act.wait_ge(et_mm, 2 * t + n + 1)
                    act.copy(eT[:, :, n * P:(n + 1) * P], ps[:].rearrange("p (h t) -> p h t", h=HP)).then_inc(eT_a, 1)

                if front:
                    if tail:
                        act.wait_ge(wt_mm, t)
                    copy_eT(0, ps0)
                if nxt:
                    act.wait_ge(g_mm, 2 * t + 2)
                    copy_xnT(t + 1)
                if front:
                    act.wait_ge(pt_mm, t + 1)
                    if tail:
                        act.wait_ge(at_mm, t)
                    act.copy(pT[:], ps1[:]).then_inc(pT_a, 1)
                if tail:
                    act.wait_ge(wn_mm, t)
                    act.copy(wnT[:], ps4[:, 0:T]).then_inc(wnT_a, 1)
                if front:
                    exp_gates(t, 1, not tail)
                    copy_eT(1, ps2)

            step(0, tail=False, q=False)
            step(1, q=False)
            with act.Fori(2, B - 1) as t:
                step(t)
            step(B - 1, nxt=False)
            step(B, front=False, nxt=False)
            context_rows()
            step(B + 1, front=False, nxt=False, tail=False)

            act.wait_ge(gr_v, 1)
            f = slice(BH, 2 * BH)
            own.step(act.activation(f_abs[f, :], gr[f, :], ACT.Abs))
            own.step(act.activation(f_exp[f, :], f_abs[f, :], ACT.Exp, scale=-1.0))
            act.activation(f_log[f, :], f_exp[f, :], ACT.Ln, bias=1.0).then_inc(flog_a, 1)
            act.wait_ge(m_v, 1)
            act.activation(em[:], m_row[:], ACT.Exp, scale=-1.0).then_inc(em_a, 1)
            act.wait_ge(rowT_v, 1)

            def mix_step(t, front=True, mid=True, tail=True):
                def decays(h):
                    act.wait_ge(d_mm, 4 * t + h + 1)
                    if mid or h >= 2:
                        act.wait_ge(c_v, 4 * t + h - 1)
                    d = halves(ps0, h)
                    g0 = rowT[:, 0, 0, bass.ds(t * NH + h, 1)]
                    g1 = rowT[:, 0, 1, bass.ds(t * NH + h, 1)]
                    act.activation(decay[:, h % 2, 0:T], d[:, 0:T], ACT.Exp, bias=g0).then_inc(d_a, 1)
                    act.activation(decay[:, h % 2, T:T + P], d[:, T:T + P], ACT.Exp, bias=g1).then_inc(d_a, 1)

                if front:
                    decays(0)
                    decays(1)
                if mid:
                    act.wait_ge(pv_mm, t)
                    if tail:
                        act.wait_ge(ht_mm, t - 1)
                    act.copy(hs[:], ps2[:, 0:T])
                    act.copy(ss[:], ps2[:, 512:512 + T]).then_inc(hs_a, 1)
                if front:
                    decays(2)
                if mid:
                    act.wait_ge(ht_mm, t)
                    if tail:
                        act.wait_ge(var4_v, t - 1)
                    act.activation(sq[:].rearrange("p g d -> p (g d)"), ps4[:, 0:T], ACT.Square).then_inc(sq_a, 1)
                if tail:
                    normalise(t - 2, rs3, nb3, xn3, rs3_p, xn3_a)
                if front:
                    decays(3)
                if tail:
                    act.wait_ge(x3_mm, t - 1)
                    act.copy(xT[:, toks(t - 2)], ps2[:, 0:T]).then_inc(x3_a, 1)

            mix_step(0, mid=False, tail=False)
            mix_step(1, tail=False)
            with act.Fori(2, B) as t:
                mix_step(t)
            mix_step(B, front=False)
            mix_step(B + 1, front=False, mid=False)

            act.wait_ge(lsub_v, 1)
            act.activation(lexp[:], lsub[:], ACT.Exp).then_inc(lexp_a, 1)
            act.wait_ge(lexp_a, 1)
            act.activation(act_warm[:], lexp[:, 0, 0:1], ACT.Silu)

            def silus(k, first):
                for j in range(E + NSH):
                    n = k * (E + NSH) + j
                    act.wait_ge(gu_mm, n + 1)
                    if not first or j >= 2:
                        act.wait_ge(hh_v, n - 1)
                    act.activation(si[j % 2][:], halves(ps0, j), ACT.Silu).then_inc(si_a, 1)

            silus(0, True)
            with act.Fori(1, NB) as k:
                silus(k, False)

        @block.vector
        def _(dve):
            own = Chain(dve, dve_own)
            tt = dve.tensor_tensor

            def stats(b, bn):
                for n in range(TT):
                    own.count(dve.bn_stats(bn[:, n, :], x[:, b * TT + n, :]))

            def moments(bn, mv, done):
                for n in range(TT):
                    ins = dve.bn_aggr(mv[:, n, :], bn[:, n, :])
                    if n < TT - 1:
                        own.count(ins)
                ins.then_inc(done, 1)

            dve.wait_ge(x0_ld, 32)
            stats(0, bn1)
            own.wait()
            moments(bn1, mv1, var1_v)
            own.step(dve.memset(lat[:], 0.0))
            for h2 in range(2):
                own.step(dve.memset(lat[64 * h2:64 * h2 + 64, :, 2 * D + h2:2 * D + h2 + 1], 1.0))
            own.step(dve.memset(vaug[:], 0.0))
            va = vaug[:, 0:HP * TT * WV].rearrange("q (p n j) -> q p n j", p=HP, n=TT)
            for n in range(TT):
                own.step(dve.memset(va[64 * n:64 * n + 64, :, n, 2 * D:WV], 1.0))
            own.step(dve.memset(zeros[:], 0.0))
            own.step(dve.memset(ones_f[:], 1.0))
            own.step(dve.memset(ones_b[:], 1.0))
            own.step(dve.memset(carry[:], 1.0))
            own.step(dve.memset(carry[:, :, 0:1], 0.0))
            own.step(dve.tensor_copy(ident_b[:], ident[:]))
            dve.wait_ge(mask_ld, 16 * len(mask_loads))
            own.step(dve.tensor_copy(latent_mask_b[:], latent_mask[:]))
            own.step(dve.tensor_copy(causal_b[:], causal[:]))
            own.step(dve.tensor_copy(before_b[:], before[:]))
            for part in range(3):
                dve.tensor_copy(pick[BH * part:BH * part + BH],
                                ident[0:BH, 0:BH].unsqueeze(2).to_broadcast([BH, BH, P])).then_inc(const_v, 1)
            dve.wait_ge(x_ld, 16)
            dve.wait_ge(attn_ld, 16 * len(attn_loads))

            def subtract_max(ps, n_groups, mx, dst, ready, count, used, used_count, done):
                dve.wait_ge(ready, count)
                if used is not None:
                    dve.wait_ge(used, used_count)
                v = ps[:].rearrange("p (g l) -> p g l", g=n_groups)
                own.step(dve.tensor_reduce(mx, v, AX_X, ALU.max))
                tt(dst.rearrange("p (g l) -> p g l", g=n_groups), v, mx.unsqueeze(2).to_broadcast([P, n_groups, L]),
                   ALU.subtract).then_inc(done, 1)

            def step(t, front=True, nxt=True, tail=True):
                first = not tail
                if nxt:
                    stats(t + 1, bn1)
                if front:
                    dve.wait_ge(kv_mm, t + 1)
                    if not first:
                        dve.wait_ge(s_mm, t)
                    own.step(tt(k1[:], ps3[:, 0:P], cos[:], ALU.mult))
                    own.step(tt(k2[:], ps3[:, P:2 * P], sin[:], ALU.mult))
                    tt(kT[:], k1[:], k2[:], ALU.add).then_inc(kT_v, 1)
                if nxt:
                    moments(bn1, mv1, var1_v)
                if front:
                    subtract_max(ps0, H, g_max[:, 0, :], g_sub[:, 0, :], g_mm, 2 * t + 1,
                                 None if first else ge_a, 2 * t - 1, gsub_v)
                    subtract_max(ps1, 16, s_max[:], s_sub[:], s_mm, t + 1, None if first else p_a, t, ssub_v)
                if tail:
                    dve.wait_ge(wtr_mm, t)
                    w = ps4[:].rearrange("p (g j) -> p g j", j=32)
                    own.step(dve.reciprocal(w_rden[:].rearrange("p (g h) -> p g h", h=2), w[:, :, 2 * D:2 * D + 2]))
                    tt(wn[:].rearrange("p n (g h d) -> p (n g) h d", h=2, d=D),
                       w[:, :, 0:2 * D].rearrange("p g (h d) -> p g h d", h=2),
                       w_rden[:].rearrange("p (g h) -> p g h", h=2).unsqueeze(3).to_broadcast([P, TT * HP, 2, D]),
                       ALU.mult).then_inc(wn_v, 1)
                if front:
                    subtract_max(ps2, H, g_max[:, 1, :], g_sub[:, 1, :], g_mm, 2 * t + 2,
                                 None if first else ge_a, 2 * t, gsub_v)
                if tail:
                    dve.wait_ge(pr_mm, t)
                    tt(x[:, tiles(t - 1), :], x[:, tiles(t - 1), :], ps4[:, 0:T].rearrange("p (n c) -> p n c", n=TT),
                       ALU.add).then_inc(x1_v, 1)
                    dve.wait_ge(x1_v, t)
                    if not front:
                        stats(t - 1, bn2)
                        own.wait()
                        moments(bn2, mv2, var2_v)
                if front:
                    dve.wait_ge(at_mm, t + 1)
                    av = ps1[:].rearrange("q (p w) -> q p w", p=HP)
                    den = av[:, :, 0:TT * WV].rearrange("q p (n j) -> q p n j", n=TT)[:, :, :, 2 * D]
                    own.step(dve.reciprocal(a_rden[:], den))
                    for h2 in range(2):
                        r = slice(64 * h2, 64 * h2 + 64)
                        for n, dst in enumerate((a_n0, a_n1)):
                            o = WV * n + D * h2
                            if h2 == 1 and n == 0:
                                own.wait()
                            own.count(tt(dst[r], av[r, :, o:o + D],
                                         a_rden[r, :, n:n + 1].to_broadcast([64, HP, D]), ALU.mult))
                            if tail and h2 == n == 0:
                                stats(t - 1, bn2)
                    if tail:
                        moments(bn2, mv2, var2_v)
                        dve.wait_ge(wt_mm, t)
                    own.step(tt(lat[0:64, :, 0:D], a_n0[0:64], a_n1[0:64], ALU.add))
                    tt(lat[64:128, :, D:2 * D], a_n0[64:128], a_n1[64:128], ALU.add).then_inc(lat_v, 1)

            step(0, tail=False)
            with dve.Fori(1, B - 1) as t:
                own.loop(t - 1, ATTN_DVE_STEPS)
                step(t)
            own.end(B - 2)
            dve.wait_ge(rows_ld, 16 * len(rows_loads))
            tt(kk[:], kk[:], kv[:], ALU.add).then_inc(kkv_a, 1)
            dve.tensor_scalar(rms[:], rms[:], 1.0, None, ALU.add).then_inc(kkv_a, 1)
            step(B - 1, nxt=False)
            step(B, front=False, nxt=False)

            f = slice(BH, 2 * BH)
            dve.wait_ge(gates_mm, 1)
            dve.wait_ge(krow_a, 1)
            tt(gr[:], ps3[0:2 * BH, 0:T], krow[:], ALU.add).then_inc(gr_v, 1)
            dve.wait_ge(gr_v, 1)
            own.step(dve.tensor_scalar(f_min[f, :], gr[f, :], 0.0, None, ALU.min))
            dve.wait_ge(flog_a, 1)
            own.step(tt(logf[:], f_min[f, :], f_log[f, :], ALU.subtract))
            own.step(dve.tensor_tensor_scan(cs[:], logf[:], zeros[:], 0.0, ALU.add, ALU.add))
            tt(gi[:], gr[0:BH, :], cs[:], ALU.subtract).then_inc(gi_v, 1)
            dve.wait_ge(gi_v, 1)
            own.step(dve.tensor_tensor_scan(top[:], gi[:], gi[:], -3.0e38, ALU.max, ALU.max))
            tt(m_row[:], cs[:], top[:], ALU.add).then_inc(m_v, 1)
            own.step(dve.tensor_scalar(neg[:], top[:], -1.0, None, ALU.mult))
            own.step(dve.tensor_copy(neg_b1[:], neg[:]))
            own.step(dve.tensor_copy(neg3[0:BH, :], neg_b1[:]))
            own.step(tt(neg_r1[:], neg[:], neg_b1[:], ALU.subtract))
            own.step(dve.tensor_copy(neg_b2[:], neg_r1[:]))
            own.step(dve.tensor_copy(neg3[BH:2 * BH, :], neg_b2[:]))
            own.step(tt(neg_r2[:], neg_r1[:], neg_b2[:], ALU.subtract))
            dve.tensor_copy(neg3[2 * BH:3 * BH, :], neg_r2[:]).then_inc(neg3_v, 1)
            dve.wait_ge(rowT_mm, 1)
            dve.tensor_copy(rowT[:].rearrange("p a n r -> p (a n r)"), ps4[:, 0:4 * BH]).then_inc(rowT_v, 1)
            dve.wait_ge(rowT_v, 1)

            def mix_step(t, par, front=True, mid=True, tail=True):
                def weigh(h):
                    dve.wait_ge(qk_mm, 4 * t + h + 1)
                    dve.wait_ge(d_a, 2 * (4 * t + h + 1))
                    if tail and h == 0:
                        dve.wait_ge(pv_mm, t - 1)
                    dve.scalar_tensor_tensor(out=cc[par][:, h, :], in0=halves(ps1, h)[:, 0:384], scalar=qk_scale,
                                             in1=decay[:, h % 2, :], op0=ALU.mult, op1=ALU.mult).then_inc(c_v, 1)

                if tail:
                    dve.wait_ge(y2_p, t - 1)
                    tt(x[:, tiles(t - 2), :], x[:, tiles(t - 2), :], y2[:], ALU.add).then_inc(x2_v, 1)
                    dve.wait_ge(x2_v, t - 1)
                if front:
                    weigh(0)
                if tail:
                    stats(t - 2, bn3)
                    own.wait()
                    if not front:
                        dve.wait_ge(rs3_p, t - 2)
                if front:
                    weigh(1)
                if tail:
                    moments(bn3, mv3, var3_v)
                if front:
                    weigh(2)
                if mid:
                    dve.wait_ge(ht_mm, t)
                    sums = ps3[:, 0:T].rearrange("p (n h d) -> p n h d", n=TT, h=NH)[:, :, :, 0]
                    tt(n4[:], sums, rowT[:, 1, :, bass.ds((t - 1) * NH, NH)], ALU.max).then_inc(n4_v, 1)
                    dve.wait_ge(n4_v, t)
                    own.step(dve.tensor_scalar(n4e[:], n4[:], RMS_EPS, None, ALU.add))
                    own.step(dve.reciprocal(r4[:], n4e[:]))
                    own.step(tt(r4s[:], r4[:], r4[:], ALU.mult))
                    dve.wait_ge(sq_a, t)
                    own.step(dve.tensor_reduce(s4[:].rearrange("p n h -> p (n h)"), sq[:], AX_X, ALU.add))
                    dve.scalar_tensor_tensor(out=v4[:], in0=s4[:], scalar=1.0 / HD, in1=r4s[:],
                                             op0=ALU.mult, op1=ALU.mult).then_inc(var4_v, 1)
                if front:
                    weigh(3)
                if mid:
                    dve.wait_ge(rs4_p, t)
                    own.step(tt(f4[:], r4[:], rs4[:], ALU.mult))
                    if tail:
                        dve.wait_ge(y2_p, t - 1)
                    tt(y1[:].rearrange("p n (h d) -> p (n h) d", h=NH), ps4[:, 0:T].rearrange("p (g d) -> p g d", d=HD),
                       f4[:].rearrange("p n h -> p (n h)").unsqueeze(2).to_broadcast([P, TT * NH, HD]),
                       ALU.mult).then_inc(y_v, 1)

            x3_guard = lambda t: not isinstance(t, int) or t > 2
            mix_step(0, 0, mid=False, tail=False)
            mix_step(1, 1, tail=False)
            mix_step(2, 0)
            with dve.Fori(1, B // 2 - 0 - 1) as i:
                own.loop(i - 1, 2 * MIX_DVE_STEPS)
                mix_step(2 * i + 1, 1)
                mix_step(2 * i + 2, 0)
            own.end(B // 2 - 2)
            mix_step(B - 1, 1)
            mix_step(B, 0, front=False)
            mix_step(B + 1, 1, front=False, mid=False)

            dve.wait_ge(lg_mm, 1)
            lg = ps4[:, 0:NT * E].rearrange("p (n e) -> p n e", e=E)
            bc = lambda v: v.unsqueeze(2).to_broadcast([P, NT, E])
            own.step(dve.tensor_reduce(lmax[:], lg, AX_X, ALU.max))
            tt(lsub[:], lg, bc(lmax[:]), ALU.subtract).then_inc(lsub_v, 1)
            dve.wait_ge(lexp_a, 1)
            own.step(dve.tensor_reduce(lsum[:], lexp[:], AX_X, ALU.add))
            own.step(dve.reciprocal(lrec[:], lsum[:]))
            own.step(tt(score[:], lexp[:], bc(lrec[:]), ALU.mult))
            for n in range(NT):
                own.step(dve.max(top8[:, n, :], score[:, n, :]))
                own.step(dve.max_index(idx8[:, n, :], top8[:, n, :], score[:, n, :]))
            dve.wait_ge(exp_ld, 16 * len(exp_loads))
            for k in range(2):
                own.step(dve.tensor_copy(idxf[:, k, :], idx8[:, :, k]))
            own.step(tt(wsum[:], top8[:, :, 0], top8[:, :, 1], ALU.add))
            own.step(dve.tensor_scalar(wsum[:], wsum[:], 1e-20, None, ALU.add))
            own.step(dve.reciprocal(wrec[:], wsum[:]))
            bn_ = lambda v: v.unsqueeze(1).to_broadcast([P, E, NT])
            for k, one_hot, weight in ((0, oh0, ow0), (1, oh1, ow1)):
                own.step(tt(w2[:, k, :], top8[:, :, k], wrec[:], ALU.mult))
                own.step(tt(one_hot[:], ids[:], bn_(idxf[:, k, :]), ALU.is_equal))
                own.step(tt(weight[:], one_hot[:], bn_(w2[:, k, :]), ALU.mult))
            own.step(tt(ow[:], ow0[:], ow1[:], ALU.add))
            tt(ohb[:], oh0[:], oh1[:], ALU.add).then_inc(ohb_v, 1)
            dve.wait_ge(cnt_mm, 1)
            flat = lambda v: v[:].rearrange("p e n -> p (e n)")
            own.step(dve.tensor_copy(flat(tot), ps3[:, P:2 * P]))
            own.step(dve.tensor_tensor_scan(flat(pre), flat(carry), flat(tot), 0.0, ALU.mult, ALU.add))
            own.step(tt(flat(pre), flat(pre), flat(tot), ALU.subtract))
            own.step(tt(flat(pos), ps3[:, 0:P], flat(pre), ALU.add))
            dve.scalar_tensor_tensor(out=comb[:], in0=pos[:], scalar=float(CAP), in1=ow[:],
                                     op0=ALU.is_lt, op1=ALU.mult).then_inc(comb_v, 1)
            dve.wait_ge(comb_v, 1)

            def experts(k, first):
                def hidden(j):
                    n = k * (E + NSH) + j
                    dve.wait_ge(si_a, n + 1)
                    if not first or j >= 2:
                        dve.wait_ge(dn_mm, n - 1)
                    tt(hh[j % 2][:], halves(ps1, j), si[j % 2][:], ALU.mult).then_inc(hh_v, 1)

                def weighted(e):
                    dve.wait_ge(dn_mm, k * (E + NSH) + NSH + e + 1)
                    if not first or e >= 2:
                        dve.wait_ge(acc_p, k * (E - 1) + max(e - 2, 1) if e >= 2 else k * (E - 1))
                    tt(yw[e % 2][:], halves(ps2, e).rearrange("p (n c) -> p n c", n=BLK),
                       comb[:, e, bass.ds(k * BLK, BLK)].unsqueeze(2).to_broadcast([P, BLK, C]), ALU.mult).then_inc(yw_v, 1)

                for j in range(E + NSH):
                    hidden(j)
                    if j > NSH:
                        weighted(j - 1 - NSH)
                weighted(E - 1)
                xb = x[:, bass.ds(k * BLK, BLK), :]
                own.step(tt(fin[:], xb, ps3[:].rearrange("p (n c) -> p n c", n=BLK), ALU.add))
                dve.wait_ge(acc_p, (k + 1) * (E - 1))
                tt(xb, fin[:], acc[:], ALU.add).then_inc(fin_v, 1)

            experts(0, True)
            with dve.Fori(1, NB) as k:
                own.loop(k - 1, 1)
                experts(k, False)
            own.end(NB - 1)

        @block.tensor
        def _(pe):
            mm = pe.matmul

            def context_rows():
                pe.wait_ge(rows_ld, 16 * len(rows_loads))
                pe.wait_ge(kkv_a, 1)
                pe.wait_ge(lat_v, B)
                for b in range(B):
                    ins = mm(ps1[0:2 * BH, 0:T], kk[:, b, :], ctxT[:, b * T:(b + 1) * T], start=(b == 0), stop=(b == B - 1))
                ins.then_inc(krow_mm, 1)

            def transpose_xn(b):
                pe.wait_ge(xn1_a, b + 1)
                for n in range(TT):
                    ins = pe.transpose(ps3[:, n * P:(n + 1) * P], xn1[:, n, :], ident[:])
                ins.then_inc(xn_mm, 1)

            pe.wait_ge(x0_ld, 32)
            transpose_xn(0)
            pe.wait_ge(attn_ld, 16 * len(attn_loads))

            def step(t, front=True, nxt=True, tail=True, q=True):
                first = not tail

                def gates(n, ps):
                    if not first:
                        pe.wait_ge(eT_a, 2 * t - 1 + n)
                    for j in range(2):
                        ins = mm(ps[:, 512 * j:512 * j + 512], xnT[:, n * P:(n + 1) * P], wg[:, 512 * j:512 * j + 512],
                                 start=True, stop=True)
                    ins.then_inc(g_mm, 1)

                if front:
                    pe.wait_ge(xnT_a, t + 1)
                    mm(ps3[:, 0:P], wk[:], xkT[:], start=True, stop=True)
                    mm(ps3[:, P:2 * P], wkr[:], xkT[:], start=True, stop=True)
                    mm(ps3[:, 2 * P:3 * P], xkT[:], wv[:], start=True, stop=True).then_inc(kv_mm, 1)
                    gates(0, ps0)
                if tail:
                    pe.wait_ge(eT_a, 2 * t)
                    pe.wait_ge(lat_v, t)
                    if q:
                        pe.wait_ge(x1_v, t - 1)
                    for p in range(HP):
                        r = 32 * (p % 4)
                        ins = mm(ps4[r:r + 32, T * (p // 4):T * (p // 4) + T], lat[:, p, :], eT[:, p, :],
                                 start=True, stop=True)
                    ins.then_inc(wt_mm, 1)
                if front:
                    pe.wait_ge(kT_v, t + 1)
                    if first:
                        pe.wait_ge(const_v, 3)
                    if not first:
                        pe.wait_ge(lat_v, t)
                    for half in range(2):
                        bank = ps1[:, 512 * half:512 * half + 512]
                        mm(bank, ident_b[:], latent_mask_b[:], start=True, stop=True)
                        for j in range(4):
                            ins = mm(bank[:, P * j:P * j + P], qblk[:, 4 * half + j, :], kT[:], start=False, stop=True,
                                     skip_group_check=True)
                    ins.then_inc(s_mm, 1)
                if q:
                    pe.wait_ge(xn2_a, t - 1)
                    if front:
                        pe.wait_ge(v_a, t + 1)
                    for n in range(TT):
                        ins = pe.transpose(ps3[:, T + n * P:T + n * P + P], xn2[:, n, :], ident[:])
                    ins.then_inc(q_mm, 1)
                if front:
                    gates(1, ps2)
                if tail:
                    pe.wait_ge(wu_a, t)
                    for n in range(TT):
                        for g in range(2):
                            ins = pe.transpose(ps4[:, (2 * n + g) * P:(2 * n + g + 1) * P], wu[:, g, n * P:(n + 1) * P], ident[:])
                    ins.then_inc(wtr_mm, 1)
                if nxt:
                    if q:
                        pe.wait_ge(qT_a, t - 1)
                    else:
                        pe.wait_ge(v_a, t + 1)
                    transpose_xn(t + 1)

                def transpose_gates(n, ps):
                    pe.wait_ge(ge_a, 2 * t + n + 1)
                    for p in range(HP):
                        ins = pe.transpose(ps[:, p * P:(p + 1) * P], g_exp[:, n, p * P:(p + 1) * P], ident[:])
                    ins.then_inc(et_mm, 1)

                if front:
                    transpose_gates(0, ps0)
                    pe.wait_ge(p_a, t + 1)
                    for p in range(HP):
                        ins = pe.transpose(ps1[:, p * P:(p + 1) * P], prob[:, p * P:(p + 1) * P], ident[:])
                    ins.then_inc(pt_mm, 1)
                if tail:
                    pe.wait_ge(wn_v, t)
                    for n in range(TT):
                        ins = pe.transpose(ps4[:, n * P:(n + 1) * P], wn[:, n, :], ident[:])
                    ins.then_inc(wn_mm, 1)
                if front:
                    pe.wait_ge(pT_a, t + 1)
                    for p in range(HP):
                        w = p * TT * WV
                        ins = mm(ps1[:, p * P:(p + 1) * P], pT[:, p * P:(p + 1) * P], vaug[:, w:w + P], start=True, stop=True)
                    ins.then_inc(at_mm, 1)
                if tail:
                    pe.wait_ge(wnT_a, t)
                    for n in range(TT):
                        ins = mm(ps4[:, n * P:(n + 1) * P], wnT[:, n * P:(n + 1) * P], wp[:], start=True, stop=True)
                    ins.then_inc(pr_mm, 1)
                if front:
                    transpose_gates(1, ps2)

            step(0, tail=False, q=False)
            step(1, q=False)
            with pe.Fori(2, B - 1) as t:
                step(t)
            step(B - 1, nxt=False)
            step(B, front=False, nxt=False)
            context_rows()
            step(B + 1, front=False, nxt=False, tail=False)

            pe.wait_ge(qT_a, B)
            for b in range(B):
                ins = mm(ps3[0:2 * BH, 0:T], kq[:, b, :], qT[:, b * T:(b + 1) * T], start=(b == 0), stop=(b == B - 1))
            ins.then_inc(gates_mm, 1)
            pe.wait_ge(gi_v, 1)
            pe.wait_ge(em_a, 1)
            for i, src in enumerate((gi, em)):
                for n in range(TT):
                    o = (TT * i + n) * BH
                    ins = pe.transpose(ps4[:, o:o + BH], src[:, n * P:(n + 1) * P], ident[0:BH, 0:BH])
            ins.then_inc(rowT_mm, 1)
            pe.wait_ge(neg3_v, 1)
            pe.wait_ge(rowT_v, 1)

            def mix_step(t, par, front=True, mid=True, tail=True):
                def scores(h):
                    d, s = halves(ps0, h), halves(ps1, h)
                    if mid or h >= 2:
                        pe.wait_ge(d_a, 2 * (4 * t + h - 1))
                    sel = pick[:, bass.ds(t * NH + h, 1), :].rearrange("r a p -> r (a p)")
                    mm(d[:, 0:T], sel, neg3[:], start=True, stop=True)
                    mm(d[:, T:T + P], sel, neg3[:, P:T], start=False, stop=True, skip_group_check=True)
                    mm(d[:, 0:P], ident_b[:], causal_b[:], start=False, stop=True, skip_group_check=True)
                    mm(d[:, T:T + P], ident_b[:], causal_b[:], start=False, stop=True, skip_group_check=True).then_inc(d_mm, 1)
                    if mid or h >= 2:
                        pe.wait_ge(c_v, 4 * t + h - 1)
                    mm(s[:, 0:T], kTm[par][:, h, 0:P], qT[:, toks(t)], start=True, stop=True)
                    mm(s[:, T:T + P], kTm[par][:, h, P:T], qT[:, bass.ds(t * T + P, P)], start=False, stop=True,
                       skip_group_check=True).then_inc(qk_mm, 1)

                if front:
                    pe.wait_ge(kv_ld[par], KV_LOADS * 16 * ((t - par) // 2 + 1) if isinstance(t, int) else kv_count[0])
                    scores(0)
                    scores(1)
                if mid:
                    pe.wait_ge(c_v, 4 * t)
                    if tail:
                        pe.wait_ge(x3_a, t - 2) if x3_guard(t) else None
                        pe.wait_ge(hs_a, t - 1)
                    o = 1 - par
                    for src, col in ((None, 0), (ones_f, 512)):
                        for n in range(TT):
                            for h in range(NH):
                                rows = slice(HD * h, HD * h + HD)
                                w = ones_f[:] if src is not None else vv[o][:, n, rows]
                                c0 = col + n * P
                                m_ = cc[o][:, h, 0:T] if n == 0 else cc[o][:, h, T:T + P]
                                ins = mm(ps2[rows, c0:col + T], w, m_, start=(n == 0), stop=True, skip_group_check=True)
                    ins.then_inc(pv_mm, 1)
                if front:
                    scores(2)
                if mid:
                    pe.wait_ge(hs_a, t)
                    if tail:
                        pe.wait_ge(y_v, t - 1)
                        pe.wait_ge(n4_v, t - 1)
                    for src, ps in ((hs, ps4), (ss, ps3)):
                        for n in range(TT):
                            ins = pe.transpose(ps[:, n * P:(n + 1) * P], src[:, n * P:(n + 1) * P], ident[:])
                    ins.then_inc(ht_mm, 1)
                if front:
                    scores(3)
                if tail:
                    pe.wait_ge(xn3_a, t - 1)
                    if mid:
                        pe.wait_ge(hs_a, t)
                    else:
                        pe.wait_ge(x3_a, t - 2)
                    for n in range(TT):
                        ins = pe.transpose(ps2[:, n * P:(n + 1) * P], xn3[:, n, :], ident[:])
                    ins.then_inc(x3_mm, 1)

            x3_guard = lambda t: not isinstance(t, int) or t > 2
            kv_count = [0]
            mix_step(0, 0, mid=False, tail=False)
            mix_step(1, 1, tail=False)
            mix_step(2, 0)
            with pe.Fori(1, B // 2 - 1) as i:
                kv_count[0] = KV_LOADS * 16 * (i + 1)
                mix_step(2 * i + 1, 1)
                kv_count[0] = KV_LOADS * 16 * (i + 2)
                mix_step(2 * i + 2, 0)
            mix_step(B - 1, 1)
            mix_step(B, 0, front=False)
            mix_step(B + 1, 1, front=False, mid=False)

            pe.wait_ge(exp_ld, 16 * len(exp_loads))
            pe.wait_ge(x3_a, B)
            pe.wait_ge(y_v, B)
            pe.wait_ge(n4_v, B)
            for n in range(NT):
                ins = mm(ps4[:, n * E:n * E + 96], xT[:, n * P:(n + 1) * P], gate_w[:], start=True, stop=True)
            ins.then_inc(lg_mm, 1)
            pe.wait_ge(ohb_v, 1)
            ohf = ohb[:].rearrange("p e n -> p (e n)")
            mm(ps3[:, 0:P], before_b[:], ohf, start=True, stop=True)
            mm(ps3[:, P:2 * P], ones_b[:], ohf, start=True, stop=True).then_inc(cnt_mm, 1)

            def experts(k, first):
                def up(j):
                    n, e = k * (E + NSH) + j, (j - NSH) % (E + NSH)
                    if not first or j >= 2:
                        pe.wait_ge(si_a, n - 1)
                        pe.wait_ge(hh_v, n - 1)
                    cols = xT[:, bass.ds(k * BLK * P, BLK * P)]
                    mm(halves(ps0, j), we_g[:, e, :], cols, start=True, stop=True)
                    mm(halves(ps1, j), we_u[:, e, :], cols, start=True, stop=True).then_inc(gu_mm, 1)

                def down(j):
                    n, e = k * (E + NSH) + j, (j - NSH) % (E + NSH)
                    pe.wait_ge(hh_v, n + 1)
                    shared = j < NSH
                    if j == 0:
                        pe.wait_ge(comb_v, 1) if first else pe.wait_ge(fin_v, k)
                    if not shared and (not first or j - NSH >= 2):
                        pe.wait_ge(yw_v, k * E + j - NSH - 1)
                    ps = ps3[:] if shared else halves(ps2, j)
                    for m in range(BLK):
                        start = (m == 0) if j == 0 or not shared else False
                        ins = mm(ps[:, m * P:(m + 1) * P], hh[j % 2][:, m * P:(m + 1) * P], we_d[:, e, :],
                                 start=start, stop=True, skip_group_check=True)
                    ins.then_inc(dn_mm, 1)

                for j in range(E + NSH):
                    up(j)
                    if j:
                        down(j - 1)
                down(E + NSH - 1)

            experts(0, True)
            with pe.Fori(1, NB) as k:
                experts(k, False)


def kernel(x, ctx_1024, L0_attn_latent_queries, L0_attn_W_k, L0_attn_W_v, L0_attn_W_g, L0_attn_W_p,
           L0_xattn_igate_kernel, L0_xattn_igate_bias, L0_xattn_fgate_kernel, L0_xattn_fgate_bias,
           L0_xattn_rms_scale, L0_ffn_gate_w, L0_ffn_we_gate, L0_ffn_we_up, L0_ffn_we_down,
           L0_ffn_ws_gate, L0_ffn_ws_up, L0_ffn_ws_down):
    import concourse.bacc as bacc
    from concourse.bass_utils import run_bass_kernel_spmd

    con = np.ascontiguousarray
    latents = np.asarray(L0_attn_latent_queries)[0]
    qblk = np.zeros((H, D, HP, 2, L), np.float32)
    for h in range(H):
        qblk[h, :, h // 2, h % 2, :] = latents[:, h, :].T
    wkT = np.asarray(L0_attn_W_k).T
    swap = np.arange(C) ^ 1
    ik, fk = np.asarray(L0_xattn_igate_kernel), np.asarray(L0_xattn_fgate_kernel)

    def gate_kernel(part):
        g = np.zeros((C, B, 2, B, NH), np.float32)
        for b in range(B):
            g[:, b, 0, b, :] = ik[part * C:(part + 1) * C]
            g[:, b, 1, b, :] = fk[part * C:(part + 1) * C]
        return g.reshape(C, B, 2 * BH)

    gate_w = np.zeros((C, 96), np.float32)
    gate_w[:, 0:E] = np.asarray(L0_ffn_gate_w).T

    def experts(routed, shared, down):
        r, s = np.asarray(routed), np.asarray(shared)
        s = s.reshape(C, NSH, I).transpose(1, 0, 2) if down else s.reshape(NSH, I, C)
        return con(np.concatenate([r, s]).transpose(2, 0, 1))

    arrays = {
        "x": con(x), "ctx": con(ctx_1024), "ctxT": con(np.asarray(ctx_1024).reshape(B * T, C).T),
        "wkT": con(wkT), "wkrT": con(wkT[:, swap]), "wvT": con(np.asarray(L0_attn_W_v).T),
        "wgT": con(np.asarray(L0_attn_W_g).T), "wpT": con(np.asarray(L0_attn_W_p).T),
        "qblk": qblk.reshape(C, HP, P),
        "kq": gate_kernel(0), "kk": gate_kernel(1), "kv": gate_kernel(2),
        "gate_bias": con(np.concatenate([np.tile(L0_xattn_igate_bias, B), np.tile(L0_xattn_fgate_bias, B)])[:, None]),
        "rms": con(np.broadcast_to(np.tile(L0_xattn_rms_scale, NH), (P, TT, C))),
        "gate_w": gate_w,
        "we_g": experts(L0_ffn_we_gate, L0_ffn_ws_gate, False),
        "we_u": experts(L0_ffn_we_up, L0_ffn_ws_up, False),
        "we_d": experts(L0_ffn_we_down, L0_ffn_ws_down, True),
        **constants(),
    }
    nc = bacc.Bacc("TRN2", target_bir_lowering=False, num_devices=1)
    ins = {n: nc.dram_tensor(f"in_{n}", v.shape, mybir.dt.from_np(v.dtype), kind="ExternalInput").ap() for n, v in arrays.items()}
    out = nc.dram_tensor("out", (B, T, C), F32, kind="ExternalOutput").ap()
    decoder_layer(nc, ins, out)
    r = run_bass_kernel_spmd(nc, [{f"in_{n}": v for n, v in arrays.items()}], core_ids=[0])
    return r.results[0]["out"]
```

```python
from contextlib import ExitStack

import numpy as np

import concourse.bass as bass
from concourse import mybir

ALU = mybir.AluOpType
ACT = mybir.ActivationFunctionType
AX_X = mybir.AxisListType.X
F32 = mybir.dt.float32
BF16 = mybir.dt.bfloat16
U32 = mybir.dt.uint32
F32R = mybir.dt.float32r

B, T, C = 8, 256, 128
P = 128
TT = T // P
NT = B * TT
H, L, D = 16, 64, 8
HP = H // 2
NH, HD = 4, 32
BH = B * NH
E, I = 8, 128
NSH = 2
CAP = 640
BLK = 4
NB = NT // BLK
WV = 2 * D + 1
VCOLS = (HP - 1) * TT * WV + P
LN_EPS = 1e-5
RMS_EPS = 1e-6
ATTN_DVE_STEPS = 18
MIX_DVE_STEPS = 8
NEG = -1.0e30

def constants():
    pos = np.concatenate([np.arange(L) + n * P for n in range(TT)]).astype(np.float32)
    inv = (np.float32(1.0) / np.float32(10000.0) ** (np.arange(0, D, 2, dtype=np.float32) / np.float32(D))).astype(np.float32)
    ang = pos[None, :] * inv[(np.arange(C) % D) // 2][:, None]
    sign = np.where(np.arange(C) % 2 == 0, -1.0, 1.0).astype(np.float32)[:, None]
    latent = np.where(np.arange(L)[None, :] <= (np.arange(P) % L)[:, None], 0.0, NEG)
    i = np.arange(P)
    return {
        "ident": np.eye(P, dtype=np.float32),
        "rope_cos": np.cos(ang).astype(np.float32),
        "rope_sin": (np.sin(ang) * sign).astype(np.float32),
        "latent_mask": np.tile(latent, (1, 8)).astype(np.float32),
        "causal_mask": np.where(i[:, None] <= i[None, :], 0.0, NEG).astype(np.float32),
        "before": (i[:, None] < i[None, :]).astype(np.float32),
        "expert_ids": np.tile(np.repeat(np.arange(E), NT)[None, :], (P, 1)).astype(np.float32),
    }


class Chain:

    def __init__(self, eng, sem):
        self.eng, self.sem, self.total, self.base, self.k = eng, sem, 0, 0, 0

    def loop(self, t, per):
        self.total += self.k
        self.base, self.per, self.k = self.total + t * per, per, 0

    def end(self, n):
        assert self.k == self.per, f"steps in the loop: {self.k}"
        self.total += n * self.per
        self.base, self.k = self.total, 0

    def count(self, ins):
        self.k += 1
        ins.then_inc(self.sem, 1)

    def wait(self):
        self.eng.wait_ge(self.sem, self.base + self.k)

    def step(self, ins):
        self.count(ins)
        self.wait()


def decoder_layer(nc, a, out):
    scale = 1.0 / float(np.sqrt(D))
    qk_scale = 1.0 / float(np.sqrt(HD))
    with ExitStack() as ctx:
        def sb(name, shape, dt=F32):
            return ctx.enter_context(nc.sbuf_tensor(name, shape, dt))

        def pb(name, shape):
            return ctx.enter_context(nc.psum_tensor(name, shape, F32))

        def sem(name):
            return ctx.enter_context(nc.semaphore(name))

        x = sb("x_res", [P, NT, C])
        qT = sb("qT", [C, B * T])
        xT = sb("xT", [C, B * T])
        ctxT = sb("ctxT_s", [C, B * T])
        wk, wkr, wv, wp = (sb(n, [C, C]) for n in ("wk", "wkr", "wv", "wp"))
        wg = sb("wg", [C, H * L])
        qblk = sb("qblk_s", [C, HP, P])
        we_g, we_u, we_d = (sb(n, [P, E + NSH, P]) for n in ("we_g_s", "we_u_s", "we_d_s"))
        we_parts = [[sb(f"we_{w}_{p}", [P, E + NSH, P], F32R) for p in ("hi", "lo")] for w in ("g", "u")]
        x_hi, x_lo = sb("x_hi", [C, B * T], F32R), sb("x_lo", [C, B * T], F32R)
        gate_w = sb("gate_w_s", [C, 96])
        kq, kk, kv = (sb(n, [C, B, 2 * BH]) for n in ("kq_s", "kk_s", "kv_s"))
        gate_bias = sb("gate_bias_s", [2 * BH, 1])
        rms = sb("rms_s", [P, TT, C])
        ident, ident_b = sb("ident_s", [P, P]), sb("ident_b", [P, P], BF16)
        cos, sin = sb("cos", [C, P]), sb("sin", [C, P])
        latent_mask, latent_mask_b = sb("latent_mask_s", [P, 512]), sb("latent_mask_b", [P, 512], BF16)
        causal, causal_b = sb("causal_s", [P, P]), sb("causal_b", [P, P], BF16)
        before, before_b = sb("before_s", [P, P]), sb("before_b", [P, P], BF16)
        ones_b, ones_f = sb("ones_b", [P, P], BF16), sb("ones_f", [P, HD])
        pick = sb("pick", [3 * BH, BH, P], BF16)
        ids = sb("ids", [P, E, NT])
        minus = sb("minus", [P, TT])
        mhalf, ln_eps, rms_eps = sb("mhalf", [P, TT * NH]), sb("ln_eps", [P, TT]), sb("rms_eps", [P, TT, NH])
        bn1, bn2, bn3 = (sb(f"bn{i}", [P, TT, 6]) for i in (1, 2, 3))
        mv1, mv2, mv3 = (sb(f"mv{i}", [P, TT, 2]) for i in (1, 2, 3))
        ve1, ve2, ve3 = (sb(f"ve{i}", [P, TT]) for i in (1, 2, 3))
        rs1, rs2, rs3 = (sb(f"rs{i}", [P, TT]) for i in (1, 2, 3))
        nb1, nb2, nb3 = (sb(f"nb{i}", [P, TT]) for i in (1, 2, 3))
        xn1, xn2, xn3 = (sb(f"xn{i}", [P, TT, C]) for i in (1, 2, 3))
        xnT, xkT = sb("xnT", [C, T]), sb("xkT", [C, P])
        k1, k2, kT = sb("k1", [C, P]), sb("k2", [C, P]), sb("kT", [C, P])
        vaug = sb("vaug", [P, VCOLS])
        s_max, s_work = sb("s_max", [P, 16]), sb("s_work", [P, 3, 1024])
        s_sub, prob, pT = (s_work[:, i, :] for i in range(3))
        g_max, g_sub, g_exp = sb("g_max", [P, TT, H]), sb("g_sub", [P, TT, 1024]), sb("g_exp", [P, TT, 1024])
        eT = sb("eT", [P, HP, T])
        a_rden, a_n0, a_n1 = sb("a_rden", [P, HP, TT]), sb("a_n0", [P, HP, D]), sb("a_n1", [P, HP, D])
        lat = sb("lat", [P, HP, 32])
        wu, wnT = sb("wu", [P, 2, T]), sb("wnT", [C, T])
        w_rden, wn = sb("w_rden", [P, NH * HP]), sb("wn", [P, TT, C])
        krow, gr = sb("krow", [2 * BH, T]), sb("gr", [2 * BH, T])
        f_abs, f_exp, f_log, f_min = (sb(n, [2 * BH, T]) for n in ("f_abs", "f_exp", "f_log", "f_min"))
        logf, cs, zeros, gi, top, m_row, em = (sb(n, [BH, T]) for n in ("logf", "cs", "zeros_r", "gi", "top", "m_row", "em"))
        neg, neg_r1, neg_r2 = (sb(n, [BH, T]) for n in ("neg", "neg_r1", "neg_r2"))
        neg_b1, neg_b2 = sb("neg_b1", [BH, T], BF16), sb("neg_b2", [BH, T], BF16)
        neg3 = sb("neg3", [3 * BH, T], BF16)
        rowT = sb("rowT", [P, 2, TT, BH])
        kTm = [sb(f"kTm{i}", [C, NH, T]) for i in range(2)]
        vv = [sb(f"vv{i}", [P, TT, C]) for i in range(2)]
        decay = sb("decay", [P, 2, 384])
        cc = [v.rearrange(r, h=NH) for v, r in (
            (eT[:].rearrange("p g t -> p (g t)")[:, 0:NH * 384], "p (h t) -> p h t"),
            (s_work[:].rearrange("p a t -> p (a t)")[:, 0:NH * 384], "p (h t) -> p h t"))]
        hs, ss, sq = wnT, wu[:, 1, :], sb("sq", [P, TT * NH, HD])
        n4, n4e, r4, s4, r4s, v4, ve4, rs4, f4 = (sb(n, [P, TT, NH]) for n in ("n4", "n4e", "r4", "s4", "r4s", "v4", "ve4", "rs4", "f4"))
        y1, y2 = wn, wu[:, 0, :].rearrange("p (n c) -> p n c", n=TT)
        lmax, lsub, lexp = sb("lmax", [P, NT]), sb("lsub", [P, NT, E]), sb("lexp", [P, NT, E])
        lsum, lrec, score = sb("lsum", [P, NT]), sb("lrec", [P, NT]), sb("score", [P, NT, E])
        top8, idx8, idxf = sb("top8", [P, NT, 8]), sb("idx8", [P, NT, 8], U32), sb("idxf", [P, 2, NT])
        wsum, wrec, w2 = sb("wsum", [P, NT]), sb("wrec", [P, NT]), sb("w2", [P, 2, NT])
        oh0, oh1, ohb = sb("oh0", [P, E, NT]), sb("oh1", [P, E, NT]), sb("ohb", [P, E, NT], BF16)
        carry, tot, pre, pos = (sb(n, [P, E, NT]) for n in ("carry", "tot", "pre", "pos"))
        ow0, ow1, ow, comb = (sb(n, [P, E, NT]) for n in ("ow0", "ow1", "ow", "comb"))
        si = [g_sub[:, 0, BLK * P * i:BLK * P * (i + 1)] for i in range(2)]
        hh = [g_sub[:, 1, BLK * P * i:BLK * P * (i + 1)] for i in range(2)]
        yw = [g_exp[:, 0, BLK * P * i:BLK * P * (i + 1)].rearrange("p (n c) -> p n c", n=BLK) for i in range(2)]
        acc = g_exp[:, 1, 0:BLK * P].rearrange("p (n c) -> p n c", n=BLK)

        ps0, ps1, ps2 = pb("ps0", [P, 1024]), pb("ps1", [P, 1024]), pb("ps2", [P, 1024])
        ps3, ps4 = pb("ps3", [P, 512]), pb("ps4", [P, 512])

        x0_ld, x_ld, attn_ld, mask_ld, rows_ld, exp_ld = (sem(n) for n in ("x0_ld", "x_ld", "attn_ld", "mask_ld", "rows_ld", "exp_ld"))
        key_ld, val_ld = [sem(f"key_ld{i}") for i in range(2)], [sem(f"val_ld{i}") for i in range(2)]
        out_st = sem("out_st")
        const_v, const_p = sem("const_v"), sem("const_p")
        we_p, xlo_v = sem("we_p"), sem("xlo_v")
        dve_own, act_own, pool_own = sem("dve_own"), sem("act_own"), sem("pool_own")
        krow_mm, krow_a = sem("krow_mm"), sem("krow_a")
        kv_mm, g_mm, s_mm, pt_mm, at_mm, et_mm = (sem(n) for n in ("kv_mm", "g_mm", "s_mm", "pt_mm", "at_mm", "et_mm"))
        wt_mm, wtr_mm, wn_mm, pr_mm, xn_mm, q_mm = (sem(n) for n in ("wt_mm", "wtr_mm", "wn_mm", "pr_mm", "xn_mm", "q_mm"))
        ge_a, p_a, wu_a, wnT_a, xnT_a, pT_a, eT_a, qT_a = (sem(n) for n in ("ge_a", "p_a", "wu_a", "wnT_a", "xnT_a", "pT_a", "eT_a", "qT_a"))
        var1_v, var2_v, var3_v = sem("var1_v"), sem("var2_v"), sem("var3_v")
        rs1_p, rs2_p, rs3_p = sem("rs1_p"), sem("rs2_p"), sem("rs3_p")
        xn1_a, xn2_a, xn3_a = sem("xn1_a"), sem("xn2_a"), sem("xn3_a")
        kT_v, v_a, gsub_v, ssub_v, lat_v, wn_v, x1_v = (sem(n) for n in ("kT_v", "v_a", "gsub_v", "ssub_v", "lat_v", "wn_v", "x1_v"))
        kkv_a, gates_mm, gr_v, flog_a, m_v, em_a, gi_v, neg3_v, rowT_mm, rowT_v = (
            sem(n) for n in ("kkv_a", "gates_mm", "gr_v", "flog_a", "m_v", "em_a", "gi_v", "neg3_v", "rowT_mm", "rowT_v"))
        d_mm, qk_mm, d_a, c_v, pv_mm, hs_a, ht_mm = (sem(n) for n in ("d_mm", "qk_mm", "d_a", "c_v", "pv_mm", "hs_a", "ht_mm"))
        sq_a, n4_v, var4_v, rs4_p, y_v, y2_p, x2_v, x3_mm, x3_a = (
            sem(n) for n in ("sq_a", "n4_v", "var4_v", "rs4_p", "y_v", "y2_p", "x2_v", "x3_mm", "x3_a"))
        lg_mm, lsub_v, lexp_a, ohb_v, cnt_mm, comb_v = (sem(n) for n in ("lg_mm", "lsub_v", "lexp_a", "ohb_v", "cnt_mm", "comb_v"))
        gu_mm, si_a, hh_v, dn_mm, sx_v, yw_v, acc_p, fin_v = (
            sem(n) for n in ("gu_mm", "si_a", "hh_v", "dn_mm", "sx_v", "yw_v", "acc_p", "fin_v"))

        block = ctx.enter_context(nc.Block())

        x_dram = a["x"].rearrange("b (n p) d -> p (b n) d", p=P)
        ctx_dram = a["ctx"].rearrange("b (n p) d -> b p n d", p=P)
        out_dram = out.rearrange("b (n p) d -> p (b n) d", p=P)
        attn_loads = ((wk, "wkT"), (wkr, "wkrT"), (wv, "wvT"), (cos, "rope_cos"), (sin, "rope_sin"), (wg, "wgT"),
                      (qblk, "qblk"), (wp, "wpT"))
        mask_loads = ((latent_mask, "latent_mask"), (causal, "causal_mask"), (before, "before"))
        rows_loads = ((ctxT, "ctxT"), (kq, "kq"), (kk, "kk"), (kv, "kv"), (gate_bias, "gate_bias"), (rms, "rms"))
        exp_loads = ((gate_w, "gate_w"), (ids, "expert_ids"), (we_g, "we_g"), (we_u, "we_u"), (we_d, "we_d"))
        tiles = lambda b: bass.ds(b * TT, TT)
        toks = lambda b: bass.ds(b * T, T)
        routed = lambda k, e: NSH * NB + k * E + e
        halves = lambda ps, j: ps[:, 512 * (j % 2):512 * (j % 2) + 512]

        @block.sync
        def _(sp):
            sp.dma_start(x[:, 0:TT, :], x_dram[:, 0:TT, :]).then_inc(x0_ld, 16)
            sp.dma_start(ident[:], a["ident"]).then_inc(x0_ld, 16)
            for dst, src in attn_loads:
                sp.dma_start(dst[:], a[src]).then_inc(attn_ld, 16)
            sp.dma_start(x[:, TT:NT, :], x_dram[:, TT:NT, :]).then_inc(x_ld, 16)
            for dst, src in rows_loads:
                sp.dma_start(dst[:], a[src]).then_inc(rows_ld, 16)
            for dst, src in exp_loads:
                sp.dma_start(dst[:], a[src]).then_inc(exp_ld, 16)

            def load_keys(b, par):
                for h in range(NH):
                    rows = slice(HD * h, HD * h + HD)
                    sp.dma_start(kTm[par][rows, h, :], a["ctxT"][rows, toks(b)]).then_inc(key_ld[par], 16)

            def load_values(b, par):
                sp.dma_start(vv[par][:], ctx_dram[b]).then_inc(val_ld[par], 16)

            sp.wait_ge(const_p, 2)
            for par in range(2):
                load_keys(par, par)
                load_values(par, par)
            with sp.Fori(0, B // 2 - 1) as i:
                for par in range(2):
                    sp.wait_ge(qk_mm, NH * (2 * i + par + 1))
                    load_keys(2 * i + par + 2, par)
                    sp.wait_ge(pv_mm, 2 * i + par + 1)
                    load_values(2 * i + par + 2, par)
            with sp.Fori(0, NB) as k:
                sp.wait_ge(fin_v, k + 1)
                sp.dma_start(out_dram[:, bass.ds(k * BLK, BLK), :], x[:, bass.ds(k * BLK, BLK), :]).then_inc(out_st, 16)
            sp.wait_ge(out_st, 16 * NB)

        @block.gpsimd
        def _(pool):
            own = Chain(pool, pool_own)
            own.step(pool.memset(mhalf[:], -0.5))
            own.step(pool.memset(minus[:], -1.0))
            own.step(pool.memset(ln_eps[:], LN_EPS))
            own.step(pool.memset(rms_eps[:], RMS_EPS))
            pool.memset(kTm[0][:], 0.0).then_inc(const_p, 1)
            pool.memset(kTm[1][:], 0.0).then_inc(const_p, 1)

            def root(var_ready, b, var, eps, ve, rs, done):
                pool.wait_ge(var_ready, b + 1)
                own.step(pool.tensor_tensor(ve, var, eps, ALU.add))
                pool.tensor_tensor(rs, ve, mh4, ALU.pow).then_inc(done, 1)

            def scale_bias(var_ready, b, mv, ve, rs, nb, applied, done):
                pool.wait_ge(var_ready, b + 1)
                if isinstance(b, int) and b > 0:
                    pool.wait_ge(applied, b)
                own.count(pool.tensor_tensor(nb, mv[:, :, 0], minus[:], ALU.mult))
                own.step(pool.tensor_tensor(ve, mv[:, :, 1], ln_eps[:], ALU.add))
                own.step(pool.tensor_tensor(rs, ve, mhalf[:, 0:TT], ALU.pow))
                pool.tensor_tensor(nb, nb, rs, ALU.mult).then_inc(done, 1)

            mh4 = mhalf[:].rearrange("p (n h) -> p n h", n=TT)

            def attn_step(t, first=False, last=False, front=True, tail=True):
                if front:
                    scale_bias(var1_v, t + 1, mv1, ve1[:], rs1[:], nb1[:], xn1_a, rs1_p)
                if tail:
                    scale_bias(var2_v, t - 1, mv2, ve2[:], rs2[:], nb2[:], xn2_a, rs2_p)

            scale_bias(var1_v, 0, mv1, ve1[:], rs1[:], nb1[:], xn1_a, rs1_p)
            attn_step(0, tail=False)
            with pool.Fori(1, B - 1) as t:
                own.loop(t - 1, 6)
                attn_step(t)
            own.end(B - 2)
            attn_step(B - 1, front=False)
            attn_step(B, front=False)

            pool.wait_ge(exp_ld, 16 * len(exp_loads))
            for w, (hi, _) in zip((we_g, we_u), we_parts):
                own.count(pool.tensor_copy(hi[:], w[:]))
            own.wait()
            for w, (hi, lo) in zip((we_g, we_u), we_parts):
                pool.tensor_tensor(lo[:], w[:], hi[:].bitcast(F32), ALU.subtract).then_inc(we_p, 1)

            def mix_step(t, mid=True, tail=True):
                if tail:
                    pool.wait_ge(y_v, t - 1)
                    if not (isinstance(t, int) and t == 2):
                        pool.wait_ge(x2_v, t - 2)
                    pool.tensor_tensor(y2, y1[:], rms[:], ALU.mult).then_inc(y2_p, 1)
                    scale_bias(var3_v, t - 2, mv3, ve3[:], rs3[:], nb3[:], xn3_a, rs3_p)
                if mid:
                    root(var4_v, t - 1, v4[:], rms_eps[:], ve4[:], rs4[:], rs4_p)

            pool.wait_ge(kkv_a, 2)
            mix_step(1, tail=False)
            mix_step(2)
            with pool.Fori(3, B) as t:
                own.loop(t - 3, 4)
                mix_step(t)
            own.end(B - 3)
            mix_step(B)
            mix_step(B + 1, mid=False)

            def sum_experts(k, first):
                for e in range(1, E):
                    pool.wait_ge(yw_v, k * E + e + 1)
                    if e > 1:
                        pool.wait_ge(acc_p, k * (E - 1) + e - 1)
                    elif not first:
                        pool.wait_ge(fin_v, k)
                    pool.tensor_tensor(acc[:], acc[:] if e > 1 else yw[0][:], yw[e % 2][:], ALU.add).then_inc(acc_p, 1)

            sum_experts(0, True)
            with pool.Fori(1, NB) as k:
                sum_experts(k, False)

        @block.scalar
        def _(act):
            own = Chain(act, act_own)

            for dst, src in mask_loads:
                act.dma_start(dst[:], a[src]).then_inc(mask_ld, 16)

            def context_rows():
                act.wait_ge(krow_mm, 1)
                act.wait_ge(rows_ld, 16 * len(rows_loads))
                act.activation(krow[:], ps1[0:2 * BH, 0:T], ACT.Identity, bias=gate_bias[:]).then_inc(krow_a, 1)

            def exp_gates(b, n, first):
                act.wait_ge(gsub_v, 2 * b + n + 1)
                if not first:
                    act.wait_ge(et_mm, 2 * b + n - 1)
                act.activation(g_exp[:, n, :], g_sub[:, n, :], ACT.Exp, scale=scale).then_inc(ge_a, 1)

            def copy_xnT(b):
                act.wait_ge(xn_mm, b + 1)
                act.copy(xkT[:].rearrange("c (n t) -> c n t", n=TT), ps3[:, 0:T].rearrange("c (n t) -> c n t", n=TT)[:, :, 0:L])
                act.copy(xnT[:], ps3[:, 0:T]).then_inc(xnT_a, 1)

            def normalise(t, rs, nb, xn, ready, done):
                act.wait_ge(ready, t + 1)
                for n in range(TT):
                    ins = act.activation(xn[:, n, :], x[:, t * TT + n, :], ACT.Identity, bias=nb[:, n:n + 1], scale=rs[:, n:n + 1])
                ins.then_inc(done, 1)

            normalise(0, rs1, nb1, xn1, rs1_p, xn1_a)
            copy_xnT(0)

            def step(t, front=True, nxt=True, tail=True, q=True):
                if front:
                    act.wait_ge(kT_v, t + 1)
                    if tail:
                        act.wait_ge(at_mm, t)
                    vps = ps3[:, 2 * P:3 * P].rearrange("q (p j) -> q p j", p=HP)
                    va = vaug[:, 0:HP * TT * WV].rearrange("q (p n j) -> q p n j", p=HP, n=TT)
                    act.copy(va[0:64, :, 0, 0:2 * D], vps[0:64])
                    act.copy(va[64:128, :, 1, 0:2 * D], vps[64:128]).then_inc(v_a, 1)
                if q:
                    normalise(t - 2, rs2, nb2, xn2, rs2_p, xn2_a)
                if nxt:
                    normalise(t + 1, rs1, nb1, xn1, rs1_p, xn1_a)
                if tail:
                    act.wait_ge(wt_mm, t)
                    act.copy(wu[:].rearrange("p g t -> p (g t)"), ps4[:]).then_inc(wu_a, 1)
                if front:
                    exp_gates(t, 0, not tail)
                if q:
                    act.wait_ge(q_mm, t - 1)
                    act.copy(qT[:, toks(t - 2)], ps3[:, T:2 * T]).then_inc(qT_a, 1)
                if front:
                    act.wait_ge(ssub_v, t + 1)
                    if tail:
                        act.wait_ge(pt_mm, t)
                    act.activation(prob[:], s_sub[:], ACT.Exp, scale=scale).then_inc(p_a, 1)

                def copy_eT(n, ps):
                    act.wait_ge(et_mm, 2 * t + n + 1)
                    act.copy(eT[:, :, n * P:(n + 1) * P], ps[:].rearrange("p (h t) -> p h t", h=HP)).then_inc(eT_a, 1)

                if front:
                    if tail:
                        act.wait_ge(wt_mm, t)
                    copy_eT(0, ps0)
                if nxt:
                    act.wait_ge(g_mm, 2 * t + 2)
                    copy_xnT(t + 1)
                if front:
                    act.wait_ge(pt_mm, t + 1)
                    if tail:
                        act.wait_ge(at_mm, t)
                    act.copy(pT[:], ps1[:]).then_inc(pT_a, 1)
                if tail:
                    act.wait_ge(wn_mm, t)
                    act.copy(wnT[:], ps4[:, 0:T]).then_inc(wnT_a, 1)
                if front:
                    exp_gates(t, 1, not tail)
                    copy_eT(1, ps2)

            step(0, tail=False, q=False)
            step(1, q=False)
            with act.Fori(2, B - 1) as t:
                step(t)
            step(B - 1, nxt=False)
            step(B, front=False, nxt=False)
            context_rows()
            step(B + 1, front=False, nxt=False, tail=False)

            act.wait_ge(gr_v, 1)
            f = slice(BH, 2 * BH)
            own.step(act.activation(f_abs[f, :], gr[f, :], ACT.Abs))
            own.step(act.activation(f_exp[f, :], f_abs[f, :], ACT.Exp, scale=-1.0))
            act.activation(f_log[f, :], f_exp[f, :], ACT.Ln, bias=1.0).then_inc(flog_a, 1)
            act.wait_ge(m_v, 1)
            act.activation(em[:], m_row[:], ACT.Exp, scale=-1.0).then_inc(em_a, 1)
            act.wait_ge(rowT_v, 1)

            def copy_xT(b):
                act.wait_ge(x3_mm, b + 1)
                act.copy(xT[:, toks(b)], ps2[:, 0:T])
                act.copy(x_hi[:, toks(b)], ps2[:, 0:T]).then_inc(x3_a, 1)

            def mix_step(t, front=True, mid=True, last=True):
                def decays(h):
                    act.wait_ge(d_mm, 4 * t + h + 1)
                    if mid or h >= 2:
                        act.wait_ge(c_v, 4 * t + h - 1)
                    d = halves(ps0, h)
                    g0 = rowT[:, 0, 0, bass.ds(t * NH + h, 1)]
                    g1 = rowT[:, 0, 1, bass.ds(t * NH + h, 1)]
                    act.activation(decay[:, h % 2, 0:T], d[:, 0:T], ACT.Exp, bias=g0).then_inc(d_a, 1)
                    act.activation(decay[:, h % 2, T:T + P], d[:, T:T + P], ACT.Exp, bias=g1).then_inc(d_a, 1)

                if front:
                    decays(0)
                if last:
                    normalise(t - 3, rs3, nb3, xn3, rs3_p, xn3_a)
                if front:
                    decays(1)
                if mid:
                    act.wait_ge(pv_mm, t)
                    if not (isinstance(t, int) and t == 1):
                        act.wait_ge(ht_mm, t - 1)
                    act.copy(hs[:], ps2[:, 0:T])
                    act.copy(ss, ps2[:, 512:512 + T]).then_inc(hs_a, 1)
                if front:
                    decays(2)
                if mid:
                    act.wait_ge(ht_mm, t)
                    if not (isinstance(t, int) and t == 1):
                        act.wait_ge(var4_v, t - 1)
                    act.activation(sq[:].rearrange("p g d -> p (g d)"), ps4[:, 0:T], ACT.Square).then_inc(sq_a, 1)
                if last:
                    copy_xT(t - 3)
                if front:
                    decays(3)

            mix_step(0, mid=False, last=False)
            mix_step(1, last=False)
            mix_step(2, last=False)
            with act.Fori(3, B) as t:
                mix_step(t)

            def silu(n, par):
                act.wait_ge(gu_mm, n + 1)
                if not (isinstance(n, int) and n < 2):
                    act.wait_ge(hh_v, n - 1)
                act.activation(si[par][:], halves(ps0, par), ACT.Silu).then_inc(si_a, 1)

            mix_step(B, front=False)
            normalise(B - 2, rs3, nb3, xn3, rs3_p, xn3_a)
            silu(0, 0)
            copy_xT(B - 2)
            silu(1, 1)
            normalise(B - 1, rs3, nb3, xn3, rs3_p, xn3_a)
            silu(2, 0)
            copy_xT(B - 1)
            silu(3, 1)
            act.wait_ge(lsub_v, 1)
            act.activation(lexp[:], lsub[:], ACT.Exp).then_inc(lexp_a, 1)
            for n in range(4, NSH * NB):
                silu(n, n % 2)
            with act.Fori(0, NB) as k:
                for e in range(E):
                    silu(routed(k, e), e % 2)

        @block.vector
        def _(dve):
            own = Chain(dve, dve_own)
            tt = dve.tensor_tensor

            def stats(b, bn):
                for n in range(TT):
                    own.count(dve.bn_stats(bn[:, n, :], x[:, b * TT + n, :]))

            def moments(bn, mv, done):
                for n in range(TT):
                    ins = dve.bn_aggr(mv[:, n, :], bn[:, n, :])
                    if n < TT - 1:
                        own.count(ins)
                ins.then_inc(done, 1)

            dve.wait_ge(x0_ld, 32)
            stats(0, bn1)
            own.wait()
            moments(bn1, mv1, var1_v)
            own.step(dve.memset(lat[:], 0.0))
            for h2 in range(2):
                own.step(dve.memset(lat[64 * h2:64 * h2 + 64, :, 2 * D + h2:2 * D + h2 + 1], 1.0))
            own.step(dve.memset(vaug[:], 0.0))
            va = vaug[:, 0:HP * TT * WV].rearrange("q (p n j) -> q p n j", p=HP, n=TT)
            for n in range(TT):
                own.step(dve.memset(va[64 * n:64 * n + 64, :, n, 2 * D:WV], 1.0))
            own.step(dve.memset(zeros[:], 0.0))
            own.step(dve.memset(ones_f[:], 1.0))
            own.step(dve.memset(ones_b[:], 1.0))
            own.step(dve.memset(carry[:], 1.0))
            own.step(dve.memset(carry[:, :, 0:1], 0.0))
            own.step(dve.tensor_copy(ident_b[:], ident[:]))
            dve.wait_ge(mask_ld, 16 * len(mask_loads))
            own.step(dve.tensor_copy(latent_mask_b[:], latent_mask[:]))
            own.step(dve.tensor_copy(causal_b[:], causal[:]))
            own.step(dve.tensor_copy(before_b[:], before[:]))
            for part in range(3):
                dve.tensor_copy(pick[BH * part:BH * part + BH],
                                ident[0:BH, 0:BH].unsqueeze(2).to_broadcast([BH, BH, P])).then_inc(const_v, 1)
            dve.wait_ge(x_ld, 16)
            dve.wait_ge(attn_ld, 16 * len(attn_loads))

            def subtract_max(ps, n_groups, mx, dst, ready, count, used, used_count, done):
                dve.wait_ge(ready, count)
                if used is not None:
                    dve.wait_ge(used, used_count)
                v = ps[:].rearrange("p (g l) -> p g l", g=n_groups)
                own.step(dve.tensor_reduce(mx, v, AX_X, ALU.max))
                tt(dst.rearrange("p (g l) -> p g l", g=n_groups), v, mx.unsqueeze(2).to_broadcast([P, n_groups, L]),
                   ALU.subtract).then_inc(done, 1)

            def step(t, front=True, nxt=True, tail=True):
                first = not tail
                if nxt:
                    stats(t + 1, bn1)
                if front:
                    dve.wait_ge(kv_mm, t + 1)
                    if not first:
                        dve.wait_ge(s_mm, t)
                    own.step(tt(k1[:], ps3[:, 0:P], cos[:], ALU.mult))
                    own.step(tt(k2[:], ps3[:, P:2 * P], sin[:], ALU.mult))
                    tt(kT[:], k1[:], k2[:], ALU.add).then_inc(kT_v, 1)
                if nxt:
                    moments(bn1, mv1, var1_v)
                if front:
                    subtract_max(ps0, H, g_max[:, 0, :], g_sub[:, 0, :], g_mm, 2 * t + 1,
                                 None if first else ge_a, 2 * t - 1, gsub_v)
                    subtract_max(ps1, 16, s_max[:], s_sub[:], s_mm, t + 1, None if first else p_a, t, ssub_v)
                if tail:
                    dve.wait_ge(wtr_mm, t)
                    w = ps4[:].rearrange("p (g j) -> p g j", j=32)
                    own.step(dve.reciprocal(w_rden[:].rearrange("p (g h) -> p g h", h=2), w[:, :, 2 * D:2 * D + 2]))
                    tt(wn[:].rearrange("p n (g h d) -> p (n g) h d", h=2, d=D),
                       w[:, :, 0:2 * D].rearrange("p g (h d) -> p g h d", h=2),
                       w_rden[:].rearrange("p (g h) -> p g h", h=2).unsqueeze(3).to_broadcast([P, TT * HP, 2, D]),
                       ALU.mult).then_inc(wn_v, 1)
                if front:
                    subtract_max(ps2, H, g_max[:, 1, :], g_sub[:, 1, :], g_mm, 2 * t + 2,
                                 None if first else ge_a, 2 * t, gsub_v)
                if tail:
                    dve.wait_ge(pr_mm, t)
                    tt(x[:, tiles(t - 1), :], x[:, tiles(t - 1), :], ps4[:, 0:T].rearrange("p (n c) -> p n c", n=TT),
                       ALU.add).then_inc(x1_v, 1)
                    dve.wait_ge(x1_v, t)
                    if not front:
                        stats(t - 1, bn2)
                        own.wait()
                        moments(bn2, mv2, var2_v)
                if front:
                    dve.wait_ge(at_mm, t + 1)
                    av = ps1[:].rearrange("q (p w) -> q p w", p=HP)
                    den = av[:, :, 0:TT * WV].rearrange("q p (n j) -> q p n j", n=TT)[:, :, :, 2 * D]
                    own.step(dve.reciprocal(a_rden[:], den))
                    for h2 in range(2):
                        r = slice(64 * h2, 64 * h2 + 64)
                        for n, dst in enumerate((a_n0, a_n1)):
                            o = WV * n + D * h2
                            if h2 == 1 and n == 0:
                                own.wait()
                            own.count(tt(dst[r], av[r, :, o:o + D],
                                         a_rden[r, :, n:n + 1].to_broadcast([64, HP, D]), ALU.mult))
                            if tail and h2 == n == 0:
                                stats(t - 1, bn2)
                    if tail:
                        moments(bn2, mv2, var2_v)
                        dve.wait_ge(wt_mm, t)
                    own.step(tt(lat[0:64, :, 0:D], a_n0[0:64], a_n1[0:64], ALU.add))
                    tt(lat[64:128, :, D:2 * D], a_n0[64:128], a_n1[64:128], ALU.add).then_inc(lat_v, 1)

            step(0, tail=False)
            with dve.Fori(1, B - 1) as t:
                own.loop(t - 1, ATTN_DVE_STEPS)
                step(t)
            own.end(B - 2)
            dve.wait_ge(rows_ld, 16 * len(rows_loads))
            tt(kk[:], kk[:], kv[:], ALU.add).then_inc(kkv_a, 1)
            dve.tensor_scalar(rms[:], rms[:], 1.0, None, ALU.add).then_inc(kkv_a, 1)
            step(B - 1, nxt=False)
            step(B, front=False, nxt=False)

            f = slice(BH, 2 * BH)
            dve.wait_ge(gates_mm, 1)
            dve.wait_ge(krow_a, 1)
            tt(gr[:], ps3[0:2 * BH, 0:T], krow[:], ALU.add).then_inc(gr_v, 1)
            dve.wait_ge(gr_v, 1)
            own.step(dve.tensor_scalar(f_min[f, :], gr[f, :], 0.0, None, ALU.min))
            dve.wait_ge(flog_a, 1)
            own.step(tt(logf[:], f_min[f, :], f_log[f, :], ALU.subtract))
            own.step(dve.tensor_tensor_scan(cs[:], logf[:], zeros[:], 0.0, ALU.add, ALU.add))
            tt(gi[:], gr[0:BH, :], cs[:], ALU.subtract).then_inc(gi_v, 1)
            dve.wait_ge(gi_v, 1)
            own.step(dve.tensor_tensor_scan(top[:], gi[:], gi[:], -3.0e38, ALU.max, ALU.max))
            tt(m_row[:], cs[:], top[:], ALU.add).then_inc(m_v, 1)
            own.step(dve.tensor_scalar(neg[:], top[:], -1.0, None, ALU.mult))
            own.step(dve.tensor_copy(neg_b1[:], neg[:]))
            own.step(dve.tensor_copy(neg3[0:BH, :], neg_b1[:]))
            own.step(tt(neg_r1[:], neg[:], neg_b1[:], ALU.subtract))
            own.step(dve.tensor_copy(neg_b2[:], neg_r1[:]))
            own.step(dve.tensor_copy(neg3[BH:2 * BH, :], neg_b2[:]))
            own.step(tt(neg_r2[:], neg_r1[:], neg_b2[:], ALU.subtract))
            dve.tensor_copy(neg3[2 * BH:3 * BH, :], neg_r2[:]).then_inc(neg3_v, 1)
            dve.wait_ge(rowT_mm, 1)
            dve.tensor_copy(rowT[:].rearrange("p a n r -> p (a n r)"), ps4[:, 0:4 * BH]).then_inc(rowT_v, 1)
            dve.wait_ge(rowT_v, 1)

            def low_part(b):
                dve.wait_ge(x3_a, b + 1)
                tt(x_lo[:, toks(b)], xT[:, toks(b)], x_hi[:, toks(b)].bitcast(F32), ALU.subtract).then_inc(xlo_v, 1)

            def scale_heads(b):
                dve.wait_ge(rs4_p, b + 1)
                own.step(tt(f4[:], r4[:], rs4[:], ALU.mult))
                tt(y1[:].rearrange("p n (h d) -> p (n h) d", h=NH), ps4[:, 0:T].rearrange("p (g d) -> p g d", d=HD),
                   f4[:].rearrange("p n h -> p (n h)").unsqueeze(2).to_broadcast([P, TT * NH, HD]),
                   ALU.mult).then_inc(y_v, 1)

            def residual(b):
                dve.wait_ge(y2_p, b + 1)
                tt(x[:, tiles(b), :], x[:, tiles(b), :], y2, ALU.add).then_inc(x2_v, 1)
                dve.wait_ge(x2_v, b + 1)

            def mix_step(t, par, front=True, mid=True, tail=True, last=True):
                def weigh(h):
                    dve.wait_ge(qk_mm, 4 * t + h + 1)
                    dve.wait_ge(d_a, 2 * (4 * t + h + 1))
                    if tail and h == 0:
                        dve.wait_ge(pv_mm, t - 1)
                    dve.scalar_tensor_tensor(out=cc[par][:, h, :], in0=halves(ps1, h)[:, 0:384], scalar=qk_scale,
                                             in1=decay[:, h % 2, :], op0=ALU.mult, op1=ALU.mult).then_inc(c_v, 1)

                if front:
                    weigh(0)
                if tail:
                    scale_heads(t - 2)
                if front:
                    weigh(1)
                if tail:
                    residual(t - 2)
                if front:
                    weigh(2)
                if tail:
                    stats(t - 2, bn3)
                    own.wait()
                if mid:
                    dve.wait_ge(ht_mm, t)
                    sums = ps3[:, 0:T].rearrange("p (n h d) -> p n h d", n=TT, h=NH)[:, :, :, 0]
                    tt(n4[:], sums, rowT[:, 1, :, bass.ds((t - 1) * NH, NH)], ALU.max).then_inc(n4_v, 1)
                    if tail:
                        moments(bn3, mv3, var3_v)
                    dve.wait_ge(n4_v, t)
                    own.step(dve.tensor_scalar(n4e[:], n4[:], RMS_EPS, None, ALU.add))
                    own.step(dve.reciprocal(r4[:], n4e[:]))
                    own.count(tt(r4s[:], r4[:], r4[:], ALU.mult))
                    dve.wait_ge(sq_a, t)
                    own.step(dve.tensor_reduce(s4[:].rearrange("p n h -> p (n h)"), sq[:], AX_X, ALU.add))
                    dve.scalar_tensor_tensor(out=v4[:], in0=s4[:], scalar=1.0 / HD, in1=r4s[:],
                                             op0=ALU.mult, op1=ALU.mult).then_inc(var4_v, 1)
                if front:
                    weigh(3)
                if last:
                    low_part(t - 3)

            mix_step(0, 0, mid=False, tail=False, last=False)
            mix_step(1, 1, tail=False, last=False)
            mix_step(2, 0, last=False)
            mix_step(3, 1)
            with dve.Fori(1, B // 2 - 1) as i:
                own.loop(i - 1, 2 * MIX_DVE_STEPS)
                mix_step(2 * i + 2, 0)
                mix_step(2 * i + 3, 1)
            own.end(B // 2 - 2)

            def hidden(n, par):
                dve.wait_ge(si_a, n + 1)
                if not (isinstance(n, int) and n < 2):
                    dve.wait_ge(dn_mm, n - 1)
                tt(hh[par][:], halves(ps1, par), si[par][:], ALU.mult).then_inc(hh_v, 1)

            def add_shared(k):
                dve.wait_ge(dn_mm, NSH * (k + 1))
                dve.wait_ge(xn3_a, min(B, (k + 1) * BLK // TT))
                xb = x[:, k * BLK:(k + 1) * BLK, :]
                tt(xb, xb, ps3[:].rearrange("p (n c) -> p n c", n=BLK), ALU.add).then_inc(sx_v, 1)

            mix_step(B, 0, front=False)
            scale_heads(B - 1)
            hidden(0, 0)
            dve.wait_ge(rs3_p, B - 1)
            residual(B - 1)
            stats(B - 1, bn3)
            own.wait()
            moments(bn3, mv3, var3_v)
            hidden(1, 1)
            low_part(B - 2)
            hidden(2, 0)
            add_shared(0)
            low_part(B - 1)
            hidden(3, 1)

            dve.wait_ge(lg_mm, 1)
            lg = ps4[:, 0:NT * E].rearrange("p (n e) -> p n e", e=E)
            bc = lambda v: v.unsqueeze(2).to_broadcast([P, NT, E])
            own.step(dve.tensor_reduce(lmax[:], lg, AX_X, ALU.max))
            tt(lsub[:], lg, bc(lmax[:]), ALU.subtract).then_inc(lsub_v, 1)
            add_shared(1)
            dve.wait_ge(lexp_a, 1)
            own.step(dve.tensor_reduce(lsum[:], lexp[:], AX_X, ALU.add))
            own.step(dve.reciprocal(lrec[:], lsum[:]))
            own.count(tt(score[:], lexp[:], bc(lrec[:]), ALU.mult))
            hidden(4, 0)
            own.wait()
            for n in range(NT):
                own.count(dve.max(top8[:, n, :], score[:, n, :]))
                if n == NT // 2:
                    hidden(5, 1)
            own.wait()
            for n in range(NT):
                own.count(dve.max_index(idx8[:, n, :], top8[:, n, :], score[:, n, :]))
            add_shared(2)
            own.step(tt(wsum[:], top8[:, :, 0], top8[:, :, 1], ALU.add))
            own.count(dve.tensor_scalar(wsum[:], wsum[:], 1e-20, None, ALU.add))
            dve.wait_ge(exp_ld, 16 * len(exp_loads))
            for k in range(2):
                own.count(dve.tensor_copy(idxf[:, k, :], idx8[:, :, k]))
            hidden(6, 0)
            own.wait()
            own.count(dve.reciprocal(wrec[:], wsum[:]))
            bn_ = lambda v: v.unsqueeze(1).to_broadcast([P, E, NT])
            for k, one_hot in enumerate((oh0, oh1)):
                own.step(tt(one_hot[:], ids[:], bn_(idxf[:, k, :]), ALU.is_equal))
            tt(ohb[:], oh0[:], oh1[:], ALU.add).then_inc(ohb_v, 1)
            hidden(7, 1)
            for k in range(2):
                own.step(tt(w2[:, k, :], top8[:, :, k], wrec[:], ALU.mult))
            for k, one_hot, weight in ((0, oh0, ow0), (1, oh1, ow1)):
                own.step(tt(weight[:], one_hot[:], bn_(w2[:, k, :]), ALU.mult))
            own.step(tt(ow[:], ow0[:], ow1[:], ALU.add))
            add_shared(3)

            def places():
                dve.wait_ge(cnt_mm, 1)
                flat = lambda v: v[:].rearrange("p e n -> p (e n)")
                own.step(dve.tensor_copy(flat(tot), ps4[:, 3 * P:4 * P]))
                own.step(dve.tensor_tensor_scan(flat(pre), flat(carry), flat(tot), 0.0, ALU.mult, ALU.add))
                own.step(tt(flat(pre), flat(pre), flat(tot), ALU.subtract))
                own.step(tt(flat(pos), ps4[:, 2 * P:3 * P], flat(pre), ALU.add))
                dve.scalar_tensor_tensor(out=comb[:], in0=pos[:], scalar=float(CAP), in1=ow[:],
                                         op0=ALU.is_lt, op1=ALU.mult).then_inc(comb_v, 1)
                dve.wait_ge(sx_v, NB)
                dve.wait_ge(comb_v, 1)

            def experts(k, first):
                def weighted(e):
                    dve.wait_ge(dn_mm, routed(k, e) + 1)
                    if not first or e >= 2:
                        dve.wait_ge(acc_p, k * (E - 1) + max(e - 2, 1) if e >= 2 else k * (E - 1))
                    tt(yw[e % 2][:], halves(ps2, e).rearrange("p (n c) -> p n c", n=BLK),
                       comb[:, e, bass.ds(k * BLK, BLK)].unsqueeze(2).to_broadcast([P, BLK, C]), ALU.mult).then_inc(yw_v, 1)

                for e in range(E):
                    hidden(routed(k, e), e % 2)
                    if first and e == 0:
                        places()
                    if e:
                        weighted(e - 1)
                weighted(E - 1)
                xb = x[:, bass.ds(k * BLK, BLK), :]
                dve.wait_ge(acc_p, (k + 1) * (E - 1))
                tt(xb, xb, acc[:], ALU.add).then_inc(fin_v, 1)

            experts(0, True)
            with dve.Fori(1, NB) as k:
                experts(k, False)

        @block.tensor
        def _(pe):
            mm = pe.matmul

            def context_rows():
                pe.wait_ge(rows_ld, 16 * len(rows_loads))
                pe.wait_ge(kkv_a, 1)
                pe.wait_ge(lat_v, B)
                for b in range(B):
                    ins = mm(ps1[0:2 * BH, 0:T], kk[:, b, :], ctxT[:, b * T:(b + 1) * T], start=(b == 0), stop=(b == B - 1))
                ins.then_inc(krow_mm, 1)

            def transpose_xn(b):
                pe.wait_ge(xn1_a, b + 1)
                for n in range(TT):
                    ins = pe.transpose(ps3[:, n * P:(n + 1) * P], xn1[:, n, :], ident[:])
                ins.then_inc(xn_mm, 1)

            pe.wait_ge(x0_ld, 32)
            transpose_xn(0)
            pe.wait_ge(attn_ld, 16 * len(attn_loads))

            def step(t, front=True, nxt=True, tail=True, q=True):
                first = not tail

                def gates(n, ps):
                    if not first:
                        pe.wait_ge(eT_a, 2 * t - 1 + n)
                    for j in range(2):
                        ins = mm(ps[:, 512 * j:512 * j + 512], xnT[:, n * P:(n + 1) * P], wg[:, 512 * j:512 * j + 512],
                                 start=True, stop=True)
                    ins.then_inc(g_mm, 1)

                if front:
                    pe.wait_ge(xnT_a, t + 1)
                    mm(ps3[:, 0:P], wk[:], xkT[:], start=True, stop=True)
                    mm(ps3[:, P:2 * P], wkr[:], xkT[:], start=True, stop=True)
                    mm(ps3[:, 2 * P:3 * P], xkT[:], wv[:], start=True, stop=True).then_inc(kv_mm, 1)
                    gates(0, ps0)
                if tail:
                    pe.wait_ge(eT_a, 2 * t)
                    pe.wait_ge(lat_v, t)
                    if q:
                        pe.wait_ge(x1_v, t - 1)
                    for p in range(HP):
                        r = 32 * (p % 4)
                        ins = mm(ps4[r:r + 32, T * (p // 4):T * (p // 4) + T], lat[:, p, :], eT[:, p, :],
                                 start=True, stop=True)
                    ins.then_inc(wt_mm, 1)
                if front:
                    pe.wait_ge(kT_v, t + 1)
                    if first:
                        pe.wait_ge(const_v, 3)
                    if not first:
                        pe.wait_ge(lat_v, t)
                    for half in range(2):
                        bank = ps1[:, 512 * half:512 * half + 512]
                        mm(bank, ident_b[:], latent_mask_b[:], start=True, stop=True)
                        for j in range(4):
                            ins = mm(bank[:, P * j:P * j + P], qblk[:, 4 * half + j, :], kT[:], start=False, stop=True,
                                     skip_group_check=True)
                    ins.then_inc(s_mm, 1)
                if q:
                    pe.wait_ge(xn2_a, t - 1)
                    if front:
                        pe.wait_ge(v_a, t + 1)
                    for n in range(TT):
                        ins = pe.transpose(ps3[:, T + n * P:T + n * P + P], xn2[:, n, :], ident[:])
                    ins.then_inc(q_mm, 1)
                if front:
                    gates(1, ps2)
                if tail:
                    pe.wait_ge(wu_a, t)
                    for n in range(TT):
                        for g in range(2):
                            ins = pe.transpose(ps4[:, (2 * n + g) * P:(2 * n + g + 1) * P], wu[:, g, n * P:(n + 1) * P], ident[:])
                    ins.then_inc(wtr_mm, 1)
                if nxt:
                    if q:
                        pe.wait_ge(qT_a, t - 1)
                    else:
                        pe.wait_ge(v_a, t + 1)
                    transpose_xn(t + 1)

                def transpose_gates(n, ps):
                    pe.wait_ge(ge_a, 2 * t + n + 1)
                    for p in range(HP):
                        ins = pe.transpose(ps[:, p * P:(p + 1) * P], g_exp[:, n, p * P:(p + 1) * P], ident[:])
                    ins.then_inc(et_mm, 1)

                if front:
                    transpose_gates(0, ps0)
                    pe.wait_ge(p_a, t + 1)
                    for p in range(HP):
                        ins = pe.transpose(ps1[:, p * P:(p + 1) * P], prob[:, p * P:(p + 1) * P], ident[:])
                    ins.then_inc(pt_mm, 1)
                if tail:
                    pe.wait_ge(wn_v, t)
                    for n in range(TT):
                        ins = pe.transpose(ps4[:, n * P:(n + 1) * P], wn[:, n, :], ident[:])
                    ins.then_inc(wn_mm, 1)
                if front:
                    pe.wait_ge(pT_a, t + 1)
                    for p in range(HP):
                        w = p * TT * WV
                        ins = mm(ps1[:, p * P:(p + 1) * P], pT[:, p * P:(p + 1) * P], vaug[:, w:w + P], start=True, stop=True)
                    ins.then_inc(at_mm, 1)
                if tail:
                    pe.wait_ge(wnT_a, t)
                    for n in range(TT):
                        ins = mm(ps4[:, n * P:(n + 1) * P], wnT[:, n * P:(n + 1) * P], wp[:], start=True, stop=True)
                    ins.then_inc(pr_mm, 1)
                if front:
                    transpose_gates(1, ps2)

            step(0, tail=False, q=False)
            step(1, q=False)
            with pe.Fori(2, B - 1) as t:
                step(t)
            step(B - 1, nxt=False)
            step(B, front=False, nxt=False)
            context_rows()
            step(B + 1, front=False, nxt=False, tail=False)

            pe.wait_ge(qT_a, B)
            for b in range(B):
                ins = mm(ps3[0:2 * BH, 0:T], kq[:, b, :], qT[:, b * T:(b + 1) * T], start=(b == 0), stop=(b == B - 1))
            ins.then_inc(gates_mm, 1)
            pe.wait_ge(gi_v, 1)
            pe.wait_ge(em_a, 1)
            for i, src in enumerate((gi, em)):
                for n in range(TT):
                    o = (TT * i + n) * BH
                    ins = pe.transpose(ps4[:, o:o + BH], src[:, n * P:(n + 1) * P], ident[0:BH, 0:BH])
            ins.then_inc(rowT_mm, 1)
            pe.wait_ge(neg3_v, 1)
            pe.wait_ge(rowT_v, 1)

            def mix_step(t, par, pair, front=True, mid=True, last=True):
                def scores(h):
                    d, s = halves(ps0, h), halves(ps1, h)
                    if mid or h >= 2:
                        pe.wait_ge(d_a, 2 * (4 * t + h - 1))
                    sel = pick[:, bass.ds(t * NH + h, 1), :].rearrange("r a p -> r (a p)")
                    mm(d[:, 0:T], sel, neg3[:], start=True, stop=True)
                    mm(d[:, T:T + P], sel, neg3[:, P:T], start=False, stop=True, skip_group_check=True)
                    mm(d[:, 0:P], ident_b[:], causal_b[:], start=False, stop=True, skip_group_check=True)
                    mm(d[:, T:T + P], ident_b[:], causal_b[:], start=False, stop=True, skip_group_check=True).then_inc(d_mm, 1)
                    if mid or h >= 2:
                        pe.wait_ge(c_v, 4 * t + h - 1)
                    mm(s[:, 0:T], kTm[par][:, h, 0:P], qT[:, toks(t)], start=True, stop=True)
                    mm(s[:, T:T + P], kTm[par][:, h, P:T], qT[:, bass.ds(t * T + P, P)], start=False, stop=True,
                       skip_group_check=True).then_inc(qk_mm, 1)

                if front:
                    pe.wait_ge(key_ld[par], 16 * NH * (pair + 1))
                    scores(0)
                    scores(1)
                if mid:
                    pe.wait_ge(c_v, 4 * t)
                    pe.wait_ge(val_ld[1 - par], 16 * (pair + par))
                    if not (isinstance(t, int) and t == 1):
                        pe.wait_ge(hs_a, t - 1)
                    if not (isinstance(t, int) and t < 4):
                        pe.wait_ge(x3_a, t - 3)
                    o = 1 - par
                    for src, col in ((None, 0), (ones_f, 512)):
                        for n in range(TT):
                            for h in range(NH):
                                rows = slice(HD * h, HD * h + HD)
                                w = ones_f[:] if src is not None else vv[o][:, n, rows]
                                c0 = col + n * P
                                m_ = cc[o][:, h, 0:T] if n == 0 else cc[o][:, h, T:T + P]
                                ins = mm(ps2[rows, c0:col + T], w, m_, start=(n == 0), stop=True, skip_group_check=True)
                    ins.then_inc(pv_mm, 1)
                if front:
                    scores(2)
                if mid:
                    pe.wait_ge(hs_a, t)
                    if not (isinstance(t, int) and t == 1):
                        pe.wait_ge(y_v, t - 1)
                        pe.wait_ge(n4_v, t - 1)
                    for src, ps in ((hs[:], ps4), (ss, ps3)):
                        for n in range(TT):
                            ins = pe.transpose(ps[:, n * P:(n + 1) * P], src[:, n * P:(n + 1) * P], ident[:])
                    ins.then_inc(ht_mm, 1)
                if last:
                    transpose_xn3(t - 3)
                if front:
                    scores(3)

            def transpose_xn3(b):
                pe.wait_ge(xn3_a, b + 1)
                for n in range(TT):
                    ins = pe.transpose(ps2[:, n * P:(n + 1) * P], xn3[:, n, :], ident[:])
                ins.then_inc(x3_mm, 1)

            mix_step(0, 0, 0, mid=False, last=False)
            mix_step(1, 1, 0, last=False)
            mix_step(2, 0, 1, last=False)
            mix_step(3, 1, 1)
            with pe.Fori(1, B // 2 - 1) as i:
                mix_step(2 * i + 2, 0, i + 1)
                mix_step(2 * i + 3, 1, i + 1)

            def up(n, e, k):
                par = e % 2
                if not (isinstance(n, int) and n < 2):
                    pe.wait_ge(si_a, n - 1)
                    pe.wait_ge(hh_v, n - 1)
                xh, xl = (v[:, bass.ds(k * BLK * P, BLK * P)] for v in (x_hi, x_lo))
                for ps, (hi, lo) in zip((ps0, ps1), we_parts):
                    for i, (w, cols) in enumerate(((hi, xh), (hi, xl), (lo, xh))):
                        ins = mm(halves(ps, par), w[:, e, :], cols, start=(i == 0), stop=(i == 2))
                ins.then_inc(gu_mm, 1)

            def down(n, e, ps, add=False):
                pe.wait_ge(hh_v, n + 1)
                for m in range(BLK):
                    ins = mm(ps[:, m * P:(m + 1) * P], hh[e % 2][:, m * P:(m + 1) * P], we_d[:, e, :],
                             start=(m == 0 and not add), stop=True, skip_group_check=True)
                ins.then_inc(dn_mm, 1)

            def shared_up(k):
                pe.wait_ge(xlo_v, (k + 1) * BLK // TT)
                for j in range(NSH):
                    up(NSH * k + j, E + j, k)

            def shared_down(k):
                if k:
                    pe.wait_ge(sx_v, k)
                for j in range(NSH):
                    down(NSH * k + j, E + j, ps3[:], add=j > 0)

            pe.wait_ge(exp_ld, 16 * len(exp_loads))
            mix_step(B, 0, B // 2, front=False)
            pe.wait_ge(we_p, 2)
            pe.wait_ge(d_a, 2 * NH * B)
            shared_up(0)
            pe.wait_ge(x3_a, B - 2)
            transpose_xn3(B - 2)
            shared_up(1)
            pe.wait_ge(x3_a, B - 1)
            transpose_xn3(B - 1)
            pe.wait_ge(n4_v, B)
            shared_down(0)
            pe.wait_ge(x3_a, B)
            pe.wait_ge(y_v, B)
            for n in range(NT):
                ins = mm(ps4[:, n * E:n * E + 96], xT[:, n * P:(n + 1) * P], gate_w[:], start=True, stop=True)
            ins.then_inc(lg_mm, 1)
            shared_down(1)
            for k in range(2, NB):
                shared_up(k)
                shared_down(k)

            def count_before():
                pe.wait_ge(ohb_v, 1)
                ohf = ohb[:].rearrange("p e n -> p (e n)")
                mm(ps4[:, 2 * P:3 * P], before_b[:], ohf, start=True, stop=True)
                mm(ps4[:, 3 * P:4 * P], ones_b[:], ohf, start=True, stop=True).then_inc(cnt_mm, 1)

            def experts(k, first):
                def routed_down(e):
                    if not first or e >= 2:
                        pe.wait_ge(yw_v, k * E + e - 1)
                    down(routed(k, e), e, halves(ps2, e))

                for e in range(E):
                    up(routed(k, e), e, k)
                    if first and e == 1:
                        count_before()
                    if e:
                        routed_down(e - 1)
                routed_down(E - 1)

            experts(0, True)
            with pe.Fori(1, NB) as k:
                experts(k, False)


def kernel(x, ctx_1024, L0_attn_latent_queries, L0_attn_W_k, L0_attn_W_v, L0_attn_W_g, L0_attn_W_p,
           L0_xattn_igate_kernel, L0_xattn_igate_bias, L0_xattn_fgate_kernel, L0_xattn_fgate_bias,
           L0_xattn_rms_scale, L0_ffn_gate_w, L0_ffn_we_gate, L0_ffn_we_up, L0_ffn_we_down,
           L0_ffn_ws_gate, L0_ffn_ws_up, L0_ffn_ws_down):
    import concourse.bacc as bacc
    from concourse.bass_utils import run_bass_kernel_spmd

    con = np.ascontiguousarray
    latents = np.asarray(L0_attn_latent_queries)[0]
    qblk = np.zeros((H, D, HP, 2, L), np.float32)
    for h in range(H):
        qblk[h, :, h // 2, h % 2, :] = latents[:, h, :].T
    wkT = np.asarray(L0_attn_W_k).T
    swap = np.arange(C) ^ 1
    ik, fk = np.asarray(L0_xattn_igate_kernel), np.asarray(L0_xattn_fgate_kernel)

    def gate_kernel(part):
        g = np.zeros((C, B, 2, B, NH), np.float32)
        for b in range(B):
            g[:, b, 0, b, :] = ik[part * C:(part + 1) * C]
            g[:, b, 1, b, :] = fk[part * C:(part + 1) * C]
        return g.reshape(C, B, 2 * BH)

    gate_w = np.zeros((C, 96), np.float32)
    gate_w[:, 0:E] = np.asarray(L0_ffn_gate_w).T

    def experts(routed, shared, down):
        r, s = np.asarray(routed), np.asarray(shared)
        s = s.reshape(C, NSH, I).transpose(1, 0, 2) if down else s.reshape(NSH, I, C)
        return con(np.concatenate([r, s]).transpose(2, 0, 1))

    arrays = {
        "x": con(x), "ctx": con(ctx_1024), "ctxT": con(np.asarray(ctx_1024).reshape(B * T, C).T),
        "wkT": con(wkT), "wkrT": con(wkT[:, swap]), "wvT": con(np.asarray(L0_attn_W_v).T),
        "wgT": con(np.asarray(L0_attn_W_g).T), "wpT": con(np.asarray(L0_attn_W_p).T),
        "qblk": qblk.reshape(C, HP, P),
        "kq": gate_kernel(0), "kk": gate_kernel(1), "kv": gate_kernel(2),
        "gate_bias": con(np.concatenate([np.tile(L0_xattn_igate_bias, B), np.tile(L0_xattn_fgate_bias, B)])[:, None]),
        "rms": con(np.broadcast_to(np.tile(L0_xattn_rms_scale, NH), (P, TT, C))),
        "gate_w": gate_w,
        "we_g": experts(L0_ffn_we_gate, L0_ffn_ws_gate, False),
        "we_u": experts(L0_ffn_we_up, L0_ffn_ws_up, False),
        "we_d": experts(L0_ffn_we_down, L0_ffn_ws_down, True),
        **constants(),
    }
    nc = bacc.Bacc("TRN2", target_bir_lowering=False, num_devices=1)
    ins = {n: nc.dram_tensor(f"in_{n}", v.shape, mybir.dt.from_np(v.dtype), kind="ExternalInput").ap() for n, v in arrays.items()}
    out = nc.dram_tensor("out", (B, T, C), F32, kind="ExternalOutput").ap()
    decoder_layer(nc, ins, out)
    r = run_bass_kernel_spmd(nc, [{f"in_{n}": v for n, v in arrays.items()}], core_ids=[0])
    return r.results[0]["out"]
```

```python
from contextlib import ExitStack

import numpy as np

import concourse.bass as bass
from concourse import mybir

ALU = mybir.AluOpType
ACT = mybir.ActivationFunctionType
AX_X = mybir.AxisListType.X
F32 = mybir.dt.float32
BF16 = mybir.dt.bfloat16
U32 = mybir.dt.uint32
F32R = mybir.dt.float32r

B, T, C = 8, 256, 128
P = 128
TT = T // P
NT = B * TT
H, L, D = 16, 64, 8
HP = H // 2
NH, HD = 4, 32
BH = B * NH
E, I = 8, 128
NSH = 2
CAP = 640
BLK = 4
NB = NT // BLK
WV = 2 * D + 1
VCOLS = (HP - 1) * TT * WV + P
LN_EPS = 1e-5
RMS_EPS = 1e-6
ATTN_DVE_STEPS = 17
MIX_DVE_STEPS = 8
NEG = -1.0e30

def constants():
    pos = np.concatenate([np.arange(L) + n * P for n in range(TT)]).astype(np.float32)
    inv = (np.float32(1.0) / np.float32(10000.0) ** (np.arange(0, D, 2, dtype=np.float32) / np.float32(D))).astype(np.float32)
    ang = pos[None, :] * inv[(np.arange(C) % D) // 2][:, None]
    sign = np.where(np.arange(C) % 2 == 0, -1.0, 1.0).astype(np.float32)[:, None]
    latent = np.where(np.arange(L)[None, :] <= (np.arange(P) % L)[:, None], 0.0, NEG)
    i = np.arange(P)
    return {
        "ident": np.eye(P, dtype=np.float32),
        "rope_cos": np.cos(ang).astype(np.float32),
        "rope_sin": (np.sin(ang) * sign).astype(np.float32),
        "latent_mask": np.tile(latent, (1, 8)).astype(np.float32),
        "causal_mask": np.where(i[:, None] <= i[None, :], 0.0, NEG).astype(np.float32),
        "before": (i[:, None] < i[None, :]).astype(np.float32),
        "expert_ids": np.tile(np.repeat(np.arange(E), NT)[None, :], (P, 1)).astype(np.float32),
    }


class Chain:

    def __init__(self, eng, sem):
        self.eng, self.sem, self.total, self.base, self.k = eng, sem, 0, 0, 0

    def loop(self, t, per):
        self.total += self.k
        self.base, self.per, self.k = self.total + t * per, per, 0

    def end(self, n):
        assert self.k == self.per, f"steps in the loop: {self.k}"
        self.total += n * self.per
        self.base, self.k = self.total, 0

    def count(self, ins):
        self.k += 1
        ins.then_inc(self.sem, 1)

    def wait(self):
        self.eng.wait_ge(self.sem, self.base + self.k)

    def step(self, ins):
        self.count(ins)
        self.wait()


def decoder_layer(nc, a, out):
    scale = 1.0 / float(np.sqrt(D))
    qk_scale = 1.0 / float(np.sqrt(HD))
    with ExitStack() as ctx:
        def sb(name, shape, dt=F32):
            return ctx.enter_context(nc.sbuf_tensor(name, shape, dt))

        def pb(name, shape):
            return ctx.enter_context(nc.psum_tensor(name, shape, F32))

        def sem(name):
            return ctx.enter_context(nc.semaphore(name))

        x = sb("x_res", [P, NT, C])
        qT = sb("qT", [C, B * T])
        xT = sb("xT", [C, B * T])
        ctxT = sb("ctxT_s", [C, B * T])
        wk, wkr, wv, wp = (sb(n, [C, C]) for n in ("wk", "wkr", "wv", "wp"))
        wg = sb("wg", [C, H * L])
        qblk = sb("qblk_s", [C, HP, P])
        we_g, we_u, we_d = (sb(n, [P, E + NSH, P]) for n in ("we_g_s", "we_u_s", "we_d_s"))
        we_parts = [[sb(f"we_{w}_{p}", [P, E + NSH, P], F32R) for p in ("hi", "lo")] for w in ("g", "u")]
        x_hi, x_lo = sb("x_hi", [C, B * T], F32R), sb("x_lo", [C, B * T], F32R)
        gate_w = sb("gate_w_s", [C, 96])
        kq, kk, kv = (sb(n, [C, B, 2 * BH]) for n in ("kq_s", "kk_s", "kv_s"))
        gate_bias = sb("gate_bias_s", [2 * BH, 1])
        rms = sb("rms_s", [P, TT, C])
        ident, ident_b = sb("ident_s", [P, P]), sb("ident_b", [P, P], BF16)
        cos, sin = sb("cos", [C, P]), sb("sin", [C, P])
        latent_mask, latent_mask_b = sb("latent_mask_s", [P, 512]), sb("latent_mask_b", [P, 512], BF16)
        causal, causal_b = sb("causal_s", [P, P]), sb("causal_b", [P, P], BF16)
        before, before_b = sb("before_s", [P, P]), sb("before_b", [P, P], BF16)
        ones_b, ones_f = sb("ones_b", [P, P], BF16), sb("ones_f", [P, HD])
        pick = sb("pick", [3 * BH, BH], BF16)
        ids = sb("ids", [P, E, NT])
        minus = sb("minus", [P, TT])
        mhalf, ln_eps, rms_eps = sb("mhalf", [P, TT * NH]), sb("ln_eps", [P, TT]), sb("rms_eps", [P, TT, NH])
        bn1, bn2, bn3 = (sb(f"bn{i}", [P, TT, 6]) for i in (1, 2, 3))
        mv1, mv2, mv3 = (sb(f"mv{i}", [P, TT, 2]) for i in (1, 2, 3))
        ve1, ve2, ve3 = (sb(f"ve{i}", [P, TT]) for i in (1, 2, 3))
        rs1, rs2, rs3 = (sb(f"rs{i}", [P, TT]) for i in (1, 2, 3))
        nb1, nb2, nb3 = (sb(f"nb{i}", [P, TT]) for i in (1, 2, 3))
        xn1, xn2, xn3 = (sb(f"xn{i}", [P, TT, C]) for i in (1, 2, 3))
        xnT, xkT = sb("xnT", [C, T]), sb("xkT", [C, P])
        xn_hi, xn_lo = sb("xn_hi", [C, T], F32R), sb("xn_lo", [C, T], F32R)
        wg_hi, wg_lo = sb("wg_hi", [C, H * L], F32R), sb("wg_lo", [C, H * L], F32R)
        k1, k2, kT = sb("k1", [C, P]), sb("k2", [C, P]), sb("kT", [C, P])
        vaug = sb("vaug", [P, VCOLS])
        s_max, s_work = sb("s_max", [P, 16]), sb("s_work", [P, 3, 1024])
        s_sub, prob, pT = (s_work[:, i, :] for i in range(3))
        g_max, g_sub, g_exp = sb("g_max", [P, TT, H]), sb("g_sub", [P, TT, 1024]), sb("g_exp", [P, TT, 1024])
        eT = sb("eT", [P, HP, T])
        a_rden, a_n0, a_n1 = sb("a_rden", [P, HP, TT]), sb("a_n0", [P, HP, D]), sb("a_n1", [P, HP, D])
        lat = sb("lat", [P, HP, 32])
        wu, wnT = sb("wu", [P, 2, T]), sb("wnT", [C, T])
        w_rden, wn = sb("w_rden", [P, NH * HP]), sb("wn", [P, TT, C])
        gr = [sb(f"gr{i}", [2 * BH, T]) for i in range(2)]
        f_abs, f_exp, f_log, f_min = (wg[0:2 * BH, i * T:(i + 1) * T] for i in range(4))
        logf, cs, zeros, gi, top, m_row, em = (sb(n, [BH, T]) for n in ("logf", "cs", "zeros_r", "gi", "top", "m_row", "em"))
        neg, neg_r1, neg_r2 = (sb(n, [BH, T]) for n in ("neg", "neg_r1", "neg_r2"))
        neg_b1, neg_b2 = sb("neg_b1", [BH, T], BF16), sb("neg_b2", [BH, T], BF16)
        neg3 = [sb(f"neg3_{i}", [3 * BH, T], BF16) for i in range(2)]
        rowT = [sb(f"rowT{i}", [P, 2, TT, BH]) for i in range(2)]
        kTm = [sb(f"kTm{i}", [C, NH, T]) for i in range(2)]
        vv = [sb(f"vv{i}", [P, TT, C]) for i in range(2)]
        decay = sb("decay", [P, 2, 384])
        cc = [v.rearrange(r, h=NH) for v, r in (
            (eT[:].rearrange("p g t -> p (g t)")[:, 0:NH * 384], "p (h t) -> p h t"),
            (s_work[:].rearrange("p a t -> p (a t)")[:, 0:NH * 384], "p (h t) -> p h t"))]
        hs, ss, sq = wnT, wu[:, 1, :], latent_mask[:, 0:T].rearrange("p (g d) -> p g d", d=HD)
        n4, n4e, r4, s4, r4s, v4, ve4, rs4, f4 = (sb(n, [P, TT, NH]) for n in ("n4", "n4e", "r4", "s4", "r4s", "v4", "ve4", "rs4", "f4"))
        y1, y2 = wn, wu[:, 0, :].rearrange("p (n c) -> p n c", n=TT)
        lsub, lexp, score = (ctxT[:, i * P:(i + 1) * P].rearrange("p (n e) -> p n e", n=NT) for i in range(3))
        oh0, oh1, tot, pre, pos, ow0, ow1, ow, comb = (
            ctxT[:, i * P:(i + 1) * P].rearrange("p (e n) -> p e n", e=E) for i in range(3, 12))
        lmax, lsum, lrec = sb("lmax", [P, NT]), sb("lsum", [P, NT]), sb("lrec", [P, NT])
        top8, idx8, idxf = sb("top8", [P, NT, 8]), sb("idx8", [P, NT, 8], U32), sb("idxf", [P, 2, NT])
        wsum, wrec, w2 = sb("wsum", [P, NT]), sb("wrec", [P, NT]), sb("w2", [P, 2, NT])
        ohb, carry = sb("ohb", [P, E, NT], BF16), sb("carry", [P, E, NT])
        si = [g_sub[:, 0, BLK * P * i:BLK * P * (i + 1)] for i in range(2)]
        hh = [g_sub[:, 1, BLK * P * i:BLK * P * (i + 1)] for i in range(2)]
        yw = [g_exp[:, 0, BLK * P * i:BLK * P * (i + 1)].rearrange("p (n c) -> p n c", n=BLK) for i in range(2)]
        acc = g_exp[:, 1, 0:BLK * P].rearrange("p (n c) -> p n c", n=BLK)

        ps0, ps1, ps2 = pb("ps0", [P, 1024]), pb("ps1", [P, 1024]), pb("ps2", [P, 1024])
        ps3, ps4 = pb("ps3", [P, 512]), pb("ps4", [P, 512])

        x0_ld, x_ld, attn_ld, mask_ld, rows_ld, exp_ld = (sem(n) for n in ("x0_ld", "x_ld", "attn_ld", "mask_ld", "rows_ld", "exp_ld"))
        key_ld, val_ld = [sem(f"key_ld{i}") for i in range(2)], [sem(f"val_ld{i}") for i in range(2)]
        out_st = sem("out_st")
        const_v, const_p = sem("const_v"), sem("const_p")
        we_p, xlo_v = sem("we_p"), sem("xlo_v")
        wg_ld, wghi_a, wglo_v, xnlo_p = sem("wg_ld"), sem("wghi_a"), sem("wglo_v"), sem("xnlo_p")
        dve_own, act_own, pool_own = sem("dve_own"), sem("act_own"), sem("pool_own")
        kv_mm, g_mm, s_mm, pt_mm, at_mm, et_mm = (sem(n) for n in ("kv_mm", "g_mm", "s_mm", "pt_mm", "at_mm", "et_mm"))
        wt_mm, wtr_mm, wn_mm, pr_mm, xn_mm, q_mm = (sem(n) for n in ("wt_mm", "wtr_mm", "wn_mm", "pr_mm", "xn_mm", "q_mm"))
        ge_a, p_a, wu_a, wnT_a, xnT_a, pT_a, eT_a, qT_a = (sem(n) for n in ("ge_a", "p_a", "wu_a", "wnT_a", "xnT_a", "pT_a", "eT_a", "qT_a"))
        var1_v, var2_v, var3_v = sem("var1_v"), sem("var2_v"), sem("var3_v")
        rs1_p, rs2_p, rs3_p = sem("rs1_p"), sem("rs2_p"), sem("rs3_p")
        xn1_a, xn2_a, xn3_a = sem("xn1_a"), sem("xn2_a"), sem("xn3_a")
        kT_v, v_a, gsub_v, ssub_v, at_v, lat_v, wn_v, x1_v = (sem(n) for n in ("kT_v", "v_a", "gsub_v", "ssub_v", "at_v", "lat_v", "wn_v", "x1_v"))
        kkv_v, gates_mm, gr_a, gr_v, flog_a, m_v, em_a, gi_v, neg3_v, rowT_mm, rowT_v = (
            sem(n) for n in ("kkv_v", "gates_mm", "gr_a", "gr_v", "flog_a", "m_v", "em_a", "gi_v", "neg3_v", "rowT_mm", "rowT_v"))
        d_mm, qk_mm, d_a, c_v, pv_mm, hs_a, ht_mm = (sem(n) for n in ("d_mm", "qk_mm", "d_a", "c_v", "pv_mm", "hs_a", "ht_mm"))
        sq_a, n4_v, var4_v, rs4_p, y_v, y2_p, x2_v, x3_mm, x3_a = (
            sem(n) for n in ("sq_a", "n4_v", "var4_v", "rs4_p", "y_v", "y2_p", "x2_v", "x3_mm", "x3_a"))
        lg_mm, lsub_v, lexp_a, ohb_v, cnt_mm, comb_v = (sem(n) for n in ("lg_mm", "lsub_v", "lexp_a", "ohb_v", "cnt_mm", "comb_v"))
        gu_mm, si_a, hh_v, dn_mm, sx_v, yw_v, acc_p, fin_v = (
            sem(n) for n in ("gu_mm", "si_a", "hh_v", "dn_mm", "sx_v", "yw_v", "acc_p", "fin_v"))

        block = ctx.enter_context(nc.Block())

        x_dram = a["x"].rearrange("b (n p) d -> p (b n) d", p=P)
        ctx_dram = a["ctx"].rearrange("b (n p) d -> b p n d", p=P)
        out_dram = out.rearrange("b (n p) d -> p (b n) d", p=P)
        attn_loads = ((wk, "wkT"), (wkr, "wkrT"), (wv, "wvT"), (cos, "rope_cos"), (sin, "rope_sin"), (qblk, "qblk"), (wp, "wpT"))
        mask_loads = ((latent_mask, "latent_mask"), (causal, "causal_mask"), (before, "before"))
        rows_loads = ((ctxT, "ctxT"), (kq, "kq"), (kk, "kk"), (kv, "kv"), (gate_bias, "gate_bias"), (rms, "rms"))
        exp_loads = ((gate_w, "gate_w"), (ids, "expert_ids"), (we_g, "we_g"), (we_u, "we_u"), (we_d, "we_d"))
        tiles = lambda b: bass.ds(b * TT, TT)
        toks = lambda b: bass.ds(b * T, T)
        routed = lambda k, e: NSH * NB + k * E + e
        rows_of = lambda t: int(not isinstance(t, int) or t >= B // 2)
        halves = lambda ps, j: ps[:, 512 * (j % 2):512 * (j % 2) + 512]

        @block.sync
        def _(sp):
            sp.dma_start(x[:, 0:TT, :], x_dram[:, 0:TT, :]).then_inc(x0_ld, 16)
            sp.dma_start(ident[:], a["ident"]).then_inc(x0_ld, 16)
            sp.dma_start(wg[:], a["wgT"]).then_inc(wg_ld, 16)
            for dst, src in attn_loads:
                sp.dma_start(dst[:], a[src]).then_inc(attn_ld, 16)
            sp.dma_start(x[:, TT:NT, :], x_dram[:, TT:NT, :]).then_inc(x_ld, 16)
            for dst, src in rows_loads:
                sp.dma_start(dst[:], a[src]).then_inc(rows_ld, 16)
            for dst, src in exp_loads:
                sp.dma_start(dst[:], a[src]).then_inc(exp_ld, 16)

            def load_keys(b, par):
                for h in range(NH):
                    rows = slice(HD * h, HD * h + HD)
                    sp.dma_start(kTm[par][rows, h, :], a["ctxT"][rows, toks(b)]).then_inc(key_ld[par], 16)

            def load_values(b, par):
                sp.dma_start(vv[par][:], ctx_dram[b]).then_inc(val_ld[par], 16)

            sp.wait_ge(const_p, 2)
            for par in range(2):
                load_keys(par, par)
                load_values(par, par)
            with sp.Fori(0, B // 2 - 1) as i:
                for par in range(2):
                    sp.wait_ge(qk_mm, NH * (2 * i + par + 1))
                    load_keys(2 * i + par + 2, par)
                    sp.wait_ge(pv_mm, 2 * i + par + 1)
                    load_values(2 * i + par + 2, par)
            with sp.Fori(0, NB) as k:
                sp.wait_ge(fin_v, k + 1)
                sp.dma_start(out_dram[:, bass.ds(k * BLK, BLK), :], x[:, bass.ds(k * BLK, BLK), :]).then_inc(out_st, 16)
            sp.wait_ge(out_st, 16 * NB)

        @block.gpsimd
        def _(pool):
            own = Chain(pool, pool_own)
            own.step(pool.memset(mhalf[:], -0.5))
            own.step(pool.memset(minus[:], -1.0))
            own.step(pool.memset(ln_eps[:], LN_EPS))
            own.step(pool.memset(rms_eps[:], RMS_EPS))
            pool.memset(kTm[0][:], 0.0).then_inc(const_p, 1)
            pool.memset(kTm[1][:], 0.0).then_inc(const_p, 1)

            def root(var_ready, b, var, eps, ve, rs, done):
                pool.wait_ge(var_ready, b + 1)
                own.step(pool.tensor_tensor(ve, var, eps, ALU.add))
                pool.tensor_tensor(rs, ve, mh4, ALU.pow).then_inc(done, 1)

            def scale_bias(var_ready, b, mv, ve, rs, nb, applied, done):
                pool.wait_ge(var_ready, b + 1)
                if isinstance(b, int) and b > 0:
                    pool.wait_ge(applied, b)
                own.count(pool.tensor_tensor(nb, mv[:, :, 0], minus[:], ALU.mult))
                own.step(pool.tensor_tensor(ve, mv[:, :, 1], ln_eps[:], ALU.add))
                own.step(pool.tensor_tensor(rs, ve, mhalf[:, 0:TT], ALU.pow))
                pool.tensor_tensor(nb, nb, rs, ALU.mult).then_inc(done, 1)

            mh4 = mhalf[:].rearrange("p (n h) -> p n h", n=TT)

            def low_part(b):
                pool.wait_ge(xnT_a, b + 1)
                pool.tensor_tensor(xn_lo[:], xnT[:], xn_hi[:].bitcast(F32), ALU.subtract).then_inc(xnlo_p, 1)

            def attn_step(t, front=True, nxt=True, tail=True):
                if front:
                    low_part(t + 1)
                if nxt:
                    scale_bias(var1_v, t + 2, mv1, ve1[:], rs1[:], nb1[:], xn1_a, rs1_p)
                if tail:
                    scale_bias(var2_v, t - 1, mv2, ve2[:], rs2[:], nb2[:], xn2_a, rs2_p)

            scale_bias(var1_v, 0, mv1, ve1[:], rs1[:], nb1[:], xn1_a, rs1_p)
            low_part(0)
            scale_bias(var1_v, 1, mv1, ve1[:], rs1[:], nb1[:], xn1_a, rs1_p)
            attn_step(0, tail=False)
            with pool.Fori(1, B - 4) as t:
                own.loop(t - 1, 6)
                attn_step(t)
            own.end(B - 5)
            pool.wait_ge(exp_ld, 16 * len(exp_loads))
            for i, (w, (hi, _)) in enumerate(zip((we_g, we_u), we_parts)):
                attn_step(B - 4 + i)
                own.count(pool.tensor_copy(hi[:], w[:]))
            for i, (w, (hi, lo)) in enumerate(zip((we_g, we_u), we_parts)):
                attn_step(B - 2 + i, front=i == 0, nxt=False)
                pool.tensor_tensor(lo[:], w[:], hi[:].bitcast(F32), ALU.subtract).then_inc(we_p, 1)
            attn_step(B, front=False, nxt=False)

            def mix_step(t, mid=True, tail=True):
                if tail:
                    pool.wait_ge(y_v, t - 1)
                    if not (isinstance(t, int) and t == 2):
                        pool.wait_ge(x2_v, t - 2)
                    pool.tensor_tensor(y2, y1[:], rms[:], ALU.mult).then_inc(y2_p, 1)
                    scale_bias(var3_v, t - 2, mv3, ve3[:], rs3[:], nb3[:], xn3_a, rs3_p)
                if mid:
                    root(var4_v, t - 1, v4[:], rms_eps[:], ve4[:], rs4[:], rs4_p)

            pool.wait_ge(kkv_v, 2)
            mix_step(1, tail=False)
            mix_step(2)
            with pool.Fori(3, B) as t:
                own.loop(t - 3, 4)
                mix_step(t)
            own.end(B - 3)
            mix_step(B)
            mix_step(B + 1, mid=False)

            def sum_experts(k, first, experts=E):
                for e in range(1, experts):
                    pool.wait_ge(yw_v, k * E + e + 1)
                    if e > 1:
                        pool.wait_ge(acc_p, k * (E - 1) + e - 1)
                    elif not first:
                        pool.wait_ge(fin_v, k)
                    pool.tensor_tensor(acc[:], acc[:] if e > 1 else yw[0][:], yw[e % 2][:], ALU.add).then_inc(acc_p, 1)

            sum_experts(0, True)
            with pool.Fori(1, NB - 1) as k:
                sum_experts(k, False)
            sum_experts(NB - 1, False, E - 1)

        @block.scalar
        def _(act):
            own = Chain(act, act_own)

            for dst, src in mask_loads:
                act.dma_start(dst[:], a[src]).then_inc(mask_ld, 16)

            def log_forget(i):
                f = slice(BH, 2 * BH)
                if i == 0:
                    act.wait_ge(gates_mm, 1)
                    act.wait_ge(rows_ld, 16 * len(rows_loads))
                    act.activation(gr[0][:], ps3[0:2 * BH, 0:T], ACT.Identity, bias=gate_bias[:]).then_inc(gr_a, 1)
                    act.wait_ge(gr_a, 1)
                else:
                    act.wait_ge(gr_v, 1)
                own.step(act.activation(f_abs[f, :], gr[i][f, :], ACT.Abs))
                own.step(act.activation(f_exp[f, :], f_abs[f, :], ACT.Exp, scale=-1.0))
                act.activation(f_log[f, :], f_exp[f, :], ACT.Ln, bias=1.0).then_inc(flog_a, 1)

            def exp_m(i):
                act.wait_ge(m_v, i + 1)
                if i:
                    act.wait_ge(rowT_mm, i)
                act.activation(em[:], m_row[:], ACT.Exp, scale=-1.0).then_inc(em_a, 1)

            def exp_gates(b, n, first):
                act.wait_ge(gsub_v, 2 * b + n + 1)
                if not first:
                    act.wait_ge(et_mm, 2 * b + n - 1)
                act.activation(g_exp[:, n, :], g_sub[:, n, :], ACT.Exp, scale=scale).then_inc(ge_a, 1)

            def copy_xnT(b):
                act.wait_ge(xn_mm, b + 1)
                act.copy(xkT[:].rearrange("c (n t) -> c n t", n=TT), ps3[:, 0:T].rearrange("c (n t) -> c n t", n=TT)[:, :, 0:L])
                act.copy(xn_hi[:], ps3[:, 0:T])
                act.copy(xnT[:], ps3[:, 0:T]).then_inc(xnT_a, 1)

            def normalise(t, rs, nb, xn, ready, done):
                act.wait_ge(ready, t + 1)
                for n in range(TT):
                    ins = act.activation(xn[:, n, :], x[:, t * TT + n, :], ACT.Identity, bias=nb[:, n:n + 1], scale=rs[:, n:n + 1])
                ins.then_inc(done, 1)

            normalise(0, rs1, nb1, xn1, rs1_p, xn1_a)
            copy_xnT(0)
            act.wait_ge(wg_ld, 16)
            act.copy(wg_hi[:], wg[:]).then_inc(wghi_a, 1)

            def copy_qT(b):
                act.wait_ge(q_mm, b + 1)
                act.copy(qT[:, toks(b)], ps3[:, T:2 * T]).then_inc(qT_a, 1)

            def step(t, front=True, nxt=True, tail=True, q=True, between=None):
                if front:
                    act.wait_ge(kT_v, t + 1)
                    if tail:
                        act.wait_ge(at_mm, t)
                    vps = ps3[:, 2 * P:3 * P].rearrange("q (p j) -> q p j", p=HP)
                    va = vaug[:, 0:HP * TT * WV].rearrange("q (p n j) -> q p n j", p=HP, n=TT)
                    act.copy(va[0:64, :, 0, 0:2 * D], vps[0:64])
                    act.copy(va[64:128, :, 1, 0:2 * D], vps[64:128]).then_inc(v_a, 1)
                if q:
                    normalise(t - 2, rs2, nb2, xn2, rs2_p, xn2_a)
                if nxt:
                    normalise(t + 1, rs1, nb1, xn1, rs1_p, xn1_a)
                if front and not tail:
                    exp_gates(t, 0, True)
                if front:
                    act.wait_ge(ssub_v, t + 1)
                    if tail:
                        act.wait_ge(pt_mm, t)
                    act.activation(prob[:], s_sub[:], ACT.Exp, scale=scale).then_inc(p_a, 1)
                if tail:
                    act.wait_ge(wt_mm, t)
                    act.copy(wu[:].rearrange("p g t -> p (g t)"), ps4[:]).then_inc(wu_a, 1)
                if q:
                    copy_qT(t - 2)
                if front and tail:
                    exp_gates(t, 0, False)
                def copy_eT(n, ps):
                    act.wait_ge(et_mm, 2 * t + n + 1)
                    act.copy(eT[:, :, n * P:(n + 1) * P], ps[:].rearrange("p (h t) -> p h t", h=HP)).then_inc(eT_a, 1)

                gates_first = not tail
                if nxt:
                    act.wait_ge(g_mm, 2 * t + 2)
                    copy_xnT(t + 1)
                if front:
                    if tail:
                        act.wait_ge(wt_mm, t)
                    if gates_first:
                        copy_eT(0, ps0)
                    act.wait_ge(pt_mm, t + 1)
                    if tail:
                        act.wait_ge(at_mm, t)
                    act.copy(pT[:], ps1[:]).then_inc(pT_a, 1)
                    if not gates_first:
                        copy_eT(0, ps0)
                if between:
                    between()
                if tail:
                    act.wait_ge(wn_mm, t)
                    act.copy(wnT[:], ps4[:, 0:T]).then_inc(wnT_a, 1)
                if front:
                    exp_gates(t, 1, not tail)
                    if not nxt:
                        log_forget(0)
                    copy_eT(1, ps2)

            step(0, tail=False, q=False)
            step(1, q=False)
            with act.Fori(2, B - 1) as t:
                step(t)
            step(B - 1, nxt=False)
            step(B, front=False, nxt=False, between=lambda: exp_m(0))

            def copy_xT(b):
                act.wait_ge(x3_mm, b + 1)
                act.copy(xT[:, toks(b)], ps2[:, 0:T])
                act.copy(x_hi[:, toks(b)], ps2[:, 0:T]).then_inc(x3_a, 1)

            def mix_step(t, front=True, mid=True, last=True, after=None):
                def decays(h):
                    act.wait_ge(d_mm, 4 * t + h + 1)
                    if mid or h >= 2:
                        act.wait_ge(c_v, 4 * t + h - 1)
                    d = halves(ps0, h)
                    rows = rowT[rows_of(t)]
                    g0 = rows[:, 0, 0, bass.ds(t * NH + h, 1)]
                    g1 = rows[:, 0, 1, bass.ds(t * NH + h, 1)]
                    act.activation(decay[:, h % 2, 0:T], d[:, 0:T], ACT.Exp, bias=g0).then_inc(d_a, 1)
                    act.activation(decay[:, h % 2, T:T + P], d[:, T:T + P], ACT.Exp, bias=g1).then_inc(d_a, 1)

                if front:
                    decays(0)
                if last:
                    normalise(t - 3, rs3, nb3, xn3, rs3_p, xn3_a)
                if front:
                    decays(1)
                if after:
                    after(1)
                if mid:
                    act.wait_ge(pv_mm, t)
                    if not (isinstance(t, int) and t == 1):
                        act.wait_ge(ht_mm, t - 1)
                    act.copy(hs[:], ps2[:, 0:T])
                    act.copy(ss, ps2[:, 512:512 + T]).then_inc(hs_a, 1)
                if front:
                    decays(2)
                if after:
                    after(2)
                if mid:
                    act.wait_ge(ht_mm, t)
                    if not (isinstance(t, int) and t == 1):
                        act.wait_ge(var4_v, t - 1)
                    act.activation(sq.rearrange("p g d -> p (g d)"), ps4[:, 0:T], ACT.Square).then_inc(sq_a, 1)
                if last:
                    copy_xT(t - 3)
                if front:
                    decays(3)

            act.wait_ge(rowT_v, 1)
            def last_q(h):
                if h == 1:
                    normalise(B - 1, rs2, nb2, xn2, rs2_p, xn2_a)
                if h == 2:
                    copy_qT(B - 1)

            mix_step(0, mid=False, last=False, after=last_q)
            log_forget(1)
            mix_step(1, last=False)
            mix_step(2, last=False)
            exp_m(1)
            mix_step(3)
            act.wait_ge(rowT_v, 2)
            with act.Fori(B // 2, B) as t:
                mix_step(t)

            def silu(n, par):
                act.wait_ge(gu_mm, n + 1)
                if not (isinstance(n, int) and n < 2):
                    act.wait_ge(hh_v, n - 1)
                act.activation(si[par][:], halves(ps0, par), ACT.Silu).then_inc(si_a, 1)

            mix_step(B, front=False, after=lambda h: silu(0, 0) if h == 1 else None)
            silu(1, 1)
            normalise(B - 2, rs3, nb3, xn3, rs3_p, xn3_a)
            silu(2, 0)
            copy_xT(B - 2)
            silu(3, 1)
            silu(4, 0)
            normalise(B - 1, rs3, nb3, xn3, rs3_p, xn3_a)
            copy_xT(B - 1)
            act.wait_ge(lsub_v, 1)
            act.activation(lexp, lsub, ACT.Exp).then_inc(lexp_a, 1)
            for n in range(5, NSH * NB):
                silu(n, n % 2)
            with act.Fori(0, NB) as k:
                for e in range(E):
                    silu(routed(k, e), e % 2)

        @block.vector
        def _(dve):
            own = Chain(dve, dve_own)
            tt = dve.tensor_tensor

            def stats(b, bn):
                for n in range(TT):
                    own.count(dve.bn_stats(bn[:, n, :], x[:, b * TT + n, :]))

            def moments(bn, mv, done):
                for n in range(TT):
                    ins = dve.bn_aggr(mv[:, n, :], bn[:, n, :])
                    if n < TT - 1:
                        own.count(ins)
                ins.then_inc(done, 1)

            dve.wait_ge(x0_ld, 32)
            stats(0, bn1)
            own.wait()
            moments(bn1, mv1, var1_v)
            own.step(dve.memset(lat[:], 0.0))
            for h2 in range(2):
                own.step(dve.memset(lat[64 * h2:64 * h2 + 64, :, 2 * D + h2:2 * D + h2 + 1], 1.0))
            own.step(dve.memset(vaug[:], 0.0))
            va = vaug[:, 0:HP * TT * WV].rearrange("q (p n j) -> q p n j", p=HP, n=TT)
            for n in range(TT):
                own.step(dve.memset(va[64 * n:64 * n + 64, :, n, 2 * D:WV], 1.0))
            own.step(dve.memset(zeros[:], 0.0))
            own.step(dve.memset(ones_f[:], 1.0))
            own.step(dve.memset(ones_b[:], 1.0))
            own.step(dve.memset(carry[:], 1.0))
            own.step(dve.memset(carry[:, :, 0:1], 0.0))
            own.step(dve.tensor_copy(ident_b[:], ident[:]))
            dve.wait_ge(mask_ld, 16 * len(mask_loads))
            own.step(dve.tensor_copy(latent_mask_b[:], latent_mask[:]))
            own.step(dve.tensor_copy(causal_b[:], causal[:]))
            own.step(dve.tensor_copy(before_b[:], before[:]))
            for part in range(3):
                dve.tensor_copy(pick[BH * part:BH * part + BH], ident[0:BH, 0:BH]).then_inc(const_v, 1)
            dve.wait_ge(wghi_a, 1)
            tt(wg_lo[:], wg[:], wg_hi[:].bitcast(F32), ALU.subtract).then_inc(wglo_v, 1)

            def subtract_max(ps, n_groups, mx, dst, ready, count, used, used_count, done):
                dve.wait_ge(ready, count)
                if used is not None:
                    dve.wait_ge(used, used_count)
                v = ps[:].rearrange("p (g l) -> p g l", g=n_groups)
                own.step(dve.tensor_reduce(mx, v, AX_X, ALU.max))
                tt(dst.rearrange("p (g l) -> p g l", g=n_groups), v, mx.unsqueeze(2).to_broadcast([P, n_groups, L]),
                   ALU.subtract).then_inc(done, 1)

            def keys(b, nxt=True):
                if nxt:
                    stats(b + 1, bn1)
                dve.wait_ge(kv_mm, b + 1)
                if not (isinstance(b, int) and b == 0):
                    dve.wait_ge(s_mm, b)
                own.step(tt(k1[:], ps3[:, 0:P], cos[:], ALU.mult))
                own.step(tt(k2[:], ps3[:, P:2 * P], sin[:], ALU.mult))
                tt(kT[:], k1[:], k2[:], ALU.add).then_inc(kT_v, 1)
                if nxt:
                    moments(bn1, mv1, var1_v)

            def step(t, front=True, nxt=2, tail=True, between=None):
                first = not tail
                if front:
                    if first:
                        subtract_max(ps0, H, g_max[:, 0, :], g_sub[:, 0, :], g_mm, 2 * t + 1,
                                     None if first else ge_a, 2 * t - 1, gsub_v)
                    subtract_max(ps1, 16, s_max[:], s_sub[:], s_mm, t + 1, None if first else p_a, t, ssub_v)
                    if not first:
                        subtract_max(ps0, H, g_max[:, 0, :], g_sub[:, 0, :], g_mm, 2 * t + 1,
                                     None if first else ge_a, 2 * t - 1, gsub_v)
                if tail:
                    dve.wait_ge(wtr_mm, t)
                    w = ps4[:].rearrange("p (g j) -> p g j", j=32)
                    own.step(dve.reciprocal(w_rden[:].rearrange("p (g h) -> p g h", h=2), w[:, :, 2 * D:2 * D + 2]))
                    tt(wn[:].rearrange("p n (g h d) -> p (n g) h d", h=2, d=D),
                       w[:, :, 0:2 * D].rearrange("p g (h d) -> p g h d", h=2),
                       w_rden[:].rearrange("p (g h) -> p g h", h=2).unsqueeze(3).to_broadcast([P, TT * HP, 2, D]),
                       ALU.mult).then_inc(wn_v, 1)
                if front:
                    subtract_max(ps2, H, g_max[:, 1, :], g_sub[:, 1, :], g_mm, 2 * t + 2,
                                 None if first else ge_a, 2 * t, gsub_v)
                if between:
                    between()
                if nxt:
                    keys(t + 1, nxt=nxt == 2)
                if front:
                    dve.wait_ge(at_mm, t + 1)
                    av = ps1[:].rearrange("q (p w) -> q p w", p=HP)
                    den = av[:, :, 0:TT * WV].rearrange("q p (n j) -> q p n j", n=TT)[:, :, :, 2 * D]
                    own.step(dve.reciprocal(a_rden[:], den))
                    for h2 in range(2):
                        r = slice(64 * h2, 64 * h2 + 64)
                        for n, dst in enumerate((a_n0, a_n1)):
                            o = WV * n + D * h2
                            ins = tt(dst[r], av[r, :, o:o + D], a_rden[r, :, n:n + 1].to_broadcast([64, HP, D]), ALU.mult)
                            if n < 1 or h2 < 1:
                                own.count(ins)
                    ins.then_inc(at_v, 1)
                if tail:
                    dve.wait_ge(pr_mm, t)
                    tt(x[:, tiles(t - 1), :], x[:, tiles(t - 1), :], ps4[:, 0:T].rearrange("p (n c) -> p n c", n=TT),
                       ALU.add).then_inc(x1_v, 1)
                    dve.wait_ge(x1_v, t)
                if front:
                    own.wait()
                    dve.wait_ge(at_v, t + 1)
                    if tail:
                        dve.wait_ge(wt_mm, t)
                    own.count(tt(lat[0:64, :, 0:D], a_n0[0:64], a_n1[0:64], ALU.add))
                if tail:
                    stats(t - 1, bn2)
                    own.wait()
                if front:
                    tt(lat[64:128, :, D:2 * D], a_n0[64:128], a_n1[64:128], ALU.add).then_inc(lat_v, 1)
                if tail:
                    moments(bn2, mv2, var2_v)

            dve.wait_ge(x_ld, 16)
            dve.wait_ge(attn_ld, 16 * len(attn_loads))
            keys(0)
            step(0, tail=False)
            with dve.Fori(1, B - 2) as t:
                own.loop(t - 1, ATTN_DVE_STEPS)
                step(t)
            own.end(B - 3)
            step(B - 2, nxt=1)
            dve.wait_ge(rows_ld, 16 * len(rows_loads))
            tt(kk[:], kk[:], kv[:], ALU.add).then_inc(kkv_v, 1)
            dve.tensor_scalar(rms[:], rms[:], 1.0, None, ALU.add).then_inc(kkv_v, 1)
            step(B - 1, nxt=0)

            f = slice(BH, 2 * BH)

            def forget_min(i):
                if i == 0:
                    dve.wait_ge(gr_a, 1)
                else:
                    dve.wait_ge(gates_mm, 2)
                    tt(gr[1][:], ps3[0:2 * BH, 0:T], gr[0][:], ALU.add).then_inc(gr_v, 1)
                    dve.wait_ge(gr_v, 1)
                own.step(dve.tensor_scalar(f_min[f, :], gr[i][f, :], 0.0, None, ALU.min))

            def running_max(i):
                dve.wait_ge(flog_a, i + 1)
                own.step(tt(logf[:], f_min[f, :], f_log[f, :], ALU.subtract))
                own.step(dve.tensor_tensor_scan(cs[:], logf[:], zeros[:], 0.0, ALU.add, ALU.add))
                if i:
                    dve.wait_ge(rowT_mm, i)
                    dve.wait_ge(em_a, i)
                tt(gi[:], gr[i][0:BH, :], cs[:], ALU.subtract).then_inc(gi_v, 1)
                dve.wait_ge(gi_v, i + 1)
                own.step(dve.tensor_tensor_scan(top[:], gi[:], gi[:], -3.0e38, ALU.max, ALU.max))
                tt(m_row[:], cs[:], top[:], ALU.add).then_inc(m_v, 1)

            def neg_parts(i):
                neg_high(i)
                neg_low(i)

            def neg_high(i):
                own.step(dve.tensor_scalar(neg[:], top[:], -1.0, None, ALU.mult))
                own.step(dve.tensor_copy(neg_b1[:], neg[:]))
                own.count(dve.tensor_copy(neg3[i][0:BH, :], neg_b1[:]))
                own.step(tt(neg_r1[:], neg[:], neg_b1[:], ALU.subtract))

            def neg_low(i):
                own.step(dve.tensor_copy(neg_b2[:], neg_r1[:]))
                own.count(dve.tensor_copy(neg3[i][BH:2 * BH, :], neg_b2[:]))
                own.step(tt(neg_r2[:], neg_r1[:], neg_b2[:], ALU.subtract))
                dve.tensor_copy(neg3[i][2 * BH:3 * BH, :], neg_r2[:]).then_inc(neg3_v, 1)

            def copy_rows(i, ps):
                dve.wait_ge(rowT_mm, i + 1)
                dve.tensor_copy(rowT[i][:].rearrange("p a n r -> p (a n r)"), ps).then_inc(rowT_v, 1)

            forget_min(0)
            running_max(0)
            neg_parts(0)
            step(B, front=False, nxt=0, between=lambda: copy_rows(0, ps1[:, 0:4 * BH]))

            def low_part(b):
                dve.wait_ge(x3_a, b + 1)
                tt(x_lo[:, toks(b)], xT[:, toks(b)], x_hi[:, toks(b)].bitcast(F32), ALU.subtract).then_inc(xlo_v, 1)

            def scale_heads(b):
                dve.wait_ge(rs4_p, b + 1)
                own.step(tt(f4[:], r4[:], rs4[:], ALU.mult))
                tt(y1[:].rearrange("p n (h d) -> p (n h) d", h=NH), ps4[:, 0:T].rearrange("p (g d) -> p g d", d=HD),
                   f4[:].rearrange("p n h -> p (n h)").unsqueeze(2).to_broadcast([P, TT * NH, HD]),
                   ALU.mult).then_inc(y_v, 1)

            def residual(b):
                dve.wait_ge(y2_p, b + 1)
                tt(x[:, tiles(b), :], x[:, tiles(b), :], y2, ALU.add).then_inc(x2_v, 1)
                dve.wait_ge(x2_v, b + 1)

            def mix_step(t, par, front=True, mid=True, tail=True, last=True, between=None):
                def weigh(h):
                    dve.wait_ge(qk_mm, 4 * t + h + 1)
                    dve.wait_ge(d_a, 2 * (4 * t + h + 1))
                    if tail and h == 0:
                        dve.wait_ge(pv_mm, t - 1)
                    dve.scalar_tensor_tensor(out=cc[par][:, h, :], in0=halves(ps1, h)[:, 0:384], scalar=qk_scale,
                                             in1=decay[:, h % 2, :], op0=ALU.mult, op1=ALU.mult).then_inc(c_v, 1)

                if front:
                    weigh(0)
                if tail:
                    scale_heads(t - 2)
                if front:
                    weigh(1)
                if between:
                    between()
                if tail:
                    residual(t - 2)
                if front:
                    weigh(2)
                if tail:
                    stats(t - 2, bn3)
                    own.wait()
                if mid:
                    dve.wait_ge(ht_mm, t)
                    sums = ps3[:, 0:T].rearrange("p (n h d) -> p n h d", n=TT, h=NH)[:, :, :, 0]
                    tt(n4[:], sums, rowT[rows_of(t)][:, 1, :, bass.ds((t - 1) * NH, NH)], ALU.max).then_inc(n4_v, 1)
                    if tail:
                        moments(bn3, mv3, var3_v)
                    dve.wait_ge(n4_v, t)
                    own.step(dve.tensor_scalar(n4e[:], n4[:], RMS_EPS, None, ALU.add))
                    own.step(dve.reciprocal(r4[:], n4e[:]))
                    own.count(tt(r4s[:], r4[:], r4[:], ALU.mult))
                    dve.wait_ge(sq_a, t)
                    own.step(dve.tensor_reduce(s4[:].rearrange("p n h -> p (n h)"), sq, AX_X, ALU.add))
                    dve.scalar_tensor_tensor(out=v4[:], in0=s4[:], scalar=1.0 / HD, in1=r4s[:],
                                             op0=ALU.mult, op1=ALU.mult).then_inc(var4_v, 1)
                if front:
                    weigh(3)
                if last:
                    low_part(t - 3)

            mix_step(0, 0, mid=False, tail=False, last=False)
            forget_min(1)
            dve.wait_ge(rowT_v, 1)
            mix_step(1, 1, tail=False, last=False)
            running_max(1)
            mix_step(2, 0, last=False, between=lambda: neg_high(1))
            copy_rows(1, ps3[:, T:T + 4 * BH])
            mix_step(3, 1, between=lambda: neg_low(1))
            dve.wait_ge(rowT_v, 2)
            with dve.Fori(1, B // 2 - 1) as i:
                own.loop(i - 1, 2 * MIX_DVE_STEPS)
                mix_step(2 * i + 2, 0)
                mix_step(2 * i + 3, 1)
            own.end(B // 2 - 2)

            def hidden(n, par):
                dve.wait_ge(si_a, n + 1)
                if not (isinstance(n, int) and n < 2):
                    dve.wait_ge(dn_mm, n - 1)
                tt(hh[par][:], halves(ps1, par), si[par][:], ALU.mult).then_inc(hh_v, 1)

            def add_shared(k):
                dve.wait_ge(dn_mm, NSH * (k + 1))
                dve.wait_ge(xn3_a, min(B, (k + 1) * BLK // TT))
                xb = x[:, k * BLK:(k + 1) * BLK, :]
                tt(xb, xb, ps3[:].rearrange("p (n c) -> p n c", n=BLK), ALU.add).then_inc(sx_v, 1)

            mix_step(B, 0, front=False, between=lambda: hidden(0, 0))
            hidden(1, 1)
            scale_heads(B - 1)
            hidden(2, 0)
            add_shared(0)
            dve.wait_ge(rs3_p, B - 1)
            residual(B - 1)
            stats(B - 1, bn3)
            own.wait()
            moments(bn3, mv3, var3_v)
            hidden(3, 1)
            low_part(B - 2)
            hidden(4, 0)
            low_part(B - 1)

            dve.wait_ge(lg_mm, 1)
            lg = ps4[:, 0:NT * E].rearrange("p (n e) -> p n e", e=E)
            bc = lambda v: v.unsqueeze(2).to_broadcast([P, NT, E])
            own.step(dve.tensor_reduce(lmax[:], lg, AX_X, ALU.max))
            tt(lsub, lg, bc(lmax[:]), ALU.subtract).then_inc(lsub_v, 1)
            add_shared(1)
            dve.wait_ge(lexp_a, 1)
            own.step(dve.tensor_reduce(lsum[:], lexp, AX_X, ALU.add))
            own.step(dve.reciprocal(lrec[:], lsum[:]))
            own.step(tt(score, lexp, bc(lrec[:]), ALU.mult))
            for n in range(NT):
                own.count(dve.max(top8[:, n, :], score[:, n, :]))
                if n == NT // 2:
                    hidden(5, 1)
            own.wait()
            for n in range(NT):
                own.count(dve.max_index(idx8[:, n, :], top8[:, n, :], score[:, n, :]))
                if n == NT // 2:
                    hidden(6, 0)
            add_shared(2)
            own.step(tt(wsum[:], top8[:, :, 0], top8[:, :, 1], ALU.add))
            own.count(dve.tensor_scalar(wsum[:], wsum[:], 1e-20, None, ALU.add))
            dve.wait_ge(exp_ld, 16 * len(exp_loads))
            for k in range(2):
                own.count(dve.tensor_copy(idxf[:, k, :], idx8[:, :, k]))
            own.wait()
            own.count(dve.reciprocal(wrec[:], wsum[:]))
            hidden(7, 1)
            bn_ = lambda v: v.unsqueeze(1).to_broadcast([P, E, NT])
            for k, one_hot in enumerate((oh0, oh1)):
                own.step(tt(one_hot, ids[:], bn_(idxf[:, k, :]), ALU.is_equal))
            tt(ohb[:], oh0, oh1, ALU.add).then_inc(ohb_v, 1)
            hidden(routed(0, 0), 0)
            for k in range(2):
                own.step(tt(w2[:, k, :], top8[:, :, k], wrec[:], ALU.mult))
            for k, one_hot, weight in ((0, oh0, ow0), (1, oh1, ow1)):
                own.step(tt(weight, one_hot, bn_(w2[:, k, :]), ALU.mult))
            own.step(tt(ow, ow0, ow1, ALU.add))
            add_shared(3)
            hidden(routed(0, 1), 1)

            def places():
                dve.wait_ge(cnt_mm, 1)
                flat = lambda v: v.rearrange("p e n -> p (e n)")
                own.step(dve.tensor_copy(flat(tot), ps4[:, 3 * P:4 * P]))
                own.step(dve.tensor_tensor_scan(flat(pre), flat(carry[:]), flat(tot), 0.0, ALU.mult, ALU.add))
                own.step(tt(flat(pre), flat(pre), flat(tot), ALU.subtract))
                own.step(tt(flat(pos), ps4[:, 2 * P:3 * P], flat(pre), ALU.add))
                dve.scalar_tensor_tensor(out=comb, in0=pos, scalar=float(CAP), in1=ow,
                                         op0=ALU.is_lt, op1=ALU.mult).then_inc(comb_v, 1)
                dve.wait_ge(sx_v, NB)
                dve.wait_ge(comb_v, 1)

            def weighted(k, e, first=False):
                dve.wait_ge(dn_mm, routed(k, e) + 1)
                if not first or e >= 2:
                    dve.wait_ge(acc_p, k * (E - 1) + max(e - 2, 1) if e >= 2 else k * (E - 1))
                tt(yw[e % 2], halves(ps2, e).rearrange("p (n c) -> p n c", n=BLK),
                   comb[:, e, bass.ds(k * BLK, BLK)].unsqueeze(2).to_broadcast([P, BLK, C]), ALU.mult).then_inc(yw_v, 1)

            def finish(k):
                xb = x[:, bass.ds(k * BLK, BLK), :]
                dve.wait_ge(acc_p, (k + 1) * (E - 1))
                tt(xb, xb, acc, ALU.add).then_inc(fin_v, 1)

            def experts(k, first):
                for e in range(E):
                    if e > 1 or not first:
                        hidden(routed(k, e), e % 2)
                    if e:
                        weighted(k, e - 1, first)
                    elif first:
                        places()
                    else:
                        weighted(k - 1, E - 1)
                    if e == 1 and not first:
                        finish(k - 1)

            experts(0, True)
            with dve.Fori(1, NB) as k:
                experts(k, False)
            weighted(NB - 1, E - 1)
            xb = x[:, (NB - 1) * BLK:NB * BLK, :]
            dve.wait_ge(acc_p, (NB - 1) * (E - 1) + E - 2)
            own.step(tt(xb, xb, acc, ALU.add))
            dve.wait_ge(yw_v, NB * E)
            tt(xb, xb, yw[(E - 1) % 2], ALU.add).then_inc(fin_v, 1)

        @block.tensor
        def _(pe):
            mm = pe.matmul

            def context_rows():
                pe.wait_ge(rows_ld, 16 * len(rows_loads))
                pe.wait_ge(kkv_v, 1)
                pe.wait_ge(v_a, B)
                pe.wait_ge(qT_a, B - 2)
                for b in range(B):
                    mm(ps3[0:2 * BH, 0:T], kk[:, b, :], ctxT[:, b * T:(b + 1) * T], start=(b == 0), stop=False)

            def gate_rows(i):
                pe.wait_ge(qT_a, (i + 1) * B // 2)
                rows = ps3[0:2 * BH, 0:T]
                for b in range(i * B // 2, (i + 1) * B // 2):
                    ins = mm(rows, kq[:, b, :], qT[:, b * T:(b + 1) * T], start=(i == 1 and b == B // 2), stop=(b == (i + 1) * B // 2 - 1))
                ins.then_inc(gates_mm, 1)

            def transpose_rows(i, ps):
                pe.wait_ge(gi_v, i + 1)
                pe.wait_ge(em_a, i + 1)
                for a_, src in enumerate((gi, em)):
                    for n in range(TT):
                        o = (TT * a_ + n) * BH
                        ins = pe.transpose(ps[:, o:o + BH], src[:, n * P:(n + 1) * P], ident[0:BH, 0:BH])
                ins.then_inc(rowT_mm, 1)

            def transpose_xn(b):
                pe.wait_ge(xn1_a, b + 1)
                for n in range(TT):
                    ins = pe.transpose(ps3[:, n * P:(n + 1) * P], xn1[:, n, :], ident[:])
                ins.then_inc(xn_mm, 1)

            pe.wait_ge(x0_ld, 32)
            transpose_xn(0)
            pe.wait_ge(attn_ld, 16 * len(attn_loads))

            def keys_values(b):
                pe.wait_ge(xnT_a, b + 1)
                mm(ps3[:, 0:P], wk[:], xkT[:], start=True, stop=True)
                mm(ps3[:, P:2 * P], wkr[:], xkT[:], start=True, stop=True)
                mm(ps3[:, 2 * P:3 * P], xkT[:], wv[:], start=True, stop=True).then_inc(kv_mm, 1)

            keys_values(0)
            pe.wait_ge(wglo_v, 1)

            def step(t, front=True, nxt=True, tail=True, q=True, between=None):
                first = not tail

                def gates(n, ps):
                    if not first:
                        pe.wait_ge(eT_a, 2 * t - 1 + n)
                    for j in range(2):
                        for i, (xp, wp_) in enumerate(((xn_hi, wg_hi), (xn_hi, wg_lo), (xn_lo, wg_hi))):
                            ins = mm(ps[:, 512 * j:512 * j + 512], xp[:, n * P:(n + 1) * P], wp_[:, 512 * j:512 * j + 512],
                                     start=(i == 0), stop=(i == 2))
                    ins.then_inc(g_mm, 1)

                if front and first:
                    pe.wait_ge(xnlo_p, t + 1)
                    gates(0, ps0)
                if front:
                    pe.wait_ge(kT_v, t + 1)
                    if first:
                        pe.wait_ge(const_v, 3)
                    if not first:
                        pe.wait_ge(at_v, t)
                    for half in range(2):
                        bank = ps1[:, 512 * half:512 * half + 512]
                        mm(bank, ident_b[:], latent_mask_b[:], start=True, stop=True)
                        for j in range(4):
                            ins = mm(bank[:, P * j:P * j + P], qblk[:, 4 * half + j, :], kT[:], start=False, stop=True,
                                     skip_group_check=True)
                    ins.then_inc(s_mm, 1)
                if front and not first:
                    pe.wait_ge(xnlo_p, t + 1)
                    gates(0, ps0)
                if tail:
                    pe.wait_ge(eT_a, 2 * t)
                    pe.wait_ge(lat_v, t)
                    if q:
                        pe.wait_ge(x1_v, t - 1)
                    for p in range(HP):
                        r = 32 * (p % 4)
                        ins = mm(ps4[r:r + 32, T * (p // 4):T * (p // 4) + T], lat[:, p, :], eT[:, p, :],
                                 start=True, stop=True)
                    ins.then_inc(wt_mm, 1)
                if q:
                    pe.wait_ge(xn2_a, t - 1)
                    if front:
                        pe.wait_ge(v_a, t + 1)
                    elif tail:
                        pe.wait_ge(gr_a, 1)
                    for n in range(TT):
                        ins = pe.transpose(ps3[:, T + n * P:T + n * P + P], xn2[:, n, :], ident[:])
                    ins.then_inc(q_mm, 1)
                if front:
                    gates(1, ps2)
                if tail:
                    pe.wait_ge(wu_a, t)
                    for n in range(TT):
                        for g in range(2):
                            ins = pe.transpose(ps4[:, (2 * n + g) * P:(2 * n + g + 1) * P], wu[:, g, n * P:(n + 1) * P], ident[:])
                    ins.then_inc(wtr_mm, 1)
                if between:
                    between()
                if front and not nxt:
                    context_rows()
                if nxt:
                    if q:
                        pe.wait_ge(qT_a, t - 1)
                    else:
                        pe.wait_ge(v_a, t + 1)
                    transpose_xn(t + 1)

                def transpose_gates(n, ps):
                    pe.wait_ge(ge_a, 2 * t + n + 1)
                    for p in range(HP):
                        ins = pe.transpose(ps[:, p * P:(p + 1) * P], g_exp[:, n, p * P:(p + 1) * P], ident[:])
                    ins.then_inc(et_mm, 1)

                gates_first = first
                if front:
                    if gates_first:
                        transpose_gates(0, ps0)
                    pe.wait_ge(p_a, t + 1)
                    for p in range(HP):
                        ins = pe.transpose(ps1[:, p * P:(p + 1) * P], prob[:, p * P:(p + 1) * P], ident[:])
                    ins.then_inc(pt_mm, 1)
                    if not gates_first:
                        transpose_gates(0, ps0)
                if tail:
                    pe.wait_ge(wn_v, t)
                    for n in range(TT):
                        ins = pe.transpose(ps4[:, n * P:(n + 1) * P], wn[:, n, :], ident[:])
                    ins.then_inc(wn_mm, 1)
                if nxt:
                    keys_values(t + 1)
                if front and not nxt:
                    gate_rows(0)
                if front:
                    pe.wait_ge(pT_a, t + 1)
                    for p in range(HP):
                        w = p * TT * WV
                        ins = mm(ps1[:, p * P:(p + 1) * P], pT[:, p * P:(p + 1) * P], vaug[:, w:w + P], start=True, stop=True)
                    ins.then_inc(at_mm, 1)
                if tail:
                    pe.wait_ge(wnT_a, t)
                    for n in range(TT):
                        ins = mm(ps4[:, n * P:(n + 1) * P], wnT[:, n * P:(n + 1) * P], wp[:], start=True, stop=True)
                    ins.then_inc(pr_mm, 1)
                if front:
                    transpose_gates(1, ps2)

            step(0, tail=False, q=False)
            step(1, q=False)
            with pe.Fori(2, B - 1) as t:
                step(t)
            step(B - 1, nxt=False)
            step(B, front=False, nxt=False, between=lambda: transpose_rows(0, ps1))

            def mix_step(t, par, pair, front=True, mid=True, last=True, after=None):
                def scores(h):
                    d, s = halves(ps0, h), halves(ps1, h)
                    if mid or h >= 2:
                        pe.wait_ge(d_a, 2 * (4 * t + h - 1))
                    sel = pick[:, bass.ds(t * NH + h, 1)].to_broadcast([3 * BH, P])
                    mm(d[:, 0:T], sel, neg3[rows_of(t)][:], start=True, stop=True)
                    mm(d[:, T:T + P], sel, neg3[rows_of(t)][:, P:T], start=False, stop=True, skip_group_check=True)
                    mm(d[:, 0:P], ident_b[:], causal_b[:], start=False, stop=True, skip_group_check=True)
                    mm(d[:, T:T + P], ident_b[:], causal_b[:], start=False, stop=True, skip_group_check=True).then_inc(d_mm, 1)
                    if mid or h >= 2:
                        pe.wait_ge(c_v, 4 * t + h - 1)
                    mm(s[:, 0:T], kTm[par][:, h, 0:P], qT[:, toks(t)], start=True, stop=True)
                    mm(s[:, T:T + P], kTm[par][:, h, P:T], qT[:, bass.ds(t * T + P, P)], start=False, stop=True,
                       skip_group_check=True).then_inc(qk_mm, 1)

                if front:
                    pe.wait_ge(key_ld[par], 16 * NH * (pair + 1))
                    scores(0)
                    scores(1)
                if mid:
                    pe.wait_ge(c_v, 4 * t)
                    pe.wait_ge(val_ld[1 - par], 16 * (pair + par))
                    if not (isinstance(t, int) and t == 1):
                        pe.wait_ge(hs_a, t - 1)
                    if not (isinstance(t, int) and t < 4):
                        pe.wait_ge(x3_a, t - 3)
                    o = 1 - par
                    for src, col in ((None, 0), (ones_f, 512)):
                        for n in range(TT):
                            for h in range(NH):
                                rows = slice(HD * h, HD * h + HD)
                                w = ones_f[:] if src is not None else vv[o][:, n, rows]
                                c0 = col + n * P
                                m_ = cc[o][:, h, 0:T] if n == 0 else cc[o][:, h, T:T + P]
                                ins = mm(ps2[rows, c0:col + T], w, m_, start=(n == 0), stop=True, skip_group_check=True)
                    ins.then_inc(pv_mm, 1)
                if front:
                    scores(2)
                if after:
                    after()
                if mid:
                    pe.wait_ge(hs_a, t)
                    if not (isinstance(t, int) and t == 1):
                        pe.wait_ge(y_v, t - 1)
                        pe.wait_ge(n4_v, t - 1)
                    if isinstance(t, int) and t == 3:
                        pe.wait_ge(rowT_v, 2)
                    for src, ps in ((hs[:], ps4), (ss, ps3)):
                        for n in range(TT):
                            ins = pe.transpose(ps[:, n * P:(n + 1) * P], src[:, n * P:(n + 1) * P], ident[:])
                    ins.then_inc(ht_mm, 1)
                if last:
                    transpose_xn3(t - 3)
                if front:
                    scores(3)

            def transpose_xn3(b):
                pe.wait_ge(xn3_a, b + 1)
                for n in range(TT):
                    ins = pe.transpose(ps2[:, n * P:(n + 1) * P], xn3[:, n, :], ident[:])
                ins.then_inc(x3_mm, 1)

            pe.wait_ge(neg3_v, 1)
            pe.wait_ge(gr_a, 1)
            pe.wait_ge(rowT_v, 1)
            mix_step(0, 0, 0, mid=False, last=False, after=lambda: step(B + 1, front=False, nxt=False, tail=False))
            gate_rows(1)
            pe.wait_ge(x1_v, B)
            pe.wait_ge(gr_v, 1)
            mix_step(1, 1, 0, last=False)
            mix_step(2, 0, 1, last=False)
            pe.wait_ge(n4_v, 2)
            transpose_rows(1, ps3[:, T:2 * T])
            mix_step(3, 1, 1)
            pe.wait_ge(neg3_v, 2)
            with pe.Fori(1, B // 2 - 1) as i:
                mix_step(2 * i + 2, 0, i + 1)
                mix_step(2 * i + 3, 1, i + 1)

            def up(n, e, k):
                par = e % 2
                if not (isinstance(n, int) and n < 2):
                    pe.wait_ge(si_a, n - 1)
                    pe.wait_ge(hh_v, n - 1)
                xh, xl = (v[:, bass.ds(k * BLK * P, BLK * P)] for v in (x_hi, x_lo))
                for ps, (hi, lo) in zip((ps0, ps1), we_parts):
                    for i, (w, cols) in enumerate(((hi, xh), (hi, xl), (lo, xh))):
                        ins = mm(halves(ps, par), w[:, e, :], cols, start=(i == 0), stop=(i == 2))
                ins.then_inc(gu_mm, 1)

            def down(n, e, ps, add=False):
                pe.wait_ge(hh_v, n + 1)
                for m in range(BLK):
                    ins = mm(ps[:, m * P:(m + 1) * P], hh[e % 2][:, m * P:(m + 1) * P], we_d[:, e, :],
                             start=(m == 0 and not add), stop=True, skip_group_check=True)
                ins.then_inc(dn_mm, 1)

            def shared_down(k, js=range(NSH)):
                if k and 0 in js:
                    pe.wait_ge(sx_v, k)
                for j in js:
                    down(NSH * k + j, E + j, ps3[:], add=j > 0)

            pe.wait_ge(exp_ld, 16 * len(exp_loads))
            pe.wait_ge(we_p, 2)
            pe.wait_ge(xlo_v, BLK // TT)
            pe.wait_ge(c_v, NH * B - 1)
            pe.wait_ge(d_a, 2 * (NH * B - 1))
            up(0, E, 0)
            pe.wait_ge(c_v, NH * B)
            pe.wait_ge(d_a, 2 * NH * B)
            mix_step(B, 0, B // 2, front=False, after=lambda: up(1, E + 1, 0))
            pe.wait_ge(xlo_v, 2 * BLK // TT)
            up(2, E, 1)
            pe.wait_ge(n4_v, B)
            shared_down(0)
            pe.wait_ge(x3_a, B - 2)
            transpose_xn3(B - 2)
            up(3, E + 1, 1)
            pe.wait_ge(xlo_v, 3 * BLK // TT)
            up(4, E, 2)
            shared_down(1)
            pe.wait_ge(x3_a, B - 1)
            transpose_xn3(B - 1)
            pe.wait_ge(x3_a, B)
            pe.wait_ge(y_v, B)
            for n in range(NT):
                ins = mm(ps4[:, n * E:n * E + 96], xT[:, n * P:(n + 1) * P], gate_w[:], start=True, stop=True)
            ins.then_inc(lg_mm, 1)
            up(5, E + 1, 2)
            shared_down(2, [0])
            pe.wait_ge(xlo_v, B)
            up(6, E, 3)
            shared_down(2, [1])
            up(7, E + 1, 3)

            def count_before():
                pe.wait_ge(ohb_v, 1)
                ohf = ohb[:].rearrange("p e n -> p (e n)")
                mm(ps4[:, 2 * P:3 * P], before_b[:], ohf, start=True, stop=True)
                mm(ps4[:, 3 * P:4 * P], ones_b[:], ohf, start=True, stop=True).then_inc(cnt_mm, 1)

            def routed_down(k, e, first=False):
                if not first or e >= 2:
                    pe.wait_ge(yw_v, k * E + e - 1)
                down(routed(k, e), e, halves(ps2, e))

            def experts(k, first):
                for e in range(E):
                    up(routed(k, e), e, k)
                    if first and e == 0:
                        shared_down(NB - 1)
                        count_before()
                    if e:
                        routed_down(k, e - 1, first)
                    elif not first:
                        routed_down(k - 1, E - 1)

            experts(0, True)
            with pe.Fori(1, NB) as k:
                experts(k, False)
            routed_down(NB - 1, E - 1)


def kernel(x, ctx_1024, L0_attn_latent_queries, L0_attn_W_k, L0_attn_W_v, L0_attn_W_g, L0_attn_W_p,
           L0_xattn_igate_kernel, L0_xattn_igate_bias, L0_xattn_fgate_kernel, L0_xattn_fgate_bias,
           L0_xattn_rms_scale, L0_ffn_gate_w, L0_ffn_we_gate, L0_ffn_we_up, L0_ffn_we_down,
           L0_ffn_ws_gate, L0_ffn_ws_up, L0_ffn_ws_down):
    import concourse.bacc as bacc
    from concourse.bass_utils import run_bass_kernel_spmd

    con = np.ascontiguousarray
    latents = np.asarray(L0_attn_latent_queries)[0]
    qblk = np.zeros((H, D, HP, 2, L), np.float32)
    for h in range(H):
        qblk[h, :, h // 2, h % 2, :] = latents[:, h, :].T
    wkT = np.asarray(L0_attn_W_k).T
    swap = np.arange(C) ^ 1
    ik, fk = np.asarray(L0_xattn_igate_kernel), np.asarray(L0_xattn_fgate_kernel)

    def gate_kernel(part):
        g = np.zeros((C, B, 2, B, NH), np.float32)
        for b in range(B):
            g[:, b, 0, b, :] = ik[part * C:(part + 1) * C]
            g[:, b, 1, b, :] = fk[part * C:(part + 1) * C]
        return g.reshape(C, B, 2 * BH)

    gate_w = np.zeros((C, 96), np.float32)
    gate_w[:, 0:E] = np.asarray(L0_ffn_gate_w).T

    def experts(routed, shared, down):
        r, s = np.asarray(routed), np.asarray(shared)
        s = s.reshape(C, NSH, I).transpose(1, 0, 2) if down else s.reshape(NSH, I, C)
        return con(np.concatenate([r, s]).transpose(2, 0, 1))

    arrays = {
        "x": con(x), "ctx": con(ctx_1024), "ctxT": con(np.asarray(ctx_1024).reshape(B * T, C).T),
        "wkT": con(wkT), "wkrT": con(wkT[:, swap]), "wvT": con(np.asarray(L0_attn_W_v).T),
        "wgT": con(np.asarray(L0_attn_W_g).T), "wpT": con(np.asarray(L0_attn_W_p).T),
        "qblk": qblk.reshape(C, HP, P),
        "kq": gate_kernel(0), "kk": gate_kernel(1), "kv": gate_kernel(2),
        "gate_bias": con(np.concatenate([np.tile(L0_xattn_igate_bias, B), np.tile(L0_xattn_fgate_bias, B)])[:, None]),
        "rms": con(np.broadcast_to(np.tile(L0_xattn_rms_scale, NH), (P, TT, C))),
        "gate_w": gate_w,
        "we_g": experts(L0_ffn_we_gate, L0_ffn_ws_gate, False),
        "we_u": experts(L0_ffn_we_up, L0_ffn_ws_up, False),
        "we_d": experts(L0_ffn_we_down, L0_ffn_ws_down, True),
        **constants(),
    }
    nc = bacc.Bacc("TRN2", target_bir_lowering=False, num_devices=1)
    ins = {n: nc.dram_tensor(f"in_{n}", v.shape, mybir.dt.from_np(v.dtype), kind="ExternalInput").ap() for n, v in arrays.items()}
    out = nc.dram_tensor("out", (B, T, C), F32, kind="ExternalOutput").ap()
    decoder_layer(nc, ins, out)
    r = run_bass_kernel_spmd(nc, [{f"in_{n}": v for n, v in arrays.items()}], core_ids=[0])
    return r.results[0]["out"]
```
